# Optimizing a Trainium2 kernel written in Bass

```python
import numpy as np
import jax
import jax.numpy as jnp

def _softmax(x, axis=-1):
    return jax.nn.softmax(x, axis=axis)

def _gelu(x):
    return jax.nn.gelu(x, approximate=True)

def _silu(x):
    return jax.nn.silu(x)

def _sigmoid(x):
    return jax.nn.sigmoid(x)

def _layernorm(x, axis=-1, eps=1e-05):
    m = jnp.mean(x, axis=axis, keepdims=True)
    v = jnp.var(x, axis=axis, keepdims=True)
    return (x - m) / jnp.sqrt(v + eps)

def _scatter_add(tgt, idx, src, axis=0):
    return tgt.at[idx].add(src)

def _segment_sum(src, seg, n):
    return jax.ops.segment_sum(src, seg, n)
kernel_name = 'mk_early_fusion_d4_tok_img1024_r4_9e746f'

def setup_inputs(seed: int=0):
    np.random.seed(seed)
    _w = jnp.asarray

    def _rec_inputs():
        import jax
        import jax.numpy as jnp
        _rk = jax.random.key(seed)
        x = -0.000222058 + 0.999998 * jax.random.normal(jax.random.fold_in(_rk, 1), (16, 3, 96, 96), jnp.float32)
        txt = 0.00193382 + 0.183443 * jax.random.normal(jax.random.fold_in(_rk, 2), (16, 77, 256), jnp.float32)
        return (x, txt)
    x, txt = _rec_inputs()

    def _L0_tok_setup():
        import jax, jax.numpy as jnp
        import numpy as np
        P = 16
        C = 3
        D = 256

        def _patchify(x, p):
            B, Cc, H, W = x.shape
            gh, gw = (H // p, W // p)
            x = x.reshape(B, Cc, gh, p, gw, p)
            x = x.transpose(0, 2, 4, 1, 3, 5)
            return x.reshape(B, gh * gw, Cc * p * p)
        key = jax.random.key(seed)
        k1, k2, k3, k4, k5 = jax.random.split(key, 5)
        patch_dim = C * P * P
        s1 = 1.0 / np.sqrt(patch_dim)
        s2 = 1.0 / np.sqrt(D)
        return {'x': jax.random.normal(k1, (32, C, 128, 128), dtype=jnp.float32), 'W1': jax.random.uniform(k2, (patch_dim, D), jnp.float32, -s1, s1), 'b1': jax.random.uniform(k3, (D,), jnp.float32, -s1, s1), 'W2': jax.random.uniform(k4, (D, D), jnp.float32, -s2, s2), 'b2': jax.random.uniform(k5, (D,), jnp.float32, -s2, s2)}
    _L0_tok_all = _L0_tok_setup()
    _L0_tok_in = {k: v for k, v in _L0_tok_all.items() if k in ('W1', 'b1', 'W2', 'b2')}
    del _L0_tok_all

    def _L0_attn_setup():
        import jax, jax.numpy as jnp
        import numpy as np
        Bsz, L, D, N = (2, 512, 256, 16)
        LN_EPS = 1e-05
        key = jax.random.key(seed)
        ks = jax.random.split(key, 5)
        A_log = -jnp.broadcast_to(jnp.log(jnp.arange(1, N + 1, dtype=jnp.float32))[None, :], (D, N))
        return {'x': jax.random.normal(ks[0], (Bsz, L, D), jnp.float32), 'W_dt': jax.random.normal(ks[1], (D, D), jnp.float32) * 0.02, 'b_dt': jnp.zeros((D,), jnp.float32), 'W_B': jax.random.normal(ks[2], (N, D), jnp.float32) * 0.02, 'W_C': jax.random.normal(ks[3], (N, D), jnp.float32) * 0.02, 'D_param': jnp.ones((D,), jnp.float32), 'A_log': A_log, 'gamma': jnp.ones((D,), jnp.float32), 'beta': jnp.zeros((D,), jnp.float32)}
    _L0_attn_all = _L0_attn_setup()
    _L0_attn_in = {k: v for k, v in _L0_attn_all.items() if k in ('W_dt', 'b_dt', 'W_B', 'W_C', 'D_param', 'A_log', 'gamma', 'beta')}
    del _L0_attn_all

    def _L0_ffn_setup():
        import jax, jax.numpy as jnp
        import numpy as np
        S, B, D = (256, 2, 256)
        E, TOPK = (15, 3)
        F = 256
        FS = 512

        def _uinit(k, shape, out_dim):
            std = out_dim ** (-0.5)
            return jax.random.uniform(k, shape, jnp.float32, -std, std)
        key = jax.random.key(seed)
        ks = jax.random.split(key, 10)
        return {'x': jax.random.normal(ks[0], (S, B, D), jnp.float32), 'gate_w': jax.random.normal(ks[1], (E, D), jnp.float32) * D ** (-0.5), 'fc1_w': _uinit(ks[2], (E, 2 * F, D), 2 * F), 'fc1_b': _uinit(ks[3], (E, 2 * F), 2 * F), 'geglu_mult': jnp.ones((E, F), jnp.float32), 'fc2_w': _uinit(ks[4], (E, D, F), D), 'fc2_b': _uinit(ks[5], (E, D), D), 's_fc1_w': _uinit(ks[6], (2 * FS, D), 2 * FS), 's_fc1_b': _uinit(ks[7], (2 * FS,), 2 * FS), 's_geglu_mult': jnp.ones((FS,), jnp.float32), 's_fc2_w': _uinit(ks[8], (D, FS), D), 's_fc2_b': _uinit(ks[9], (D,), D)}
    _L0_ffn_all = _L0_ffn_setup()
    _L0_ffn_in = {k: v for k, v in _L0_ffn_all.items() if k in ('gate_w', 'fc1_w', 'fc1_b', 'geglu_mult', 'fc2_w', 'fc2_b', 's_fc1_w', 's_fc1_b', 's_geglu_mult', 's_fc2_w', 's_fc2_b')}
    del _L0_ffn_all

    def _L1_attn_setup():
        import jax, jax.numpy as jnp
        import numpy as np
        LOG_HALF = float(np.log(0.5))

        def log_g(x):
            return jnp.where(x >= 0.0, jnp.log(jnp.maximum(x, 0.0) + 0.5), -jax.nn.softplus(-x))
        key = jax.random.key(seed)
        k1, k2, k3, k4 = jax.random.split(key, 4)
        B, T, D, E = (4, 1024, 256, 384)
        x = jax.random.normal(k1, (B, T, D), dtype=jnp.float32)
        W_f = jax.random.normal(k2, (2 * E, D), dtype=jnp.float32) * 0.02
        b_f = jax.random.normal(k3, (2 * E,), dtype=jnp.float32) * 0.02
        W_down = jax.random.normal(k4, (D, E), dtype=jnp.float32) * 0.02
        return {'x': x, 'W_f': W_f, 'b_f': b_f, 'W_down': W_down}
    _L1_attn_all = _L1_attn_setup()
    _L1_attn_in = {k: v for k, v in _L1_attn_all.items() if k in ('W_f', 'b_f', 'W_down')}
    del _L1_attn_all

    def _L1_ffn_setup():
        import jax, jax.numpy as jnp
        import numpy as np
        EPS = 1e-06
        LN_EPS = 1e-05

        def _absmean_core(W):
            gamma = jnp.mean(jnp.abs(W)) + EPS
            Ws = W / gamma
            Wq = jnp.sign(Ws) * jnp.minimum(jnp.round(jnp.abs(Ws)), 1.0)
            return (Wq, gamma)

        @jax.custom_vjp
        def absmean(W):
            return _absmean_core(W)[0]

        def _absmean_fwd(W):
            Wq, gamma = _absmean_core(W)
            return (Wq, gamma)

        def _absmean_bwd(gamma, g):
            return (g / gamma,)
        absmean.defvjp(_absmean_fwd, _absmean_bwd)

        def layernorm(x, w, b, eps=LN_EPS):
            mu = jnp.mean(x, axis=-1, keepdims=True)
            var = jnp.mean((x - mu) ** 2, axis=-1, keepdims=True)
            return (x - mu) * jax.lax.rsqrt(var + eps) * w + b
        key = jax.random.key(seed)
        k1, k2, k3 = jax.random.split(key, 3)
        d, h = (256, 1024)
        B, T = (8, 512)
        return {'x': jax.random.normal(k1, (B, T, d), jnp.float32), 'W_fc': jax.random.normal(k2, (h, d), jnp.float32), 'ln_w': jnp.ones((h,), jnp.float32), 'ln_b': jnp.zeros((h,), jnp.float32), 'W_proj': jax.random.normal(k3, (d, h), jnp.float32)}
    _L1_ffn_all = _L1_ffn_setup()
    _L1_ffn_in = {k: v for k, v in _L1_ffn_all.items() if k in ('W_fc', 'ln_w', 'ln_b', 'W_proj')}
    del _L1_ffn_all

    def _L2_attn_setup():
        import jax, jax.numpy as jnp
        import numpy as np
        import math
        IN_DIM = 256
        LATENT_DIM = 64
        OUT_DIM = 256

        def _kaiming(key, fan_out, fan_in):
            std = math.sqrt(2.0 / fan_in)
            return jax.random.normal(key, (fan_out, fan_in), dtype=jnp.float32) * std
        key = jax.random.key(seed)
        kx, kt, kp, kg = jax.random.split(key, 4)
        x = jax.random.normal(kx, (8, 1024, IN_DIM), dtype=jnp.float32)
        W_theta = _kaiming(kt, LATENT_DIM, IN_DIM)
        W_phi = _kaiming(kp, LATENT_DIM, IN_DIM)
        W_g = _kaiming(kg, OUT_DIM, IN_DIM)
        return {'x': x, 'W_theta': W_theta, 'W_phi': W_phi, 'W_g': W_g}
    _L2_attn_all = _L2_attn_setup()
    _L2_attn_in = {k: v for k, v in _L2_attn_all.items() if k in ('W_theta', 'W_phi', 'W_g')}
    del _L2_attn_all

    def _L2_ffn_setup():
        import jax, jax.numpy as jnp
        import numpy as np
        HIDDEN = 256
        INNER = 1024

        def _weight_quant(w):
            scale = 1.0 / jnp.clip(jnp.mean(jnp.abs(w)), 1e-05)
            wq = jnp.clip(jnp.round(w * scale), -1.0, 1.0) / scale
            return w + jax.lax.stop_gradient(wq - w)

        def _act_quant(x):
            scale = 127.0 / jnp.clip(jnp.max(jnp.abs(x), axis=-1, keepdims=True), 1e-05)
            xq = jnp.clip(jnp.round(x * scale), -128.0, 127.0) / scale
            return x + jax.lax.stop_gradient(xq - x)

        def _bitlinear(x, w):
            return jnp.einsum('bsi,oi->bso', _act_quant(x), _weight_quant(w))
        key = jax.random.key(seed)
        k0, k1, k2, k3 = jax.random.split(key, 4)
        x = jax.random.normal(k0, (4, 512, HIDDEN), dtype=jnp.float32)
        w_gate = jax.random.normal(k1, (INNER, HIDDEN), dtype=jnp.float32) / np.sqrt(HIDDEN)
        w_up = jax.random.normal(k2, (INNER, HIDDEN), dtype=jnp.float32) / np.sqrt(HIDDEN)
        w_down = jax.random.normal(k3, (HIDDEN, INNER), dtype=jnp.float32) / np.sqrt(INNER)
        return {'x': x, 'w_gate': w_gate, 'w_up': w_up, 'w_down': w_down}
    _L2_ffn_all = _L2_ffn_setup()
    _L2_ffn_in = {k: v for k, v in _L2_ffn_all.items() if k in ('w_gate', 'w_up', 'w_down')}
    del _L2_ffn_all

    def _L3_attn_setup():
        import jax, jax.numpy as jnp
        import numpy as np
        B, S, E, H = (2, 512, 256, 16)
        D = E // H
        TRIL = D * (D + 1) // 2
        key = jax.random.key(seed)
        ks = jax.random.split(key, 6)
        return {'x': jax.random.normal(ks[0], (B, S, E), dtype=jnp.float32), 'params': jax.random.normal(ks[1], (H, TRIL), dtype=jnp.float32), 'Wv': jax.random.normal(ks[2], (E, E), dtype=jnp.float32) * 0.02, 'bv': jax.random.normal(ks[3], (E,), dtype=jnp.float32) * 0.02, 'Wo': jax.random.normal(ks[4], (E, E), dtype=jnp.float32) * 0.02, 'bo': jax.random.normal(ks[5], (E,), dtype=jnp.float32) * 0.02}
    _L3_attn_all = _L3_attn_setup()
    _L3_attn_in = {k: v for k, v in _L3_attn_all.items() if k in ('params', 'Wv', 'bv', 'Wo', 'bo')}
    del _L3_attn_all

    def _L3_ffn_setup():
        import jax, jax.numpy as jnp
        import numpy as np
        B, S, H, F, E = (2, 512, 256, 1024, 8)
        key = jax.random.key(seed)
        ks = jax.random.split(key, 4)
        x = jax.random.normal(ks[0], (B, S, H), dtype=jnp.float32)
        w_router = jax.random.normal(ks[1], (H, E), dtype=jnp.float32) * 0.02
        w1 = jax.random.normal(ks[2], (E, H, F), dtype=jnp.float32) * 0.02
        b1 = jnp.zeros((E, F), dtype=jnp.float32)
        w2 = jax.random.normal(ks[3], (E, F, H), dtype=jnp.float32) * 0.02
        b2 = jnp.zeros((E, H), dtype=jnp.float32)
        return {'x': x, 'w_router': w_router, 'w1': w1, 'b1': b1, 'w2': w2, 'b2': b2}
    _L3_ffn_all = _L3_ffn_setup()
    _L3_ffn_in = {k: v for k, v in _L3_ffn_all.items() if k in ('w_router', 'w1', 'b1', 'w2', 'b2')}
    del _L3_ffn_all
    return {'x': x, 'txt': txt, 'L0_tok_W1': _L0_tok_in['W1'], 'L0_tok_b1': _L0_tok_in['b1'], 'L0_tok_W2': _L0_tok_in['W2'], 'L0_tok_b2': _L0_tok_in['b2'], 'L0_attn_W_dt': _L0_attn_in['W_dt'], 'L0_attn_b_dt': _L0_attn_in['b_dt'], 'L0_attn_W_B': _L0_attn_in['W_B'], 'L0_attn_W_C': _L0_attn_in['W_C'], 'L0_attn_D_param': _L0_attn_in['D_param'], 'L0_attn_A_log': _L0_attn_in['A_log'], 'L0_attn_gamma': _L0_attn_in['gamma'], 'L0_attn_beta': _L0_attn_in['beta'], 'L0_ffn_gate_w': _L0_ffn_in['gate_w'], 'L0_ffn_fc1_w': _L0_ffn_in['fc1_w'], 'L0_ffn_fc1_b': _L0_ffn_in['fc1_b'], 'L0_ffn_geglu_mult': _L0_ffn_in['geglu_mult'], 'L0_ffn_fc2_w': _L0_ffn_in['fc2_w'], 'L0_ffn_fc2_b': _L0_ffn_in['fc2_b'], 'L0_ffn_s_fc1_w': _L0_ffn_in['s_fc1_w'], 'L0_ffn_s_fc1_b': _L0_ffn_in['s_fc1_b'], 'L0_ffn_s_geglu_mult': _L0_ffn_in['s_geglu_mult'], 'L0_ffn_s_fc2_w': _L0_ffn_in['s_fc2_w'], 'L0_ffn_s_fc2_b': _L0_ffn_in['s_fc2_b'], 'L1_attn_W_f': _L1_attn_in['W_f'], 'L1_attn_b_f': _L1_attn_in['b_f'], 'L1_attn_W_down': _L1_attn_in['W_down'], 'L1_ffn_W_fc': _L1_ffn_in['W_fc'], 'L1_ffn_ln_w': _L1_ffn_in['ln_w'], 'L1_ffn_ln_b': _L1_ffn_in['ln_b'], 'L1_ffn_W_proj': _L1_ffn_in['W_proj'], 'L2_attn_W_theta': _L2_attn_in['W_theta'], 'L2_attn_W_phi': _L2_attn_in['W_phi'], 'L2_attn_W_g': _L2_attn_in['W_g'], 'L2_ffn_w_gate': _L2_ffn_in['w_gate'], 'L2_ffn_w_up': _L2_ffn_in['w_up'], 'L2_ffn_w_down': _L2_ffn_in['w_down'], 'L3_attn_params': _L3_attn_in['params'], 'L3_attn_Wv': _L3_attn_in['Wv'], 'L3_attn_bv': _L3_attn_in['bv'], 'L3_attn_Wo': _L3_attn_in['Wo'], 'L3_attn_bo': _L3_attn_in['bo'], 'L3_ffn_w_router': _L3_ffn_in['w_router'], 'L3_ffn_w1': _L3_ffn_in['w1'], 'L3_ffn_b1': _L3_ffn_in['b1'], 'L3_ffn_w2': _L3_ffn_in['w2'], 'L3_ffn_b2': _L3_ffn_in['b2']}

def reference(x, txt, L0_tok_W1, L0_tok_b1, L0_tok_W2, L0_tok_b2, L0_attn_W_dt, L0_attn_b_dt, L0_attn_W_B, L0_attn_W_C, L0_attn_D_param, L0_attn_A_log, L0_attn_gamma, L0_attn_beta, L0_ffn_gate_w, L0_ffn_fc1_w, L0_ffn_fc1_b, L0_ffn_geglu_mult, L0_ffn_fc2_w, L0_ffn_fc2_b, L0_ffn_s_fc1_w, L0_ffn_s_fc1_b, L0_ffn_s_geglu_mult, L0_ffn_s_fc2_w, L0_ffn_s_fc2_b, L1_attn_W_f, L1_attn_b_f, L1_attn_W_down, L1_ffn_W_fc, L1_ffn_ln_w, L1_ffn_ln_b, L1_ffn_W_proj, L2_attn_W_theta, L2_attn_W_phi, L2_attn_W_g, L2_ffn_w_gate, L2_ffn_w_up, L2_ffn_w_down, L3_attn_params, L3_attn_Wv, L3_attn_bv, L3_attn_Wo, L3_attn_bo, L3_ffn_w_router, L3_ffn_w1, L3_ffn_b1, L3_ffn_w2, L3_ffn_b2):
    import jax
    import jax.numpy as jnp

    def _L0_tok_ref(x, W1, b1, W2, b2):
        import jax, jax.numpy as jnp
        import numpy as np
        P = 16
        C = 3
        D = 256

        def _patchify(x, p):
            B, Cc, H, W = x.shape
            gh, gw = (H // p, W // p)
            x = x.reshape(B, Cc, gh, p, gw, p)
            x = x.transpose(0, 2, 4, 1, 3, 5)
            return x.reshape(B, gh * gw, Cc * p * p)
        patches = _patchify(x, P)
        h = jax.nn.silu(jnp.einsum('blk,kd->bld', patches, W1) + b1)
        return jnp.einsum('bld,de->ble', h, W2) + b2

    def _L0_attn_ref(x, W_dt, b_dt, W_B, W_C, D_param, A_log, gamma, beta):
        import jax, jax.numpy as jnp
        import numpy as np
        Bsz, L, D, N = (2, 512, 256, 16)
        LN_EPS = 1e-05
        residual = x
        mu = jnp.mean(x, axis=-1, keepdims=True)
        var = jnp.var(x, axis=-1, keepdims=True)
        xn = (x - mu) * jax.lax.rsqrt(var + LN_EPS) * gamma + beta
        dt = jax.nn.softplus(xn @ W_dt.T + b_dt)
        A = -jnp.exp(A_log)
        B_in = xn @ W_B.T
        C_in = xn @ W_C.T
        A_bar = jnp.exp(dt[..., None] * A)
        Bx = dt[..., None] * B_in[:, :, None, :] * xn[..., None]

        def step(h, inputs):
            a_t, bx_t, c_t = inputs
            h = a_t * h + bx_t
            y_t = jnp.einsum('bn,bdn->bd', c_t, h)
            return (h, y_t)
        h0 = jnp.zeros((x.shape[0], D, N), x.dtype)
        _, ys = jax.lax.scan(step, h0, (jnp.transpose(A_bar, (1, 0, 2, 3)), jnp.transpose(Bx, (1, 0, 2, 3)), jnp.transpose(C_in, (1, 0, 2))))
        y = jnp.transpose(ys, (1, 0, 2)) + D_param * residual
        return y

    def _L0_ffn_ref(x, gate_w, fc1_w, fc1_b, geglu_mult, fc2_w, fc2_b, s_fc1_w, s_fc1_b, s_geglu_mult, s_fc2_w, s_fc2_b):
        import jax, jax.numpy as jnp
        import numpy as np
        S, B, D = (256, 2, 256)
        E, TOPK = (15, 3)
        F = 256
        FS = 512

        def _uinit(k, shape, out_dim):
            std = out_dim ** (-0.5)
            return jax.random.uniform(k, shape, jnp.float32, -std, std)
        s, b, d = x.shape
        xt = x.reshape(-1, d)
        T = xt.shape[0]
        logits = xt @ gate_w.T
        scores = jax.nn.softmax(logits, axis=-1)
        topk_w, topk_idx = jax.lax.top_k(scores, TOPK)
        topk_w = topk_w / (jnp.sum(topk_w, axis=-1, keepdims=True) + 1e-20)
        comb = jnp.zeros((T, E), xt.dtype).at[jnp.arange(T)[:, None], topk_idx].add(topk_w)
        h = jnp.einsum('td,efd->etf', xt, fc1_w) + fc1_b[:, None, :]
        xh, g = (h[..., :F], h[..., F:])
        a = jax.nn.gelu(g, approximate=False) * xh * geglu_mult[:, None, :]
        yexp = jnp.einsum('etf,edf->etd', a, fc2_w) + fc2_b[:, None, :]
        y = jnp.einsum('etd,te->td', yexp, comb)
        hs = xt @ s_fc1_w.T + s_fc1_b
        xs, gs = (hs[..., :FS], hs[..., FS:])
        as_ = jax.nn.gelu(gs, approximate=False) * xs * s_geglu_mult
        ys = as_ @ s_fc2_w.T + s_fc2_b
        return (y + ys).reshape(s, b, d)

    def _L1_attn_ref(x, W_f, b_f, W_down):
        import jax, jax.numpy as jnp
        import numpy as np
        LOG_HALF = float(np.log(0.5))

        def log_g(x):
            return jnp.where(x >= 0.0, jnp.log(jnp.maximum(x, 0.0) + 0.5), -jax.nn.softplus(-x))
        B, T, D = x.shape
        E = W_down.shape[1]
        kz, h_x = jnp.split(jnp.einsum('btd,ed->bte', x, W_f) + b_f, 2, axis=-1)
        log_z = -jax.nn.softplus(-kz)
        log_coeffs = -jax.nn.softplus(kz)
        log_tilde_h = log_g(h_x)
        log_h0 = jnp.full((B, 1, E), LOG_HALF, dtype=x.dtype)
        log_values = jnp.concatenate([log_h0, log_tilde_h + log_z], axis=1)
        a_star = jnp.concatenate([jnp.zeros((B, 1, E), dtype=x.dtype), jnp.cumsum(log_coeffs, axis=1)], axis=1)
        log_h = a_star + jax.lax.cumlogsumexp(log_values - a_star, axis=1)
        h = jnp.exp(log_h)[:, 1:]
        return jnp.einsum('bte,de->btd', h, W_down)

    def _L1_ffn_ref(x, W_fc, ln_w, ln_b, W_proj):
        import jax, jax.numpy as jnp
        import numpy as np
        EPS = 1e-06
        LN_EPS = 1e-05

        def _absmean_core(W):
            gamma = jnp.mean(jnp.abs(W)) + EPS
            Ws = W / gamma
            Wq = jnp.sign(Ws) * jnp.minimum(jnp.round(jnp.abs(Ws)), 1.0)
            return (Wq, gamma)

        @jax.custom_vjp
        def absmean(W):
            return _absmean_core(W)[0]

        def _absmean_fwd(W):
            Wq, gamma = _absmean_core(W)
            return (Wq, gamma)

        def _absmean_bwd(gamma, g):
            return (g / gamma,)
        absmean.defvjp(_absmean_fwd, _absmean_bwd)

        def layernorm(x, w, b, eps=LN_EPS):
            mu = jnp.mean(x, axis=-1, keepdims=True)
            var = jnp.mean((x - mu) ** 2, axis=-1, keepdims=True)
            return (x - mu) * jax.lax.rsqrt(var + eps) * w + b
        h = jnp.einsum('btd,hd->bth', x, absmean(W_fc))
        h = jax.nn.gelu(h, approximate=False)
        h = layernorm(h, ln_w, ln_b)
        return jnp.einsum('bth,dh->btd', h, absmean(W_proj))

    def _L2_attn_ref(x, W_theta, W_phi, W_g):
        import jax, jax.numpy as jnp
        import numpy as np
        import math
        IN_DIM = 256
        LATENT_DIM = 64
        OUT_DIM = 256

        def _kaiming(key, fan_out, fan_in):
            std = math.sqrt(2.0 / fan_in)
            return jax.random.normal(key, (fan_out, fan_in), dtype=jnp.float32) * std
        theta_x = jnp.einsum('bnf,lf->bnl', x, W_theta)
        phi_x = jnp.einsum('bnf,lf->bnl', x, W_phi)
        fun_g_x = jnp.einsum('bnf,of->bno', x, W_g)
        scale = 1.0 / math.sqrt(IN_DIM)
        att = jnp.einsum('bnl,bml->bnm', theta_x, phi_x) * scale
        return jnp.einsum('bnm,bmo->bno', att, fun_g_x)

    def _L2_ffn_ref(x, w_gate, w_up, w_down):
        import jax, jax.numpy as jnp
        import numpy as np
        HIDDEN = 256
        INNER = 1024

        def _weight_quant(w):
            scale = 1.0 / jnp.clip(jnp.mean(jnp.abs(w)), 1e-05)
            wq = jnp.clip(jnp.round(w * scale), -1.0, 1.0) / scale
            return w + jax.lax.stop_gradient(wq - w)

        def _act_quant(x):
            scale = 127.0 / jnp.clip(jnp.max(jnp.abs(x), axis=-1, keepdims=True), 1e-05)
            xq = jnp.clip(jnp.round(x * scale), -128.0, 127.0) / scale
            return x + jax.lax.stop_gradient(xq - x)

        def _bitlinear(x, w):
            return jnp.einsum('bsi,oi->bso', _act_quant(x), _weight_quant(w))
        gate = jax.nn.silu(_bitlinear(x, w_gate))
        up = _bitlinear(x, w_up)
        return _bitlinear(gate * up, w_down)

    def _L3_attn_ref(x, params, Wv, bv, Wo, bo):
        import jax, jax.numpy as jnp
        import numpy as np
        B, S, E, H = (2, 512, 256, 16)
        D = E // H
        TRIL = D * (D + 1) // 2
        bs, seq_len, emb_dim = x.shape
        d = D
        rows, cols = jnp.tril_indices(d)
        tril = jnp.zeros((H, d, d), dtype=x.dtype).at[:, rows, cols].set(params)
        Wqk = jnp.einsum('hij,hkj->hik', tril, tril)
        xh = x.reshape(bs, seq_len, H, d)
        t = jnp.einsum('bshd,hde->bshe', xh, Wqk)
        scores = jnp.einsum('bshe,bthe->bhst', t, xh) / jnp.sqrt(jnp.asarray(d, x.dtype))
        attn = jax.nn.softmax(scores, axis=-1)
        Vh = (x @ Wv.T + bv).reshape(bs, seq_len, H, d)
        out = jnp.einsum('bhst,bthd->bshd', attn, Vh).reshape(bs, seq_len, emb_dim)
        return out @ Wo.T + bo

    def _L3_ffn_ref(x, w_router, w1, b1, w2, b2):
        import jax, jax.numpy as jnp
        import numpy as np
        B, S, H, F, E = (2, 512, 256, 1024, 8)
        'Top-1 MoE layer: route -> per-expert FFN -> weighted combine.\n\n            Faithful to ExpertParallelWrapper._process_moe_layer on a single group:\n            router picks one expert per token with a routing weight; tokens are\n            dispatched to experts (here expressed as a static mask over the fixed\n            expert set), processed by the expert FFN, and scatter-combined back\n            weighted by the routing probability.\n            '
        Bs, Ss, Hs = x.shape
        n_experts = w1.shape[0]
        logits = jnp.einsum('bsh,he->bse', x, w_router)
        probs = jax.nn.softmax(logits, axis=-1)
        sel = jnp.argmax(probs, axis=-1)
        wgt = jnp.take_along_axis(probs, sel[..., None], axis=-1)[..., 0]
        xt = x.reshape(-1, Hs)
        sel_t = sel.reshape(-1)
        wgt_t = wgt.reshape(-1)
        out = jnp.zeros_like(xt)
        for e in range(n_experts):
            h = jax.nn.relu(xt @ w1[e] + b1[e])
            y = h @ w2[e] + b2[e]
            m = (sel_t == e).astype(xt.dtype) * wgt_t
            out = out + m[:, None] * y
        return out.reshape(Bs, Ss, Hs)
    h = _L0_tok_ref(x, L0_tok_W1, L0_tok_b1, L0_tok_W2, L0_tok_b2)
    h = jnp.concatenate([h, txt], axis=1)
    h = h + _L0_attn_ref(_layernorm(h, axis=-1), L0_attn_W_dt, L0_attn_b_dt, L0_attn_W_B, L0_attn_W_C, L0_attn_D_param, L0_attn_A_log, L0_attn_gamma, L0_attn_beta)
    h = h + _L0_ffn_ref(_layernorm(h, axis=-1), L0_ffn_gate_w, L0_ffn_fc1_w, L0_ffn_fc1_b, L0_ffn_geglu_mult, L0_ffn_fc2_w, L0_ffn_fc2_b, L0_ffn_s_fc1_w, L0_ffn_s_fc1_b, L0_ffn_s_geglu_mult, L0_ffn_s_fc2_w, L0_ffn_s_fc2_b)
    h = h + _L1_attn_ref(_layernorm(h, axis=-1), L1_attn_W_f, L1_attn_b_f, L1_attn_W_down)
    h = h + _L1_ffn_ref(_layernorm(h, axis=-1), L1_ffn_W_fc, L1_ffn_ln_w, L1_ffn_ln_b, L1_ffn_W_proj)
    h = h + _L2_attn_ref(_layernorm(h, axis=-1), L2_attn_W_theta, L2_attn_W_phi, L2_attn_W_g)
    h = h + _L2_ffn_ref(_layernorm(h, axis=-1), L2_ffn_w_gate, L2_ffn_w_up, L2_ffn_w_down)
    h = h + _L3_attn_ref(_layernorm(h, axis=-1), L3_attn_params, L3_attn_Wv, L3_attn_bv, L3_attn_Wo, L3_attn_bo)
    h = h + _L3_ffn_ref(_layernorm(h, axis=-1), L3_ffn_w_router, L3_ffn_w1, L3_ffn_b1, L3_ffn_w2, L3_ffn_b2)
    return h

_drawn_inputs = setup_inputs


def setup_inputs(seed=0):
    import zlib

    import numpy as np

    out = dict(_drawn_inputs(seed))
    spreads = {'L0_attn_b_dt': (0.0, 0.1),
     'L0_attn_D_param': (1.0, 0.2),
     'L0_attn_gamma': (1.0, 0.2),
     'L0_attn_beta': (0.0, 0.1),
     'L0_ffn_geglu_mult': (1.0, 0.6),
     'L0_ffn_s_geglu_mult': (1.0, 0.6),
     'L1_ffn_ln_w': (1.0, 0.2),
     'L1_ffn_ln_b': (0.0, 0.1),
     'L3_ffn_b1': (0.0, 2.0),
     'L3_ffn_b2': (0.0, 2.0)}
    factors = {'L0_ffn_fc1_b': 8.0,
     'L0_ffn_s_fc1_b': 8.0,
     'L1_attn_b_f': 8.0,
     'L2_ffn_w_gate': 8.0,
     'L2_ffn_w_up': 8.0,
     'L2_ffn_w_down': 8.0,
     'L3_attn_params': 8.0,
     'L3_attn_Wv': 8.0,
     'L3_attn_bv': 64.0,
     'L3_attn_Wo': 8.0,
     'L3_attn_bo': 200.0,
     'L3_ffn_w_router': 8.0,
     'L3_ffn_w1': 8.0,
     'L3_ffn_w2': 8.0}
    for name, (base, spread) in spreads.items():
        noise = np.random.default_rng([zlib.crc32(name.encode()), seed]).standard_normal(out[name].shape)
        drawn = base * np.exp(spread * noise) if base else spread * noise
        out[name] = jnp.asarray(drawn.astype(out[name].dtype))
    for name, factor in factors.items():
        out[name] = (out[name] * factor).astype(out[name].dtype)
    return out
```

```python
import numpy as np
import concourse.bass as bass
from concourse import mybir
from contextlib import ExitStack

F32 = mybir.dt.float32
F16 = mybir.dt.float16
I32 = mybir.dt.int32
U32 = mybir.dt.uint32
ALU = mybir.AluOpType
ACT = mybir.ActivationFunctionType
AX = mybir.AxisListType

NB = 16
L = 113
LP = 36
D = 256
KC = D // 128
GB = 4
NG = NB // GB
GT = GB * L
T = NB * L
WS = 64.0
EPS = 1e-5


def wait_alone(eng, core, sem, value):
    if not isinstance(value, int):
        value = eng.to_reg(value)
    eng.wait_ge(core.gate, 1)
    eng.wait_ge(sem, value)


class Chain:

    def __init__(self, eng, sem, base=0):
        self.eng, self.sem, self.base, self.n = eng, sem, base, 0

    def step(self, ins):
        ins.then_inc(self.sem, 1)
        self.n += 1
        self.eng.wait_ge(self.sem, self.base + self.n)


class Stage:

    available, resting = [], []

    def __init__(self, nc, name):
        self.nc, self.name, self.ctx, self.sems = nc, name, ExitStack(), []

    def __enter__(self):
        return self

    def sb(self, name, shape, dt=F32):
        return self.ctx.enter_context(self.nc.sbuf_tensor(f"{self.name}_{name}", shape, dt))

    def ps(self, name, shape, dt=F32):
        return self.ctx.enter_context(self.nc.psum_tensor(f"{self.name}_{name}", shape, dt))

    def sem(self, name):
        number = Stage.available.pop(0)
        self.sems.append(self.nc.alloc_semaphore(f"{self.name}_{name}", number))
        return self.sems[-1]

    def __exit__(self, *exc):
        self.ctx.close()
        if exc[0] is None and self.sems:
            numbers = [s.num for s in self.sems]
            self.nc.clear_and_free_semaphores(self.sems)
            Stage.available += Stage.resting
            Stage.resting = numbers
        return False


class Core:
    pass


def split_weights(st, core, loads):
    bufs, sems = [], []
    for name, dram, hi, lo in loads:
        bufs.append(st.sb(f"{name}_f32", list(dram.shape)))
        sems.append(st.sem(f"{name}_landed"))
    hi_done = st.sem("weights_hi")
    ready = st.sem("weights_split")

    def on_sync(sp):
        for (name, dram, hi, lo), buf, landed in zip(loads, bufs, sems):
            sp.dma_start(buf[:], dram).then_inc(landed, 16)

    def on_scalar(act):
        for (name, dram, hi, lo), buf, landed in zip(loads, bufs, sems):
            act.wait_ge(landed, 16)
            act.activation(hi, buf[:], ACT.Copy, scale=WS).then_inc(hi_done, 1)

    def on_vector(dve):
        for n, ((name, dram, hi, lo), buf) in enumerate(zip(loads, bufs)):
            dve.wait_ge(hi_done, n + 1)
            dve.scalar_tensor_tensor(lo, buf[:], WS, hi, ALU.mult, ALU.subtract).then_inc(ready, 1)

    return on_sync, on_scalar, on_vector, (ready, len(loads))


def mm3(pe, out, w_hi, w_lo, x_hi, x_lo, start, stop):
    pe.matmul(out, w_hi, x_hi, start=start, stop=False)
    pe.matmul(out, w_hi, x_lo, start=False, stop=False)
    return pe.matmul(out, w_lo, x_hi, start=False, stop=stop)


def stage_constants(nc, core):
    with Stage(nc, "const") as st:
        zeroed, made, cast = st.sem("zeroed"), st.sem("made"), st.sem("cast")
        with nc.Block() as block:
            @block.gpsimd
            def _(pool):
                pool.memset(core.ident[:, :], 0.0).then_inc(zeroed, 1)
                pool.wait_ge(zeroed, 1)
                pool.affine_select(out=core.ident[:, :], in_=core.ident[:, :], compare_op=ALU.not_equal, fill=1.0,
                                   base=0, pattern=[[-1, 128]], channel_multiplier=1).then_inc(made, 1)
                pool.memset(core.eps[:, :], EPS)
                pool.memset(core.ones16[:, :], 1.0)
                pool.memset(core.ones[:, :], 1.0)
                pool.wait_ge(made, 1)
                pool.tensor_copy(core.ident16[:, :], core.ident[:, :]).then_inc(cast, 1)
                pool.sem_inc(core.gate, 1)
                pool.wait_ge(cast, 1)


def stage_tokens(nc, core, d):
    PC = 6
    NP = NB * LP
    HP = NP // 2
    with Stage(nc, "tok") as st:
        pt_hi, pt_lo = st.sb("pt_hi", [128, PC, NP], F16), st.sb("pt_lo", [128, PC, NP], F16)
        w1_hi, w1_lo = st.sb("w1_hi", [128, PC, D], F16), st.sb("w1_lo", [128, PC, D], F16)
        w2_hi, w2_lo = st.sb("w2_hi", [128, KC, D], F16), st.sb("w2_lo", [128, KC, D], F16)
        b2_hi, b2_lo = st.sb("b2_hi", [1, D], F16), st.sb("b2_lo", [1, D], F16)
        b1 = st.sb("b1", [128, KC])
        g = st.sb("g", [128, KC, NP])
        g_hi, g_lo = st.sb("g_hi", [128, KC, NP], F16), st.sb("g_lo", [128, KC, NP], F16)
        hid = [st.ps(f"hid{j}", [128, 512]) for j in range(2)]
        emb = [st.ps(f"emb{j}", [128, D]) for j in range(2)]
        consts = st.sem("consts_landed")
        hid_ready, hid_free = st.sem("hid_ready"), st.sem("hid_free")
        g_high, g_split = st.sem("g_high"), st.sem("g_split")
        emb_ready = [st.sem(f"emb_ready{j}") for j in range(2)]
        emb_free = [st.sem(f"emb_free{j}") for j in range(2)]
        text = st.sem("text_landed")
        w_sync, w_act, w_dve, (w_ready, w_n) = split_weights(st, core, [
            ("w1", d["w1"], w1_hi[:].rearrange("p c n -> p (c n)"), w1_lo[:].rearrange("p c n -> p (c n)")),
            ("pt", d["patches"], pt_hi[:].rearrange("p c n -> p (c n)"), pt_lo[:].rearrange("p c n -> p (c n)")),
            ("w2", d["w2"], w2_hi[:].rearrange("p c n -> p (c n)"), w2_lo[:].rearrange("p c n -> p (c n)")),
            ("b2", d["b2"], b2_hi[:], b2_lo[:]),
        ])
        units = [(c, s) for c in range(KC) for s in range(2)]
        with nc.Block() as block:
            @block.sync
            def _(sp):
                w_sync(sp)
                sp.dma_start(b1[:], d["b1"]).then_inc(consts, 16)
                sp.dma_start(core.h[LP:L, :, :], d["txt"]).then_inc(text, 16)
                sp.wait_ge(text, 16)

            @block.scalar
            def _(act):
                w_act(act)
                act.wait_ge(consts, 16)
                for n, (c, s) in enumerate(units):
                    act.wait_ge(hid_ready, n + 1)
                    act.activation(g[:, c, s * HP:(s + 1) * HP], hid[n % 2][:, 0:HP], ACT.Silu, bias=b1[:, c:c + 1],
                                   scale=1.0 / (WS * WS)).then_inc(hid_free, 1)
                    act.wait_ge(hid_free, n + 1)
                    act.activation(g_hi[:, c, s * HP:(s + 1) * HP], g[:, c, s * HP:(s + 1) * HP],
                                   ACT.Copy).then_inc(g_high, 1)

            @block.vector
            def _(dve):
                w_dve(dve)
                for n, (c, s) in enumerate(units):
                    dve.wait_ge(g_high, n + 1)
                    dve.tensor_tensor(g_lo[:, c, s * HP:(s + 1) * HP], g[:, c, s * HP:(s + 1) * HP],
                                      g_hi[:, c, s * HP:(s + 1) * HP], ALU.subtract).then_inc(g_split, 1)
                with dve.Fori(0, NB // 2) as i:
                    for j in range(2):
                        dve.wait_ge(emb_ready[j], i + 1)
                        dve.tensor_scalar(core.h[0:LP, bass.ds(2 * i + j, 1), :],
                                          emb[j][0:LP, :].rearrange("p (a n) -> p a n", a=1),
                                          1.0 / WS, None, ALU.mult).then_inc(emb_free[j], 1)

            @block.tensor
            def _(pe):
                pe.wait_ge(w_ready, w_n)
                for n, (c, s) in enumerate(units):
                    if n >= 2:
                        pe.wait_ge(hid_free, n - 1)
                    for k in range(PC):
                        last = mm3(pe, hid[n % 2][:, 0:HP], w1_hi[:, k, c * 128:(c + 1) * 128],
                                   w1_lo[:, k, c * 128:(c + 1) * 128], pt_hi[:, k, s * HP:(s + 1) * HP],
                                   pt_lo[:, k, s * HP:(s + 1) * HP], k == 0, k == PC - 1)
                    last.then_inc(hid_ready, 1)
                pe.wait_ge(g_split, len(units))
                with pe.Fori(0, NB // 2) as i:
                    for j in range(2):
                        pe.wait_ge(emb_free[j], i)
                        tok = bass.ds(i * (2 * LP) + j * LP, LP)
                        for k in range(KC):
                            mm3(pe, emb[j][0:LP, :], g_hi[:, k, tok], g_lo[:, k, tok],
                                w2_hi[:, k, :], w2_lo[:, k, :], k == 0, False)
                        pe.matmul(emb[j][0:LP, :], core.ones16[0:1, 0:LP], b2_hi[:], start=False, stop=False)
                        pe.matmul(emb[j][0:LP, :], core.ones16[0:1, 0:LP], b2_lo[:], start=False,
                                  stop=True).then_inc(emb_ready[j], 1)


def stage_norm_stats(nc, core, name, src, second=None):
    with Stage(nc, name) as st:
        six = st.sb("six", [L, NB, 6])
        s, dd, sd = st.sb("s", [L, NB]), st.sb("dd", [L, NB]), st.sb("sd", [L, NB])
        var = st.sb("var", [L, NB])
        counted, chain_sem = st.sem("counted"), st.sem("chain")
        var_ready, sd_ready = st.sem("var_ready"), st.sem("sd_ready")
        with nc.Block() as block:
            @block.scalar
            def _(act):
                act.preload_act_table(ACT.Sqrt)
                act.wait_ge(var_ready, 1)
                act.activation(sd[:], var[:], ACT.Sqrt, bias=core.eps[0:L, :], scale=1.0 / D).then_inc(sd_ready, 1)

            @block.vector
            def _(dve):
                with dve.Fori(0, NB) as b:
                    dve.bn_stats(six[:, bass.ds(b, 1), :], src[:, bass.ds(b, 1), :]).then_inc(counted, 1)
                dve.wait_ge(counted, NB)
                norm_moments(dve, Chain(dve, chain_sem), six, s, dd, var, core.mean, var_ready)
                dve.wait_ge(sd_ready, 1)
                dve.reciprocal(core.rstd[:], sd[:]).then_inc(counted, 1)
                dve.wait_ge(counted, NB + 1)


def norm_moments(dve, chain, six, s, dd, var, mean, var_ready):
    me, m2e, mo, m2o = six[:, :, 1], six[:, :, 2], six[:, :, 4], six[:, :, 5]
    dve.tensor_tensor(s[:], me, mo, ALU.add)
    chain.step(dve.tensor_tensor(dd[:], me, mo, ALU.subtract))
    dve.tensor_scalar(mean[:], s[:], 0.5, None, ALU.mult)
    chain.step(dve.tensor_tensor(dd[:], dd[:], dd[:], ALU.mult))
    chain.step(dve.scalar_tensor_tensor(var[:], dd[:], D / 4.0, m2e, ALU.mult, ALU.add))
    dve.tensor_tensor(var[:], var[:], m2o, ALU.add).then_inc(var_ready, 1)


def stage_features(nc, core, name, src, affine=None, full=None, rows=None):
    with Stage(nc, name) as st:
        xr = [st.sb(f"xr{u}", [L, GB, D]) for u in range(2)]
        tp = [[st.ps(f"tp{u}{c}", [128, 512]) for c in range(KC)] for u in range(2)]
        normed, tp_ready, hi_done = st.sem("normed"), st.sem("tp_ready"), st.sem("hi_done")
        tp_free = [st.sem(f"tp_free{u}") for u in range(2)]
        if affine is not None:
            full_done = st.sem("full_done")
        if rows is not None:
            parts = [st.sb(f"parts{u}", [L, GB, 2, D], F16) for u in range(2)]
            row_hi, row_lo = st.sem("row_hi"), st.sem("row_lo")
            stored = [st.sem(f"stored{u}") for u in range(2)]
        with nc.Block() as block:
            @block.vector
            def _(dve):
                with dve.Fori(0, NG // 2) as i:
                    for u in range(2):
                        if rows is not None:
                            dve.wait_ge(row_lo, i * 2)
                        for j in range(GB):
                            b = bass.ds(i * (2 * GB) + (u * GB + j), 1)
                            dve.tensor_scalar(xr[u][:, j, :].rearrange("p (a n) -> p a n", a=1), src[:, b, :],
                                              core.mean[:, b], core.rstd[:, b],
                                              ALU.subtract, ALU.mult).then_inc(normed, 1)
                    for u in range(2):
                        for c in range(KC):
                            done = i * 4 + (u * KC + c + 1)
                            cols = bass.ds(i * (2 * GT) + u * GT, GT)
                            source = tp[u][c][:, 0:GT]
                            dve.wait_ge(hi_done, done)
                            if affine is not None:
                                source = full[:, c, cols]
                                dve.tensor_scalar(source, tp[u][c][:, 0:GT], affine[0][:, c:c + 1],
                                                  affine[1][:, c:c + 1], ALU.mult, ALU.add).then_inc(full_done, 1)
                                dve.wait_ge(full_done, done)
                            dve.tensor_tensor(core.xt_lo[:, c, cols], source, core.xt_hi[:, c, cols],
                                              ALU.subtract).then_inc(tp_free[u], 1)

            @block.tensor
            def _(pe):
                with pe.Fori(0, NG // 2) as i:
                    for u in range(2):
                        pe.wait_ge(tp_free[u], i * KC)
                        for j in range(GB):
                            pe.wait_ge(normed, i * 8 + (u * 4 + j + 1))
                            for c in range(KC):
                                last = pe.transpose(tp[u][c][:, j * L:(j + 1) * L], xr[u][:, j, c * 128:(c + 1) * 128],
                                                    core.ident[0:L, 0:L])
                                if j == GB - 1:
                                    last.then_inc(tp_ready, 1)

            @block.scalar
            def _(act):
                with act.Fori(0, NG // 2) as i:
                    for u in range(2):
                        for c in range(KC):
                            cols = bass.ds(i * (2 * GT) + u * GT, GT)
                            act.wait_ge(tp_ready, i * 4 + (u * KC + c + 1))
                            if affine is not None:
                                act.activation(core.xt_hi[:, c, cols], tp[u][c][:, 0:GT], ACT.Identity,
                                               bias=affine[1][:, c:c + 1],
                                               scale=affine[0][:, c:c + 1]).then_inc(hi_done, 1)
                            else:
                                act.activation(core.xt_hi[:, c, cols], tp[u][c][:, 0:GT], ACT.Copy).then_inc(hi_done, 1)
                        if rows is not None:
                            act.wait_ge(stored[u], i * 16)
                            act.activation(parts[u][:, :, 0, :], xr[u][:], ACT.Copy).then_inc(row_hi, 1)

            if rows is not None:
                @block.gpsimd
                def _(pool):
                    with pool.Fori(0, NG // 2) as i:
                        for u in range(2):
                            pool.wait_ge(row_hi, i * 2 + (u + 1))
                            pool.tensor_tensor(parts[u][:, :, 1, :], xr[u][:], parts[u][:, :, 0, :],
                                               ALU.subtract).then_inc(row_lo, 1)

                @block.sync
                def _(sp):
                    table = rows.rearrange("(g b t) n -> g t b n", b=GB, t=L)
                    with sp.Fori(0, NG // 2) as i:
                        for u in range(2):
                            sp.wait_ge(row_lo, i * 2 + (u + 1))
                            sp.dma_start(table[bass.ds(i * 2 + u, 1)].rearrange("a t b n -> (a t) b n"),
                                         parts[u][:].rearrange("p b a n -> p b (a n)")).then_inc(stored[u], 16)
                    for u in range(2):
                        sp.wait_ge(stored[u], 16 * (NG // 2))


def stage_norm_twice(nc, core, d_row):
    with Stage(nc, "twice") as st:
        skip = st.sb("skip", [L, D])
        six = st.sb("six", [L, NB, 6])
        s, dd, sd, var = (st.sb(n, [L, NB]) for n in ("s", "dd", "sd", "var"))
        prod = [st.sb(f"prod{j}", [L, 1, D]) for j in range(2)]
        landed, normed, counted = st.sem("skip_landed"), st.sem("normed"), st.sem("counted")
        chain_sem, pool_mul, pool_add = st.sem("chain"), st.sem("pool_mul"), st.sem("pool_add")
        var_ready, sd_ready = st.sem("var_ready"), st.sem("sd_ready")
        with nc.Block() as block:
            @block.sync
            def _(sp):
                sp.dma_start(skip[:], d_row.partition_broadcast(L)).then_inc(landed, 16)

            @block.vector
            def _(dve):
                with dve.Fori(0, NB) as i:
                    b = bass.ds(i, 1)
                    dve.tensor_scalar(core.xn[:, b, :], core.h[:, b, :], core.mean[:, b], core.rstd[:, b],
                                      ALU.subtract, ALU.mult).then_inc(normed, 1)
                with dve.Fori(0, NB) as i:
                    b = bass.ds(i, 1)
                    dve.wait_ge(normed, i + 1)
                    dve.bn_stats(six[:, b, :], core.xn[:, b, :]).then_inc(counted, 1)
                dve.wait_ge(counted, NB)
                norm_moments(dve, Chain(dve, chain_sem), six, s, dd, var, core.mean, var_ready)
                dve.wait_ge(sd_ready, 1)
                dve.reciprocal(core.rstd[:], sd[:]).then_inc(counted, 1)
                dve.wait_ge(counted, NB + 1)

            @block.scalar
            def _(act):
                act.wait_ge(var_ready, 1)
                act.activation(sd[:], var[:], ACT.Sqrt, bias=core.eps[0:L, :], scale=1.0 / D).then_inc(sd_ready, 1)

            @block.gpsimd
            def _(pool):
                pool.wait_ge(landed, 16)
                with pool.Fori(0, NB // 2) as i:
                    for j in range(2):
                        b = bass.ds(2 * i + j, 1)
                        wait_alone(pool, core, normed, 2 * i + (j + 1))
                        wait_alone(pool, core, pool_add, 2 * i)
                        pool.tensor_tensor(prod[j][:], core.xn[:, b, :], skip[:].rearrange("p (a n) -> p a n", a=1),
                                           ALU.mult).then_inc(pool_mul, 1)
                    for j in range(2):
                        b = bass.ds(2 * i + j, 1)
                        wait_alone(pool, core, pool_mul, 2 * i + 2)
                        pool.tensor_tensor(core.h[:, b, :], core.h[:, b, :], prod[j][:], ALU.add).then_inc(pool_add, 1)


def stage_ssm_inputs(nc, core, d, ssm):
    with Stage(nc, "ssmin") as st:
        wd_hi, wd_lo = st.sb("wd_hi", [128, KC, D], F16), st.sb("wd_lo", [128, KC, D], F16)
        wb_hi, wb_lo = st.sb("wb_hi", [128, 2, KC, 128], F16), st.sb("wb_lo", [128, 2, KC, 128], F16)
        b_dt = st.sb("b_dt", [128, KC])
        alog = st.sb("alog", [128, 32])
        az, ez, lz, rz, dt, dx = ([st.sb(f"{n}{j}", [128, GT]) for j in range(2)]
                                  for n in ("az", "ez", "lz", "rz", "dt", "dx"))
        pd = [st.ps(f"pd{j}", [128, 512]) for j in range(2)]
        pb = [st.ps(f"pb{j}", [128, 512]) for j in range(2)]
        landed = st.sem("landed")
        pd_ready, pd_abs, pd_lin, ln_done = st.sem("pd_ready"), st.sem("pd_abs"), st.sem("pd_lin"), st.sem("ln_done")
        pb_ready, pb_free = st.sem("pb_ready"), st.sem("pb_free")
        act_chain, neg = st.sem("act_chain"), st.sem("neg")
        dt_done, dt_hi, dx_done, dx_hi, split = (st.sem(n) for n in ("dt_done", "dt_hi", "dx_done", "dx_hi", "split"))
        flat = lambda t: t[:].rearrange("p a n -> p (a n)")
        w_sync, w_act, w_dve, (w_ready, w_n) = split_weights(st, core, [
            ("wd", d["w_dt"], flat(wd_hi), flat(wd_lo)),
            ("wb", d["w_bc"], wb_hi[:].rearrange("p s c n -> p (s c n)"), wb_lo[:].rearrange("p s c n -> p (s c n)")),
        ])
        with nc.Block() as block:
            @block.sync
            def _(sp):
                w_sync(sp)
                sp.dma_start(b_dt[:], d["b_dt"]).then_inc(landed, 16)
                sp.dma_start(alog[:], d["a_log"]).then_inc(landed, 16)

            @block.tensor
            def _(pe):
                pe.wait_ge(w_ready, w_n)
                with pe.Fori(0, NG) as i:
                    cols = bass.ds(i * GT, GT)
                    for c in range(KC):
                        pe.wait_ge(pd_lin, i * 2)
                        pe.wait_ge(pd_abs, i * 2)
                        for k in range(KC):
                            last = mm3(pe, pd[c][:, 0:GT], wd_hi[:, k, c * 128:(c + 1) * 128],
                                       wd_lo[:, k, c * 128:(c + 1) * 128], core.xt_hi[:, k, cols],
                                       core.xt_lo[:, k, cols], k == 0, k == KC - 1)
                        last.then_inc(pd_ready, 1)
                    for s in range(2):
                        pe.wait_ge(pb_free, i * 2)
                        for k in range(KC):
                            last = mm3(pe, pb[s][:, 0:GT], wb_hi[:, s, k, :], wb_lo[:, s, k, :],
                                       core.xt_hi[:, k, cols], core.xt_lo[:, k, cols], k == 0, k == KC - 1)
                        last.then_inc(pb_ready, 1)

            @block.scalar
            def _(act):
                act.preload_act_table_set("natural_log_exp_and_others")
                w_act(act)
                act.wait_ge(landed, 32)
                act.activation(ssm.a[:], alog[:], ACT.Exp).then_inc(neg, 1)
                act.wait_ge(neg, 1)
                act.activation(ssm.a[:], ssm.a[:], ACT.Copy, scale=-1.0).then_inc(neg, 1)
                with act.Fori(0, NG) as i:
                    cols = bass.ds(i * GT, GT)
                    for c in range(KC):
                        act.wait_ge(pd_ready, i * 2 + (c + 1))
                        act.activation(az[c][:], pd[c][:, 0:GT], ACT.Abs, bias=b_dt[:, c:c + 1],
                                       scale=1.0 / WS).then_inc(pd_abs, 1)
                    for c in range(KC):
                        act.wait_ge(pd_abs, i * 2 + (c + 1))
                        act.activation(ez[c][:], az[c][:], ACT.Exp, scale=-1.0).then_inc(act_chain, 1)
                    for c in range(KC):
                        act.wait_ge(act_chain, i * 2 + (c + 1))
                        act.wait_ge(dt_done, i * 2)
                        act.activation(lz[c][:], ez[c][:], ACT.Ln, bias=1.0).then_inc(ln_done, 1)
                    for s, dst in enumerate((ssm.bt, ssm.ct)):
                        act.wait_ge(pb_ready, i * 2 + (s + 1))
                        act.activation(dst[:, cols], pb[s][:, 0:GT], ACT.Copy, scale=1.0 / WS).then_inc(pb_free, 1)
                    for c in range(KC):
                        act.wait_ge(dt_done, i * 2 + (c + 1))
                        act.activation(ssm.dt_hi[:, c, cols], dt[c][:], ACT.Copy).then_inc(dt_hi, 1)
                    for c in range(KC):
                        act.wait_ge(dx_done, i * 2 + (c + 1))
                        act.activation(ssm.dx_hi[:, c, cols], dx[c][:], ACT.Copy).then_inc(dx_hi, 1)
                act.wait_ge(neg, 2)

            @block.vector
            def _(dve):
                w_dve(dve)
                dve.wait_ge(landed, 32)
                with dve.Fori(0, NG) as i:
                    cols = bass.ds(i * GT, GT)
                    for c in range(KC):
                        dve.wait_ge(pd_abs, i * 2 + (c + 1))
                        dve.tensor_scalar(rz[c][:], pd[c][:, 0:GT], 1.0 / WS, b_dt[:, c:c + 1],
                                          ALU.mult, ALU.add).then_inc(pd_lin, 1)
                    for c in range(KC):
                        dve.wait_ge(ln_done, i * 2 + (c + 1))
                        dve.wait_ge(pd_lin, i * 2 + (c + 1))
                        dve.wait_ge(split, i * 4)
                        dve.scalar_tensor_tensor(dt[c][:], rz[c][:], 0.0, lz[c][:],
                                                 ALU.max, ALU.add).then_inc(dt_done, 1)
                    for c in range(KC):
                        dve.wait_ge(dt_done, i * 2 + (c + 1))
                        dve.tensor_tensor(dx[c][:], dt[c][:], ssm.xn[:, c, cols], ALU.mult).then_inc(dx_done, 1)
                    for c in range(KC):
                        dve.wait_ge(dt_hi, i * 2 + (c + 1))
                        dve.tensor_tensor(ssm.dt_lo[:, c, cols], dt[c][:], ssm.dt_hi[:, c, cols],
                                          ALU.subtract).then_inc(split, 1)
                    for c in range(KC):
                        dve.wait_ge(dx_hi, i * 2 + (c + 1))
                        dve.tensor_tensor(ssm.dx_lo[:, c, cols], dx[c][:], ssm.dx_hi[:, c, cols],
                                          ALU.subtract).then_inc(split, 1)


def stage_ssm_scan(nc, core, ssm):
    NS, DS = 16, 8
    UN = 128 // DS
    R = 4
    with Stage(nc, "scan") as st:
        sel = st.sb("sel", [128, UN, 128], F16)
        ssum = st.sb("ssum", [128, UN, 128])
        abar = [st.sb(f"abar{r}", [128, GB, L]) for r in range(R)]
        bx = [st.sb(f"bx{r}", [128, GT]) for r in range(R)]
        hs = [st.sb(f"hs{r}", [128, GT]) for r in range(R)]
        ch = [st.sb(f"ch{r}", [128, GT]) for r in range(R)]
        yt = [st.sb(f"yt{r}", [128, GT]) for r in range(2)]
        pdt = [st.ps(f"pdt{j}", [128, 512]) for j in range(2)]
        pdx = [st.ps(f"pdx{j}", [128, 512]) for j in range(2)]
        py = [st.ps(f"py{j}", [128, 512]) for j in range(2)]
        pt = [st.ps(f"pt{j}", [128, GB, 128]) for j in range(2)]
        sel_made, ssum_made, zeroed = st.sem("sel_made"), st.sem("ssum_made"), st.sem("zeroed")
        dt_ready, dx_ready = st.sem("dt_ready"), st.sem("dx_ready")
        decay, drive, scanned, weighed = st.sem("decay"), st.sem("drive"), st.sem("scanned"), st.sem("weighed")
        summed = st.sem("summed")
        y_ready, y_out, turned, added = st.sem("y_ready"), st.sem("y_out"), st.sem("turned"), st.sem("added")
        per_q = KC * UN
        with nc.Block() as block:
            @block.gpsimd
            def _(pool):
                made = Chain(pool, sel_made)
                made.step(pool.memset(sel[:], 0.0))
                made.step(pool.affine_select(out=sel[:].rearrange("p g (s n) -> p g s n", n=NS),
                                             in_=sel[:].rearrange("p g (s n) -> p g s n", n=NS),
                                             compare_op=ALU.not_equal, fill=1.0, base=0,
                                             pattern=[[-DS, UN], [-1, DS], [0, NS]], channel_multiplier=1))
                made.step(pool.memset(ssum[:], 1.0))
                made.step(pool.affine_select(out=ssum[:], in_=ssum[:], compare_op=ALU.is_ge, fill=0.0, base=0,
                                             pattern=[[128, UN], [-NS, 128]], channel_multiplier=1))
                made.step(pool.affine_select(out=ssum[:], in_=ssum[:], compare_op=ALU.is_ge, fill=0.0, base=NS - 1,
                                             pattern=[[-128, UN], [NS, 128]], channel_multiplier=-1))
                with pool.Fori(0, NG) as q:
                    for n in range(per_q):
                        r = n % R
                        wait_alone(pool, core, summed, q * per_q + max(n + 1 - R, 0))
                        wait_alone(pool, core, scanned, q * per_q + (n + 1))
                        pool.tensor_tensor(ch[r][:], hs[r][:], ssm.ct[:, bass.ds(q * GT, GT)],
                                           ALU.mult).then_inc(weighed, 1)

            @block.tensor
            def _(pe):
                pe.wait_ge(sel_made, 5)
                LAG = 3

                def sum_states(q, n):
                    c, g = divmod(n, UN)
                    pe.wait_ge(weighed, q * per_q + (n + 1))
                    if g == 0:
                        pe.wait_ge(y_out, q * KC)
                    ins = pe.matmul(py[c][:, 0:GT], ssum[:, g, :], ch[n % R][:], start=g == 0, stop=g == UN - 1)
                    ins.then_inc(summed, 1)

                def turn(q, c):
                    pe.wait_ge(y_out, q * KC + (c + 1))
                    pe.wait_ge(added, q * KC)
                    for j in range(GB):
                        last = pe.transpose(pt[c][0:L, j, :], yt[c][:, j * L:(j + 1) * L], core.ident[:])
                    last.then_inc(turned, 1)

                with pe.Fori(0, NG) as q:
                    cols = bass.ds(q * GT, GT)
                    for n in range(per_q):
                        c, g = divmod(n, UN)
                        if n >= 2:
                            pe.wait_ge(decay, q * per_q + (n - 1))
                            pe.wait_ge(drive, q * per_q + (n - 1))
                        else:
                            pe.wait_ge(decay, q * per_q)
                            pe.wait_ge(drive, q * per_q)
                        pe.matmul(pdt[n % 2][:, 0:GT], sel[:, g, :], ssm.dt_hi[:, c, cols], start=True, stop=False)
                        pe.matmul(pdt[n % 2][:, 0:GT], sel[:, g, :], ssm.dt_lo[:, c, cols], start=False,
                                  stop=True).then_inc(dt_ready, 1)
                        pe.matmul(pdx[n % 2][:, 0:GT], sel[:, g, :], ssm.dx_hi[:, c, cols], start=True, stop=False)
                        pe.matmul(pdx[n % 2][:, 0:GT], sel[:, g, :], ssm.dx_lo[:, c, cols], start=False,
                                  stop=True).then_inc(dx_ready, 1)
                        if n >= LAG:
                            sum_states(q, n - LAG)
                        if n == UN + LAG + 3:
                            turn(q, 0)
                    for n in range(per_q - LAG, per_q):
                        sum_states(q, n)
                    turn(q, 1)

            @block.scalar
            def _(act):
                act.wait_ge(zeroed, R)

                def copy_out(q, c):
                    act.wait_ge(summed, q * per_q + UN * (c + 1))
                    act.wait_ge(turned, q * KC)
                    act.activation(yt[c][:], py[c][:, 0:GT], ACT.Copy).then_inc(y_out, 1)

                with act.Fori(0, NG) as q:
                    for n in range(per_q):
                        c, g = divmod(n, UN)
                        act.wait_ge(dt_ready, q * per_q + (n + 1))
                        if n >= R:
                            act.wait_ge(scanned, q * per_q + (n + 1 - R))
                        else:
                            act.wait_ge(scanned, q * per_q)
                        act.activation(abar[n % R][:, :, 1:L],
                                       pdt[n % 2][:, 0:GT].rearrange("p (b t) -> p b t", t=L)[:, :, 1:L],
                                       ACT.Exp, scale=ssm.a[:, n:n + 1]).then_inc(decay, 1)
                        if n == UN + 4:
                            copy_out(q, 0)
                    copy_out(q, 1)

            @block.vector
            def _(dve):
                for r in range(R):
                    dve.memset(abar[r][:, :, 0:1], 0.0).then_inc(zeroed, 1)

                def add_y(q, c):
                    dve.wait_ge(turned, q * KC + (c + 1))
                    b = bass.ds(q * GB, GB)
                    half = slice(c * 128, (c + 1) * 128)
                    dve.tensor_tensor(core.h[:, b, half], core.h[:, b, half], pt[c][0:L, :, :],
                                      ALU.add).then_inc(added, 1)

                with dve.Fori(0, NG) as q:
                    for n in range(per_q):
                        r = n % R
                        dve.wait_ge(dx_ready, q * per_q + (n + 1))
                        if n >= R:
                            dve.wait_ge(scanned, q * per_q + (n + 1 - R))
                        else:
                            dve.wait_ge(scanned, q * per_q)
                        dve.tensor_tensor(bx[r][:], pdx[n % 2][:, 0:GT], ssm.bt[:, bass.ds(q * GT, GT)],
                                          ALU.mult).then_inc(drive, 1)
                        dve.wait_ge(drive, q * per_q + (n + 1))
                        dve.wait_ge(decay, q * per_q + (n + 1))
                        if n >= R:
                            dve.wait_ge(weighed, q * per_q + (n + 1 - R))
                        else:
                            dve.wait_ge(weighed, q * per_q)
                        dve.tensor_tensor_scan(hs[r][:], abar[r][:].rearrange("p b t -> p (b t)"), bx[r][:], 0.0,
                                               ALU.mult, ALU.add).then_inc(scanned, 1)
                        if n == UN + 8:
                            add_y(q, 0)
                    add_y(q, 1)


def ring(eng, n, body):
    off = n % 2
    if off:
        body(0, 0, 0)
    with eng.Fori(0, n // 2) as i:
        for u in range(2):
            body(i * 2 + (off + u), (off + u) % 2, i + (off + u) // 2)


class Moe:

    def __init__(self, name, experts, picks, in_chunks, hid_chunks, gelu, mult, norm):
        self.name, self.E, self.K, self.NF, self.FH = name, experts, picks, in_chunks, hid_chunks
        self.gelu, self.mult, self.norm = gelu, mult, norm
        self.blocks = (picks * T + 127 * experts) // 128
        self.blocks += 1 - self.blocks % 2


def stage_moe_weights(nc, core, m, d):
    n1, n2 = KC * m.NF * 128, m.FH * D
    halves = 2 if n1 > 1024 else 1
    with Stage(nc, m.name + "w") as st:
        buf = [st.sb(f"buf{p}", [128, (n1 + n2) // halves]) for p in range(2)]
        landed = [st.sem(f"landed{p}") for p in range(2)]
        hi_done, lo_done = [st.sem(f"hi{p}") for p in range(2)], [st.sem(f"lo{p}") for p in range(2)]
        ready = st.sem("mult_ready")
        small = st.sem("small_landed")
        w1h, w1l = (w[:].rearrange("p e k n -> p e (k n)") for w in (m.w1_hi, m.w1_lo))
        w2h, w2l = (w[:].rearrange("p e k n -> p e (k n)") for w in (m.w2_hi, m.w2_lo))
        if m.mult:
            gain = st.sb("gain", [128, m.E, m.FH])

        def pieces(j, p, h_w1, h_w2):
            if halves == 2:
                e = j // 2 if isinstance(j, int) else None
                return [(h_w1 if p == 0 else h_w2, slice(0, n1), None)]
            return [(h_w1, slice(0, n1), None)] + [(h_w2, slice(n1 + f * D, n1 + (f + 1) * D), f)
                                                   for f in range(m.FH)]

        def each(j, p, before, w1, w2):
            if halves == 2:
                return [((w1 if p == 0 else w2)[:, bass.ds(before, 1), :], buf[p][:], None)]
            e = bass.ds(j, 1)
            out = [(w1[:, e, :], buf[p][:, 0:n1], None)]
            for f in range(m.FH):
                out.append((w2[:, e, f * D:(f + 1) * D], buf[p][:, n1 + f * D:n1 + (f + 1) * D],
                            gain[:, e, f:f + 1].rearrange("p a b -> p (a b)")))
            return out

        with nc.Block() as block:
            @block.sync
            def _(sp):
                if m.mult:
                    sp.dma_start(gain[:].rearrange("p e f -> p (e f)"), d[m.name + "mult"]).then_inc(small, 16)
                sp.dma_start(m.b1[:], d[m.name + "b1"]).then_inc(small, 16)

                def load(j, p, before):
                    sp.wait_ge(lo_done[p], before)
                    sp.dma_start(buf[p][:].rearrange("p (a n) -> p a n", a=1),
                                 d[m.name + "w"][:, bass.ds(j, 1), :]).then_inc(landed[p], 16)
                ring(sp, m.E * halves, load)

            @block.scalar
            def _(act):
                act.wait_ge(ready, 1)

                def high(j, p, before):
                    act.wait_ge(landed[p], before * 16 + 16)
                    parts = each(j, p, before, w1h, w2h)
                    for n, (dst, src, g) in enumerate(parts):
                        ins = act.activation(dst, src.rearrange("p (a n) -> p a n", a=1), ACT.Copy if g is None
                                             else ACT.Identity, scale=WS if g is None else g)
                    ins.then_inc(hi_done[p], 1)
                ring(act, m.E * halves, high)

            @block.vector
            def _(dve):
                dve.wait_ge(small, 32 if m.mult else 16)
                if m.mult:
                    dve.tensor_scalar(gain[:], gain[:], WS, None, ALU.mult).then_inc(ready, 1)
                    dve.tensor_scalar(m.b1[:, :, 0:m.NF // 2], m.b1[:, :, 0:m.NF // 2], WS, None,
                                      ALU.mult).then_inc(ready, 1)
                else:
                    dve.tensor_scalar(m.b1[:], m.b1[:], WS, None, ALU.mult).then_inc(ready, 2)
                dve.wait_ge(ready, 2)

                def low(j, p, before):
                    dve.wait_ge(hi_done[p], before + 1)
                    for (dst, src, g), (hi, _, _) in zip(each(j, p, before, w1l, w2l),
                                                         each(j, p, before, w1h, w2h)):
                        ins = dve.scalar_tensor_tensor(dst, src.rearrange("p (a n) -> p a n", a=1),
                                                       WS if g is None else g, hi, ALU.mult, ALU.subtract)
                    ins.then_inc(lo_done[p], 1)
                ring(dve, m.E * halves, low)


def stage_route(nc, core, m, d):
    E, K, N = m.E, m.K, m.blocks
    with Stage(nc, m.name + "r") as st:
        wr_hi, wr_lo = st.sb("wr_hi", [128, KC * E], F16), st.sb("wr_lo", [128, KC * E], F16)
        b2_hi, b2_lo = st.sb("b2_hi", [E, D], F16), st.sb("b2_lo", [E, D], F16)
        logit, prob = st.sb("logit", [L, NB, E]), st.sb("prob", [L, NB, E])
        top, rsum = st.sb("top", [L, NB]), st.sb("rsum", [L, NB])
        vals, idx, idxf = st.sb("vals", [L, NB, 8]), st.sb("idx", [L, NB, 8], U32), st.sb("idxf", [L, NB, 8])
        iota_e = st.sb("iota_e", [L, E])
        iota_n, iota_p, token = st.sb("iota_n", [L, N]), st.sb("iota_p", [L, 128]), st.sb("token", [L, NB])
        below = st.sb("below", [L, L], F16)
        hot = [st.sb(f"hot{k}", [L, NB, E]) for k in range(K)]
        comb, comb_hi, comb_lo = st.sb("comb", [L, NB, E]), st.sb("ch", [E, T], F16), st.sb("cl", [E, T], F16)
        part = st.sb("part", [L, NB, E])
        many = st.sb("many", [L, NB, E], F16)
        tot, run, keep = st.sb("tot", [L, E, NB]), st.sb("run", [L, E, NB]), st.sb("keep", [L, E, NB])
        cnt, cnt_i, nblk = st.sb("cnt", [L, E]), st.sb("cnt_i", [L, E], I32), st.sb("nblk", [L, E])
        bend, base, one_e = st.sb("bend", [L, E]), st.sb("base", [L, E]), st.sb("one_e", [L, E])
        rank = st.sb("rank", [L, NB, E])
        slotf = st.sb("slotf", [L, NB, K])
        lane_i, block_i = st.sb("lane_i", [L, NB, K], I32), st.sb("block_i", [L, NB, K], I32)
        lane, blockf = st.sb("lane", [L, NB, K]), st.sb("blockf", [L, NB, K])
        past = st.sb("past", [1, N, E])
        owner = st.sb("owner", [1, N])
        R = 4
        lane_hot = [st.sb(f"lane_hot{r}", [L, 128], F16) for r in range(R)]
        block_hot = [st.sb(f"block_hot{r}", [L, N], F16) for r in range(R)]
        plog, ppos, ptot = (st.ps(n, [L, NB, E]) for n in ("plog", "ppos", "ptot"))
        pids = st.ps("pids", [128, N])
        pcomb = st.ps("pcomb", [E, 512])
        pbias = [st.ps(f"pbias{u}", [L, D]) for u in range(2)]
        (log_ready, log_out, shifted, exped, masks, hot_ready, counts, hots, used, ids_ready, comb_done, turned,
         comb_high, comb_split, consts) = (st.sem(n) for n in (
             "log_ready", "log_out", "shifted", "exped", "masks", "hot_ready", "counts", "hots", "used", "ids_ready",
             "comb_done", "turned", "comb_high", "comb_split", "consts"))
        bias_ready, bias_free = ([st.sem(f"{n}{u}") for u in range(2)] for n in ("bias_ready", "bias_free"))
        chain_sem = st.sem("chain")
        w_sync, w_act, w_dve, (w_ready, w_n) = split_weights(st, core, [
            ("wr", d[m.name + "router"], wr_hi[:], wr_lo[:]),
            ("b2", d[m.name + "b2"], b2_hi[:], b2_lo[:]),
        ])
        with nc.Block() as block:
            @block.sync
            def _(sp):
                w_sync(sp)

            @block.gpsimd
            def _(pool):
                made = Chain(pool, masks)
                made.step(pool.memset(below[:], 1.0))
                made.step(pool.affine_select(out=below[:], in_=below[:], compare_op=ALU.is_ge, fill=0.0, base=-1,
                                             pattern=[[1, L]], channel_multiplier=-1))
                imprecise = dict(allow_small_or_imprecise_dtypes=True)
                made.step(pool.iota(iota_e[:], pattern=[[1, E]], base=0, channel_multiplier=0, **imprecise))
                made.step(pool.iota(iota_n[:], pattern=[[1, N]], base=0, channel_multiplier=0, **imprecise))
                made.step(pool.iota(iota_p[:], pattern=[[1, 128]], base=0, channel_multiplier=0, **imprecise))
                made.step(pool.iota(token[:], pattern=[[L, NB]], base=0, channel_multiplier=1, **imprecise))
                made.step(pool.memset(keep[:], 1.0))
                made.step(pool.memset(keep[:, :, 0:1], 0.0))
                made.step(pool.memset(one_e[:], 1.0))

            @block.tensor
            def _(pe):
                pe.wait_ge(w_ready, w_n)
                with pe.Fori(0, NB) as b:
                    cols = bass.ds(b * L, L)
                    for k in range(KC):
                        last = mm3(pe, plog[:, bass.ds(b, 1), :], core.xt_hi[:, k, cols], core.xt_lo[:, k, cols],
                                   wr_hi[:, k * E:(k + 1) * E].rearrange("p (a n) -> p a n", a=1),
                                   wr_lo[:, k * E:(k + 1) * E].rearrange("p (a n) -> p a n", a=1), k == 0,
                                   k == KC - 1)
                    last.then_inc(log_ready, 1)
                pe.wait_ge(hot_ready, 1)
                flat = many[:].rearrange("p b e -> p (b e)")
                pe.matmul(ppos[:].rearrange("p b e -> p (b e)"), below[:], flat, start=True, stop=True)
                pe.matmul(ptot[:].rearrange("p b e -> p (b e)"), core.ones16[0:L, 0:L], flat, start=True,
                          stop=True).then_inc(counts, 1)
                for n in range(NB * K):
                    pe.wait_ge(hots, n + 1)
                    pe.matmul(pids[:], lane_hot[n % R][:], block_hot[n % R][:], start=n == 0,
                              stop=n == NB * K - 1).then_inc(used, 1)
                pe.wait_ge(comb_done, 1)
                for q in range(NG):
                    if q:
                        pe.wait_ge(comb_split, q)
                    for j in range(GB):
                        last = pe.transpose(pcomb[:, j * L:(j + 1) * L], comb[:, q * GB + j, :],
                                            core.ident[0:L, 0:L])
                    last.then_inc(turned, 1)
                pe.wait_ge(comb_split, NG)

                def bias(j, p, before):
                    pe.wait_ge(bias_free[p], before)
                    cols = bass.ds(j * L, L)
                    mm3(pe, pbias[p][:], comb_hi[:, cols], comb_lo[:, cols], b2_hi[:], b2_lo[:], True,
                        True).then_inc(bias_ready[p], 1)
                ring(pe, NB, bias)

            @block.scalar
            def _(act):
                w_act(act)
                act.wait_ge(log_ready, NB)
                act.activation(logit[:], plog[:], ACT.Copy, scale=1.0 / WS).then_inc(log_out, 1)
                act.wait_ge(shifted, 1)
                act.activation(prob[:], part[:], ACT.Exp).then_inc(exped, 1)
                for q in range(NG):
                    act.wait_ge(turned, q + 1)
                    act.activation(comb_hi[:, q * GT:(q + 1) * GT], pcomb[:, 0:GT], ACT.Copy).then_inc(comb_high, 1)

            @block.vector
            def _(dve):
                w_dve(dve)
                dve.wait_ge(masks, 9)
                ch = Chain(dve, chain_sem)
                over_e = lambda a: a.unsqueeze(2).to_broadcast([L, NB, E])
                dve.wait_ge(log_out, 1)
                ch.step(dve.tensor_reduce(out=top[:], in_=logit[:], op=ALU.max, axis=AX.X))
                dve.tensor_tensor(part[:], logit[:], over_e(top[:]), ALU.subtract).then_inc(shifted, 1)
                dve.wait_ge(exped, 1)
                ch.step(dve.tensor_reduce(out=rsum[:], in_=prob[:], op=ALU.add, axis=AX.X))
                ch.step(dve.reciprocal(rsum[:], rsum[:]))
                ch.step(dve.tensor_tensor(prob[:], prob[:], over_e(rsum[:]), ALU.mult))
                for b in range(NB):
                    ins = dve.max(vals[:, b, :], prob[:, b, :])
                ch.step(ins)
                for b in range(NB):
                    ins = dve.max_index(idx[:, b, :], vals[:, b, :], prob[:, b, :])
                ch.step(ins)
                ch.step(dve.tensor_copy(idxf[:], idx[:]))
                for k in range(K):
                    ins = dve.tensor_tensor(hot[k][:], iota_e[:].unsqueeze(1).to_broadcast([L, NB, E]),
                                            over_e(idxf[:, :, k]), ALU.is_equal)
                ch.step(ins)
                if K == 1:
                    dve.tensor_copy(many[:], hot[0][:]).then_inc(hot_ready, 1)
                else:
                    ch.step(dve.tensor_tensor(part[:], hot[0][:], hot[1][:], ALU.add))
                    dve.tensor_tensor(many[:], part[:], hot[2][:], ALU.add).then_inc(hot_ready, 1)
                if m.norm:
                    ch.step(dve.tensor_tensor(rsum[:], vals[:, :, 0], vals[:, :, 1], ALU.add))
                    ch.step(dve.tensor_tensor(rsum[:], rsum[:], vals[:, :, 2], ALU.add))
                    ch.step(dve.tensor_scalar(rsum[:], rsum[:], 1e-20, None, ALU.add))
                    ch.step(dve.reciprocal(rsum[:], rsum[:]))
                    ch.step(dve.tensor_tensor(m.weight[:], vals[:, :, 0:K],
                                              rsum[:].unsqueeze(2).to_broadcast([L, NB, K]), ALU.mult))
                else:
                    ch.step(dve.tensor_copy(m.weight[:], vals[:, :, 0:K]))
                ch.step(dve.tensor_tensor(comb[:], hot[0][:], over_e(m.weight[:, :, 0]), ALU.mult))
                for k in range(1, K):
                    ch.step(dve.tensor_tensor(rank[:], hot[k][:], over_e(m.weight[:, :, k]), ALU.mult))
                    ch.step(dve.tensor_tensor(comb[:], comb[:], rank[:], ALU.add))
                dve.sem_inc(comb_done, 1)
                dve.wait_ge(counts, 1)
                ch.step(dve.tensor_copy(tot[:], ptot[:].rearrange("p b e -> p e b")))
                ch.step(dve.tensor_tensor_scan(run[:].rearrange("p e b -> p (e b)"),
                                               keep[:].rearrange("p e b -> p (e b)"),
                                               tot[:].rearrange("p e b -> p (e b)"), 0.0, ALU.mult, ALU.add))
                ch.step(dve.tensor_scalar(cnt_i[:], run[:, :, NB - 1], 127.0, None, ALU.add))
                ch.step(dve.tensor_scalar(cnt_i[:], cnt_i[:], 7, None, ALU.logical_shift_right))
                ch.step(dve.tensor_copy(nblk[:], cnt_i[:]))
                ch.step(dve.tensor_tensor_scan(bend[:], one_e[:], nblk[:], 0.0, ALU.mult, ALU.add))
                ch.step(dve.tensor_tensor(base[:], bend[:], nblk[:], ALU.subtract))
                ch.step(dve.tensor_tensor(run[:], run[:], tot[:], ALU.subtract))
                ch.step(dve.scalar_tensor_tensor(run[:], base[:].unsqueeze(2).to_broadcast([L, E, NB]), 128.0, run[:],
                                                 ALU.mult, ALU.add))
                ch.step(dve.tensor_tensor(rank[:], ppos[:], run[:].rearrange("p e b -> p b e"), ALU.add))
                for k in range(K):
                    ch.step(dve.tensor_tensor(part[:], hot[k][:], rank[:], ALU.mult))
                    ch.step(dve.tensor_reduce(out=slotf[:, :, k], in_=part[:], op=ALU.add, axis=AX.X))
                dve.tensor_copy(m.slot[:], slotf[:])
                ch.step(dve.tensor_copy(block_i[:], slotf[:]))
                dve.tensor_scalar(lane_i[:], block_i[:], 127, None, ALU.bitwise_and)
                ch.step(dve.tensor_scalar(block_i[:], block_i[:], 7, None, ALU.logical_shift_right))
                dve.tensor_copy(lane[:], lane_i[:])
                ch.step(dve.tensor_copy(blockf[:], block_i[:]))
                for b in range(NB):
                    for k in range(K):
                        n = b * K + k
                        if n >= R:
                            dve.wait_ge(used, n - R + 1)
                        dve.tensor_scalar(lane_hot[n % R][:], iota_p[:], lane[:, b, k:k + 1], None, ALU.is_equal)
                        dve.tensor_scalar(block_hot[n % R][:], iota_n[:], blockf[:, b, k:k + 1], token[:, b:b + 1],
                                          ALU.is_equal, ALU.mult).then_inc(hots, 1)
                ch.step(dve.tensor_tensor(past[:], bend[0:1, :].unsqueeze(1).to_broadcast([1, N, E]),
                                          iota_n[0:1, :].unsqueeze(2).to_broadcast([1, N, E]), ALU.is_le))
                ch.step(dve.tensor_reduce(out=owner[:], in_=past[:], op=ALU.add, axis=AX.X))
                ch.step(dve.tensor_scalar(m.expert[:], owner[:], E - 1.0, None, ALU.min))
                dve.wait_ge(used, NB * K)
                ch.step(dve.tensor_copy(m.ids[:], pids[:]))
                for q in range(NG):
                    dve.wait_ge(comb_high, q + 1)
                    dve.tensor_tensor(comb_lo[:, q * GT:(q + 1) * GT], pcomb[:, 0:GT],
                                      comb_hi[:, q * GT:(q + 1) * GT], ALU.subtract).then_inc(comb_split, 1)

                def add(j, p, before):
                    dve.wait_ge(bias_ready[p], before + 1)
                    b = bass.ds(j, 1)
                    dve.scalar_tensor_tensor(core.h[:, b, :], pbias[p][:].unsqueeze(1), 1.0 / WS, core.h[:, b, :],
                                             ALU.mult, ALU.add).then_inc(bias_free[p], 1)
                ring(dve, NB, add)


def stage_experts(nc, core, m):
    N, NF, FH = m.blocks, m.NF, m.FH
    HB = NF * 128 // 512
    with Stage(nc, m.name + "x") as st:
        two = range(2)
        idx = [st.sb(f"idx{p}", [128, 1], U32) for p in two]
        xg = [st.sb(f"xg{p}", [128, 2 * D], F16) for p in two]
        xb = [st.sb(f"xb{p}", [128, 2 * KC, 128], F16) for p in two]
        b1 = [st.sb(f"b1{p}", [128, 1, NF]) for p in two]
        gate = [st.sb(f"gate{p}", [128, FH, 128]) for p in two] if m.gelu else None
        act32 = [st.sb(f"a{p}", [128, FH, 128]) for p in two]
        a_hi, a_lo = ([st.sb(f"{n}{p}", [128, FH, 128], F16) for p in two] for n in ("ah", "al"))
        yo = [st.sb(f"yo{p}", [128, D]) for p in two]
        pt = [st.ps(f"pt{p}", [128, 2 * KC, 128], F16) for p in two]
        ph = [st.ps(f"ph{p}", [128, NF, 128]) for p in two]
        py = [st.ps(f"py{p}", [128, 512]) for p in ([0] if m.FH > 2 else two)]
        PY = len(py)
        sems = lambda n: [st.sem(f"{n}{p}") for p in two]
        idx_ready, gathered, turned, xb_ready, h_ready = (sems(n) for n in (
            "idx_ready", "gathered", "turned", "xb_ready", "h_ready"))
        b1_ready, gate_ready, a_ready, hi_ready, lo_ready = (sems(n) for n in (
            "b1_ready", "gate_ready", "a_ready", "hi_ready", "lo_ready"))
        y_ready, y_out, stored = (sems(n) for n in ("y_ready", "y_out", "stored"))
        with nc.Block() as block:
            @block.gpsimd
            def _(pool):
                def step(j, p, before):
                    wait_alone(pool, core, turned[p], before)
                    pool.tensor_copy(idx[p][:], m.ids[:, bass.ds(j, 1)]).then_inc(idx_ready[p], 1)
                    e = pool.value_load(m.expert[0:1, bass.ds(j, 1)], min_val=0, max_val=m.E - 1)
                    wait_alone(pool, core, lo_ready[p], before)
                    pool.tensor_copy(b1[p][:], m.b1[:, bass.ds(e, 1), :]).then_inc(b1_ready[p], 1)
                    wait_alone(pool, core, idx_ready[p], before + 1)
                    pool.indirect_dma_start(xg[p][:], None, m.rows[:, :],
                                            bass.IndirectOffsetOnAxis(ap=idx[p][:, 0:1], axis=0)
                                            ).then_inc(gathered[p], 16)
                ring(pool, N, step)

            @block.tensor
            def _(pe):
                def first(j, p, before):
                    e = pe.value_load(m.expert[0:1, bass.ds(j, 1)], min_val=0, max_val=m.E - 1)
                    pe.wait_ge(gathered[p], before * 16 + 16)
                    pe.wait_ge(xb_ready[p], before)
                    for c in range(2 * KC):
                        last = pe.transpose(pt[p][:, c, :], xg[p][:, c * 128:(c + 1) * 128], core.ident16[:])
                    last.then_inc(turned[p], 1)
                    pe.wait_ge(xb_ready[p], before + 1)
                    pe.wait_ge(lo_ready[p], before)
                    for f in range(NF):
                        for k in range(KC):
                            w = [w[:, bass.ds(e, 1), k, f * 128:(f + 1) * 128].rearrange("p a n -> p (a n)")
                                 for w in (m.w1_hi, m.w1_lo)]
                            last = mm3(pe, ph[p][:, f, :], w[0], w[1], xb[p][:, k, :], xb[p][:, KC + k, :],
                                       k == 0, k == KC - 1)
                    last.then_inc(h_ready[p], 1)
                    return e

                def second(e, p, before):
                    pe.wait_ge(hi_ready[p], before + 1)
                    pe.wait_ge(lo_ready[p], before + 1)
                    for f in range(FH):
                        w = [w[:, bass.ds(e, 1), f, :].rearrange("p a n -> p (a n)") for w in (m.w2_hi, m.w2_lo)]
                        last = mm3(pe, py[p % PY][:, 0:D], a_hi[p][:, f, :], a_lo[p][:, f, :], w[0], w[1],
                                   f == 0, f == FH - 1)
                    last.then_inc(y_ready[p], 1)

                first(0, 0, 0)
                with pe.Fori(0, (N - 1) // 2) as i:
                    for u in range(2):
                        e = pe.value_load(m.expert[0:1, bass.ds(i * 2 + u, 1)], min_val=0, max_val=m.E - 1)
                        first(i * 2 + (1 + u), (1 + u) % 2, i + u)
                        if PY == 2:
                            pe.wait_ge(y_out[u], i)
                        else:
                            pe.wait_ge(y_out[1 - u], i + u)
                        second(e, u, i)
                e = pe.value_load(m.expert[0:1, N - 1:N], min_val=0, max_val=m.E - 1)
                pe.wait_ge(y_out[0], (N - 1) // 2)
                pe.wait_ge(y_out[1], (N - 1) // 2)
                second(e, 0, (N - 1) // 2)

            @block.scalar
            def _(act):
                def step(j, p, before):
                    act.wait_ge(turned[p], before + 1)
                    act.wait_ge(h_ready[p], before)
                    act.activation(xb[p][:], pt[p][:], ACT.Copy).then_inc(xb_ready[p], 1)
                    act.wait_ge(h_ready[p], before + 1)
                    act.wait_ge(b1_ready[p], before + 1)
                    if m.gelu:
                        act.wait_ge(a_ready[p], before)
                        for f in range(FH):
                            ins = act.activation(gate[p][:, f, :], ph[p][:, FH + f, :], ACT.Gelu,
                                                 bias=b1[p][:, 0, FH + f:FH + f + 1], scale=1.0 / WS)
                        ins.then_inc(gate_ready[p], 1)
                        act.wait_ge(a_ready[p], before + 1)
                        act.wait_ge(y_ready[p], before)
                        act.activation(a_hi[p][:], act32[p][:], ACT.Copy).then_inc(hi_ready[p], 1)
                    else:
                        act.wait_ge(y_ready[p], before)
                        for f in range(FH):
                            ins = act.activation(a_hi[p][:, f, :], ph[p][:, f, :], ACT.Relu,
                                                 bias=b1[p][:, 0, f:f + 1])
                        ins.then_inc(hi_ready[p], 1)

                ring(act, N, step)

            @block.vector
            def _(dve):
                def step(j, p, before):
                    if m.gelu:
                        dve.wait_ge(gate_ready[p], before + 1)
                        dve.wait_ge(hi_ready[p], before)
                        for f in range(FH):
                            ins = dve.scalar_tensor_tensor(act32[p][:, f, :], ph[p][:, f, :], b1[p][:, 0, f:f + 1],
                                                           gate[p][:, f, :], ALU.add, ALU.mult)
                        ins.then_inc(a_ready[p], 1)
                    else:
                        dve.wait_ge(hi_ready[p], before + 1)
                        for f in range(FH):
                            ins = dve.tensor_scalar(act32[p][:, f, :], ph[p][:, f, :], b1[p][:, 0, f:f + 1], 0.0,
                                                    ALU.add, ALU.max)
                        ins.then_inc(a_ready[p], 1)
                        dve.wait_ge(a_ready[p], before + 1)
                    dve.wait_ge(hi_ready[p], before + 1)
                    dve.wait_ge(y_ready[p], before)
                    dve.tensor_tensor(a_lo[p][:], act32[p][:], a_hi[p][:], ALU.subtract).then_inc(lo_ready[p], 1)
                    dve.wait_ge(y_ready[p], before + 1)
                    dve.wait_ge(stored[p], before * 16)
                    dve.tensor_scalar(yo[p][:], py[p % PY][:, 0:D], 1.0 / (WS * WS), None,
                                      ALU.mult).then_inc(y_out[p], 1)
                ring(dve, N, step)

            @block.sync
            def _(sp):
                def step(j, p, before):
                    sp.wait_ge(y_out[p], before + 1)
                    sp.dma_start(m.out[bass.ds(j * 128, 128), :], yo[p][:]).then_inc(stored[p], 16)
                ring(sp, N, step)
                sp.wait_ge(stored[0], 16 * ((N + 1) // 2))
                sp.wait_ge(stored[1], 16 * (N // 2))


def stage_combine(nc, core, m):
    K = m.K
    with Stage(nc, m.name + "c") as st:
        two = range(2)
        idx = [st.sb(f"idx{p}", [L, K], U32) for p in two]
        got = [[st.sb(f"got{p}{k}", [L, 1, D]) for k in range(K)] for p in two]
        gathered = [st.sem(f"gathered{p}") for p in two]
        added = [st.sem(f"added{p}") for p in two]
        idx_ready = [st.sem(f"idx_ready{p}") for p in two]
        chain_sem = st.sem("chain")
        with nc.Block() as block:
            @block.gpsimd
            def _(pool):
                def step(j, p, before):
                    wait_alone(pool, core, added[p], before)
                    pool.tensor_copy(idx[p][:].unsqueeze(1), m.slot[:, bass.ds(j, 1), :]).then_inc(idx_ready[p], 1)
                    wait_alone(pool, core, idx_ready[p], before + 1)
                    for k in range(K):
                        pool.indirect_dma_start(got[p][k][:].rearrange("p a n -> p (a n)"), None, m.out[:, :],
                                                bass.IndirectOffsetOnAxis(ap=idx[p][:, k:k + 1], axis=0)
                                                ).then_inc(gathered[p], 16)
                ring(pool, NB, step)

            @block.vector
            def _(dve):
                def step(j, p, before):
                    dve.wait_ge(gathered[p], before * (16 * K) + 16 * K)
                    b = bass.ds(j, 1)
                    for k in range(K):
                        ins = dve.scalar_tensor_tensor(core.h[:, b, :], got[p][k][:], m.weight[:, b, k:k + 1]
                                                       .rearrange("p a b -> p (a b)"), core.h[:, b, :],
                                                       ALU.mult, ALU.add)
                        if k < K - 1:
                            ins.then_inc(chain_sem, 1)
                            dve.wait_ge(chain_sem, j * (K - 1) + (k + 1))
                    ins.then_inc(added[p], 1)
                ring(dve, NB, step)



def stage_shared(nc, core, d):
    FC = 4
    with Stage(nc, "shared") as st:
        s1_hi, s1_lo = (st.sb(n, [128, KC, 2 * FC * 128], F16) for n in ("s1_hi", "s1_lo"))
        s2_hi, s2_lo = (st.sb(n, [128, FC, D], F16) for n in ("s2_hi", "s2_lo"))
        s2_f, gain, b1 = st.sb("s2_f", [128, FC, D]), st.sb("gain", [128, FC]), st.sb("b1", [128, 2 * FC])
        b2_hi, b2_lo = st.sb("b2_hi", [1, D], F16), st.sb("b2_lo", [1, D], F16)
        b2_scaled = st.sb("b2_scaled", [1, D])
        two = range(2)
        gate, a32 = ([st.sb(f"{n}{p}", [128, GT]) for p in two] for n in ("gate", "a32"))
        a_hi, a_lo = (st.sb(n, [128, FC, GT], F16) for n in ("a_hi", "a_lo"))
        px, pg = ([st.ps(f"{n}{p}", [128, 512]) for p in two] for n in ("px", "pg"))
        po = [st.ps(f"po{p}", [L, D]) for p in two]
        small, scaled, gained = st.sem("small"), st.sem("scaled"), st.sem("gained")
        x_ready, g_ready, gated, a_ready, hi_ready, lo_ready = (st.sem(n) for n in (
            "x_ready", "g_ready", "gated", "a_ready", "hi_ready", "lo_ready"))
        o_ready, o_free = ([st.sem(f"{n}{p}") for p in two] for n in ("o_ready", "o_free"))
        flat = lambda t: t[:].rearrange("p a n -> p (a n)")
        w_sync, w_act, w_dve, (w_ready, w_n) = split_weights(st, core, [
            ("s1", d["s1"], flat(s1_hi), flat(s1_lo)),
        ])
        with nc.Block() as block:
            @block.sync
            def _(sp):
                w_sync(sp)
                for dst, src in ((flat(s2_f), d["s2"]), (gain[:], d["s_mult"]), (b1[:], d["s_b1"]),
                                 (b2_scaled[:], d["s_b2"])):
                    sp.dma_start(dst, src).then_inc(small, 16)

            @block.tensor
            def _(pe):
                pe.wait_ge(w_ready, w_n)
                pe.wait_ge(gained, 2)
                with pe.Fori(0, NG) as q:
                    cols = bass.ds(q * GT, GT)
                    for f in range(FC):
                        p = f % 2
                        pe.wait_ge(a_ready, q * FC + max(f - 1, 0))
                        for out, ff, sem in ((pg[p], FC + f, g_ready), (px[p], f, x_ready)):
                            for k in range(KC):
                                last = mm3(pe, out[:, 0:GT], s1_hi[:, k, ff * 128:(ff + 1) * 128],
                                           s1_lo[:, k, ff * 128:(ff + 1) * 128], core.xt_hi[:, k, cols],
                                           core.xt_lo[:, k, cols], k == 0, k == KC - 1)
                            last.then_inc(sem, 1)
                    for j in range(GB):
                        p = j % 2
                        pe.wait_ge(lo_ready, q * FC + FC)
                        pe.wait_ge(o_free[p], q * 2 + j // 2)
                        tok = slice(j * L, (j + 1) * L)
                        for f in range(FC):
                            mm3(pe, po[p][:], a_hi[:, f, tok], a_lo[:, f, tok], s2_hi[:, f, :], s2_lo[:, f, :],
                                f == 0, False)
                        pe.matmul(po[p][:], core.ones16[0:1, 0:L], b2_hi[:], start=False, stop=False)
                        pe.matmul(po[p][:], core.ones16[0:1, 0:L], b2_lo[:], start=False,
                                  stop=True).then_inc(o_ready[p], 1)

            @block.scalar
            def _(act):
                w_act(act)
                act.wait_ge(scaled, 3)
                for f in range(FC):
                    act.activation(s2_hi[:, f, :], s2_f[:, f, :], ACT.Identity, scale=gain[:, f:f + 1])
                act.activation(b2_hi[:], b2_scaled[:], ACT.Copy).then_inc(gained, 1)
                with act.Fori(0, NG) as q:
                    for f in range(FC):
                        p = f % 2
                        act.wait_ge(g_ready, q * FC + (f + 1))
                        act.wait_ge(a_ready, q * FC + max(f - 1, 0))
                        act.activation(gate[p][:], pg[p][:, 0:GT], ACT.Gelu, bias=b1[:, FC + f:FC + f + 1],
                                       scale=1.0 / WS).then_inc(gated, 1)
                        act.wait_ge(a_ready, q * FC + (f + 1))
                        if f == 0:
                            act.wait_ge(o_ready[0], q * 2)
                            act.wait_ge(o_ready[1], q * 2)
                        act.activation(a_hi[:, f, :], a32[p][:], ACT.Copy).then_inc(hi_ready, 1)

            @block.vector
            def _(dve):
                w_dve(dve)
                dve.wait_ge(small, 64)
                dve.tensor_scalar(gain[:], gain[:], WS, None, ALU.mult).then_inc(scaled, 1)
                dve.tensor_scalar(b2_scaled[:], b2_scaled[:], WS * WS, None, ALU.mult).then_inc(scaled, 1)
                dve.tensor_scalar(b1[:, 0:FC], b1[:, 0:FC], WS, None, ALU.mult).then_inc(scaled, 1)
                dve.wait_ge(gained, 1)
                for f in range(FC):
                    dve.scalar_tensor_tensor(s2_lo[:, f, :], s2_f[:, f, :], gain[:, f:f + 1], s2_hi[:, f, :],
                                             ALU.mult, ALU.subtract)
                dve.tensor_tensor(b2_lo[:], b2_scaled[:], b2_hi[:], ALU.subtract).then_inc(gained, 1)
                with dve.Fori(0, NG) as q:
                    for f in range(FC):
                        p = f % 2
                        dve.wait_ge(x_ready, q * FC + (f + 1))
                        dve.wait_ge(gated, q * FC + (f + 1))
                        dve.wait_ge(lo_ready, q * FC + max(f - 1, 0))
                        dve.scalar_tensor_tensor(a32[p][:], px[p][:, 0:GT], b1[:, f:f + 1], gate[p][:],
                                                 ALU.add, ALU.mult).then_inc(a_ready, 1)
                        dve.wait_ge(hi_ready, q * FC + (f + 1))
                        dve.tensor_tensor(a_lo[:, f, :], a32[p][:], a_hi[:, f, :], ALU.subtract).then_inc(lo_ready, 1)
                    for j in range(GB):
                        p = j % 2
                        dve.wait_ge(o_ready[p], q * 2 + (j // 2 + 1))
                        b = bass.ds(q * GB + j, 1)
                        dve.scalar_tensor_tensor(core.h[:, b, :], po[p][:].unsqueeze(1), 1.0 / (WS * WS),
                                                 core.h[:, b, :], ALU.mult, ALU.add).then_inc(o_free[p], 1)


def stage_gru(nc, core, d):
    EC = 3
    LS = L + 1
    with Stage(nc, "gru") as st:
        wf_hi, wf_lo = (st.sb(n, [128, KC, 2 * EC * 128], F16) for n in ("wf_hi", "wf_lo"))
        wd_hi, wd_lo = (st.sb(n, [128, EC, D], F16) for n in ("wd_hi", "wd_lo"))
        bf, nbf = st.sb("bf", [128, 2 * EC]), st.sb("nbf", [128, 2 * EC])
        two = range(2)
        keep, drive, hs = ([st.sb(f"{n}{p}", [128, GB, LS]) for p in two] for n in ("keep", "drive", "hs"))
        zg, sx, rx = ([st.sb(f"{n}{p}", [128, GT]) for p in two] for n in ("zg", "sx", "rx"))
        h_hi, h_lo = (st.sb(n, [128, EC, GB, LS], F16) for n in ("h_hi", "h_lo"))
        pk, px = ([st.ps(f"{n}{p}", [128, 512]) for p in two] for n in ("pk", "px"))
        po = [st.ps(f"po{p}", [L, D]) for p in two]
        small, negated, edges = st.sem("small"), st.sem("negated"), st.sem("edges")
        k_ready, x_ready, sig_ready, rx_ready, sum_ready, drive_ready, scanned, hi_ready, lo_ready = (
            st.sem(n) for n in ("k_ready", "x_ready", "sig_ready", "rx_ready", "sum_ready", "drive_ready", "scanned",
                                "hi_ready", "lo_ready"))
        o_ready, o_free = ([st.sem(f"{n}{p}") for p in two] for n in ("o_ready", "o_free"))
        flat = lambda t: t[:].rearrange("p a n -> p (a n)")
        w_sync, w_act, w_dve, (w_ready, w_n) = split_weights(st, core, [
            ("wf", d["w_f"], flat(wf_hi), flat(wf_lo)), ("wd", d["w_down"], flat(wd_hi), flat(wd_lo)),
        ])
        N = NG * EC
        unit = lambda n: divmod(n, EC)
        groups = lambda t: t.rearrange("p (b t) -> p b t", t=L)
        with nc.Block() as block:
            @block.sync
            def _(sp):
                w_sync(sp)
                sp.dma_start(bf[:], d["b_f"]).then_inc(small, 16)

            @block.gpsimd
            def _(pool):
                for p in two:
                    pool.memset(keep[p][:, :, 0:1], 0.0).then_inc(edges, 1)
                    pool.memset(drive[p][:, :, 0:1], 0.5).then_inc(edges, 1)

            @block.tensor
            def _(pe):
                pe.wait_ge(w_ready, w_n)
                for n in range(N):
                    q, e = unit(n)
                    p = n % 2
                    cols = slice(q * GT, (q + 1) * GT)
                    if n >= 2:
                        pe.wait_ge(sig_ready, n - 1)
                        pe.wait_ge(rx_ready, n - 1)
                    for out, ee, sem in ((pk[p], e, k_ready), (px[p], EC + e, x_ready)):
                        for k in range(KC):
                            last = mm3(pe, out[:, 0:GT], wf_hi[:, k, ee * 128:(ee + 1) * 128],
                                       wf_lo[:, k, ee * 128:(ee + 1) * 128], core.xt_hi[:, k, cols],
                                       core.xt_lo[:, k, cols], k == 0, k == KC - 1)
                        last.then_inc(sem, 1)
                    if e == EC - 1:
                        pe.wait_ge(lo_ready, n + 1)
                        for j in range(GB):
                            p2 = j % 2
                            pe.wait_ge(o_free[p2], q * 2 + j // 2)
                            for k in range(EC):
                                last = mm3(pe, po[p2][:], h_hi[:, k, j, 1:LS], h_lo[:, k, j, 1:LS], wd_hi[:, k, :],
                                           wd_lo[:, k, :], k == 0, k == EC - 1)
                            last.then_inc(o_ready[p2], 1)

            @block.scalar
            def _(act):
                w_act(act)
                act.wait_ge(small, 16)
                act.activation(nbf[:], bf[:], ACT.Copy, scale=-1.0).then_inc(negated, 1)
                act.wait_ge(negated, 1)
                act.wait_ge(edges, 4)
                for n in range(N):
                    q, e = unit(n)
                    p = n % 2
                    act.wait_ge(k_ready, n + 1)
                    if n >= 2:
                        act.wait_ge(scanned, n - 1)
                    act.activation(keep[p][:, :, 1:LS], groups(pk[p][:, 0:GT]), ACT.Sigmoid, bias=nbf[:, e:e + 1],
                                   scale=-1.0 / WS)
                    act.activation(zg[p][:], pk[p][:, 0:GT], ACT.Sigmoid, bias=bf[:, e:e + 1], scale=1.0 / WS)
                    act.wait_ge(x_ready, n + 1)
                    act.activation(sx[p][:], px[p][:, 0:GT], ACT.Sigmoid, bias=bf[:, EC + e:EC + e + 1],
                                   scale=1.0 / WS).then_inc(sig_ready, 1)
                    act.wait_ge(scanned, n + 1)
                    if e == 0 and q:
                        act.wait_ge(o_ready[0], q * 2)
                        act.wait_ge(o_ready[1], q * 2)
                    act.activation(h_hi[:, e, :, :], hs[p][:], ACT.Copy).then_inc(hi_ready, 1)

            @block.vector
            def _(dve):
                w_dve(dve)
                dve.wait_ge(edges, 4)
                dve.wait_ge(small, 16)
                for n in range(N):
                    q, e = unit(n)
                    p = n % 2
                    dve.wait_ge(sig_ready, n + 1)
                    dve.tensor_scalar(rx[p][:], px[p][:, 0:GT], 1.0 / WS, bf[:, EC + e:EC + e + 1],
                                      ALU.mult, ALU.add).then_inc(rx_ready, 1)
                    dve.wait_ge(rx_ready, n + 1)
                    dve.tensor_scalar(rx[p][:], rx[p][:], 0.0, None, ALU.max).then_inc(sum_ready, 1)
                    dve.wait_ge(sum_ready, 2 * n + 1)
                    dve.scalar_tensor_tensor(rx[p][:], sx[p][:], 0.5, rx[p][:], ALU.min, ALU.add).then_inc(sum_ready, 1)
                    dve.wait_ge(sum_ready, 2 * n + 2)
                    dve.tensor_tensor(drive[p][:, :, 1:LS], groups(rx[p][:]), groups(zg[p][:]),
                                      ALU.mult).then_inc(drive_ready, 1)
                    dve.wait_ge(drive_ready, n + 1)
                    if n >= 2:
                        dve.wait_ge(hi_ready, n - 1)
                    dve.tensor_tensor_scan(hs[p][:].rearrange("p b t -> p (b t)"),
                                           keep[p][:].rearrange("p b t -> p (b t)"),
                                           drive[p][:].rearrange("p b t -> p (b t)"), 0.0,
                                           ALU.mult, ALU.add).then_inc(scanned, 1)
                    dve.wait_ge(hi_ready, n + 1)
                    dve.tensor_tensor(h_lo[:, e, :, :], hs[p][:], h_hi[:, e, :, :], ALU.subtract).then_inc(lo_ready, 1)
                    if e == EC - 1:
                        for j in range(GB):
                            p2 = j % 2
                            dve.wait_ge(o_ready[p2], q * 2 + (j // 2 + 1))
                            dve.scalar_tensor_tensor(core.h[:, q * GB + j, :], po[p2][:], 1.0 / WS,
                                                     core.h[:, q * GB + j, :], ALU.mult, ALU.add).then_inc(o_free[p2], 1)


def stage_ternary(nc, core, name, mats, floor):
    M = len(mats)
    with Stage(nc, name) as st:
        buf = [st.sb(f"buf{i}", list(m[0].shape)) for i, m in enumerate(mats)]
        neg = [st.sb(f"neg{i}", list(m[0].shape), F16) for i, m in enumerate(mats)]
        asum, thr, nthr = st.sb("asum", [128, M]), st.sb("thr", [128, M]), st.sb("nthr", [128, M])
        tot = st.ps("tot", [128, M])
        landed = [st.sem(f"landed{i}") for i in range(M)]
        summed, totals, chain_sem = st.sem("summed"), st.sem("totals"), st.sem("chain")
        with nc.Block() as block:
            @block.sync
            def _(sp):
                for b, m, s in zip(buf, mats, landed):
                    sp.dma_start(b[:], m[0]).then_inc(s, 16)

            @block.tensor
            def _(pe):
                pe.wait_ge(summed, M)
                pe.matmul(tot[:], core.ones[:], asum[:], start=True, stop=True).then_inc(totals, 1)

            @block.vector
            def _(dve):
                for i, s in enumerate(landed):
                    dve.wait_ge(s, 16)
                    dve.tensor_reduce(out=asum[:, i:i + 1], in_=buf[i][:], op=ALU.add, axis=AX.X,
                                      apply_absolute_value=True).then_inc(summed, 1)
                dve.wait_ge(totals, 1)
                ch = Chain(dve, chain_sem)
                for i, (dram, out, scale) in enumerate(mats):
                    floor(dve, scale, tot[:, i:i + 1], 1.0 / (128 * dram.shape[1])).then_inc(summed, 1)
                dve.wait_ge(summed, 2 * M)
                for i, (dram, out, scale) in enumerate(mats):
                    dve.tensor_scalar(thr[:, i:i + 1], scale, 0.5, None, ALU.mult)
                    ch.step(dve.tensor_scalar(nthr[:, i:i + 1], scale, -0.5, None, ALU.mult))
                for i, (dram, out, scale) in enumerate(mats):
                    ch.step(dve.tensor_scalar(neg[i][:], buf[i][:], nthr[:, i:i + 1], None, ALU.is_lt))
                    ch.step(dve.scalar_tensor_tensor(out, buf[i][:], thr[:, i:i + 1], neg[i][:],
                                                     ALU.is_gt, ALU.subtract))


def stage_bit_gelu(nc, core, d):
    FC, HF = 8, 1024
    with Stage(nc, "bg") as outer:
        wq, wp = outer.sb("wq", [128, KC, HF], F16), outer.sb("wp", [128, FC, D], F16)
        scales = outer.sb("scales", [128, 2])
        lnw, lnb = outer.sb("lnw", [128, FC]), outer.sb("lnb", [128, FC])
        flat = lambda t: t[:].rearrange("p a n -> p (a n)")
        stage_ternary(nc, core, "bgt", [(d["w_fc"], flat(wq), scales[:, 0:1]), (d["w_proj"], flat(wp), scales[:, 1:2])],
                      lambda dve, out, tot, inv: dve.tensor_scalar(out, tot, inv, 1e-6, ALU.mult, ALU.add))
        with Stage(nc, "bgm") as st:
            two = range(2)
            g = [st.sb(f"g{p}", [L, HF]) for p in two]
            gn = st.sb("gn", [L, GB, HF])
            six, mv, rs = st.sb("six", [L, 2, 6]), st.sb("mv", [L, 2]), st.sb("rs", [L, 1])
            half = st.sb("half", [L, 1])
            full = [st.sb(f"full{p}", [128, GT]) for p in two]
            a_hi, a_lo = (st.sb(n, [128, FC, GT], F16) for n in ("a_hi", "a_lo"))
            ph = [st.ps(f"ph{p}", [L, HF]) for p in two]
            pt = [st.ps(f"pt{p}", [128, 512]) for p in two]
            po = [st.ps(f"po{p}", [L, D]) for p in two]
            small, pow_ready, half_made = st.sem("small"), st.sem("pow_ready"), st.sem("half_made")
            h_ready, gelu_done, stats, aggr, normed = (st.sem(n) for n in (
                "h_ready", "gelu_done", "stats", "aggr", "normed"))
            eps_added = st.sem("eps_added")
            t_ready, hi_ready, full_ready, lo_ready = (st.sem(n) for n in (
                "t_ready", "hi_ready", "full_ready", "lo_ready"))
            o_ready, o_free = ([st.sem(f"{n}{p}") for p in two] for n in ("o_ready", "o_free"))
            with nc.Block() as block:
                @block.sync
                def _(sp):
                    sp.dma_start(lnw[:], d["ln_w"]).then_inc(small, 16)
                    sp.dma_start(lnb[:], d["ln_b"]).then_inc(small, 16)

                @block.gpsimd
                def _(pool):
                    pool.memset(half[:], -0.5).then_inc(half_made, 1)
                    pool.wait_ge(half_made, 1)
                    with pool.Fori(0, NB) as b:
                        pool.wait_ge(eps_added, b + 1)
                        pool.tensor_tensor(rs[:], mv[:, 1:2], half[:], ALU.pow).then_inc(pow_ready, 1)

                @block.tensor
                def _(pe):
                    with pe.Fori(0, NG) as q:
                        for j in range(GB):
                            p = j % 2
                            if j >= 2:
                                pe.wait_ge(gelu_done, q * GB + (j - 1))
                            else:
                                pe.wait_ge(gelu_done, q * GB)
                            tok = bass.ds(q * GT + j * L, L)
                            for s in range(2):
                                n = 0
                                for k in range(KC):
                                    for x in (core.xt_hi, core.xt_lo):
                                        last = pe.matmul(ph[p][:, s * 512:(s + 1) * 512], x[:, k, tok],
                                                         wq[:, k, s * 512:(s + 1) * 512], start=n == 0, stop=n == 3)
                                        n += 1
                            last.then_inc(h_ready, 1)
                        pe.wait_ge(normed, q * GB + GB)
                        for f in range(FC):
                            pe.wait_ge(lo_ready, q * FC + max(f - 1, 0))
                            for j in range(GB):
                                last = pe.transpose(pt[f % 2][:, j * L:(j + 1) * L], gn[:, j, f * 128:(f + 1) * 128],
                                                    core.ident[0:L, 0:L])
                            last.then_inc(t_ready, 1)
                        pe.wait_ge(lo_ready, q * FC + FC)
                        for j in range(GB):
                            p = j % 2
                            pe.wait_ge(o_free[p], q * 2 + j // 2)
                            tok = slice(j * L, (j + 1) * L)
                            for f in range(FC):
                                pe.matmul(po[p][:], a_hi[:, f, tok], wp[:, f, :], start=f == 0, stop=False)
                                last = pe.matmul(po[p][:], a_lo[:, f, tok], wp[:, f, :], start=False,
                                                 stop=f == FC - 1)
                            last.then_inc(o_ready[p], 1)

                @block.scalar
                def _(act):
                    act.wait_ge(small, 32)
                    with act.Fori(0, NG) as q:
                        for j in range(GB):
                            p = j % 2
                            act.wait_ge(h_ready, q * GB + (j + 1))
                            act.wait_ge(normed, q * GB + max(j - 1, 0))
                            act.activation(g[p][:], ph[p][:], ACT.Gelu).then_inc(gelu_done, 1)
                        act.wait_ge(o_ready[0], q * 2)
                        act.wait_ge(o_ready[1], q * 2)
                        for f in range(FC):
                            act.wait_ge(t_ready, q * FC + (f + 1))
                            act.activation(a_hi[:, f, :], pt[f % 2][:, 0:GT], ACT.Identity, bias=lnb[:, f:f + 1],
                                           scale=lnw[:, f:f + 1]).then_inc(hi_ready, 1)

                @block.vector
                def _(dve):
                    dve.wait_ge(small, 32)
                    with dve.Fori(0, NG) as q:
                        for j in range(GB):
                            p, n = j % 2, q * GB + j
                            dve.wait_ge(gelu_done, n + 1)
                            dve.wait_ge(pow_ready, n)
                            dve.bn_stats(six[:, 0, :], g[p][:, 0:512])
                            dve.bn_stats(six[:, 1, :], g[p][:, 512:1024]).then_inc(stats, 1)
                            wait_alone(dve, core, stats, n + 1)
                            dve.bn_aggr(mv[:], six[:].rearrange("p a n -> p (a n)")).then_inc(aggr, 1)
                            dve.wait_ge(aggr, n + 1)
                            dve.tensor_scalar(mv[:, 1:2], mv[:, 1:2], EPS, None, ALU.add).then_inc(eps_added, 1)
                            dve.wait_ge(pow_ready, n + 1)
                            if j == 0:
                                dve.wait_ge(t_ready, q * FC)
                            dve.tensor_scalar(gn[:, j, :], g[p][:], mv[:, 0:1], rs[:],
                                              ALU.subtract, ALU.mult).then_inc(normed, 1)
                            dve.wait_ge(normed, n + 1)
                        for f in range(FC):
                            dve.wait_ge(hi_ready, q * FC + (f + 1))
                            dve.tensor_scalar(full[f % 2][:], pt[f % 2][:, 0:GT], lnw[:, f:f + 1], lnb[:, f:f + 1],
                                              ALU.mult, ALU.add).then_inc(full_ready, 1)
                            dve.wait_ge(full_ready, q * FC + (f + 1))
                            dve.tensor_tensor(a_lo[:, f, :], full[f % 2][:], a_hi[:, f, :],
                                              ALU.subtract).then_inc(lo_ready, 1)
                        for j in range(GB):
                            p = j % 2
                            dve.wait_ge(o_ready[p], q * 2 + (j // 2 + 1))
                            b = bass.ds(q * GB + j, 1)
                            dve.tensor_tensor(core.h[:, b, :], po[p][:].unsqueeze(1), core.h[:, b, :],
                                              ALU.add).then_inc(o_free[p], 1)


def stage_linear_attention(nc, core, d):
    Z = 64
    W2 = Z + D
    with Stage(nc, "la") as st:
        wt_hi, wt_lo = (st.sb(n, [128, KC, Z], F16) for n in ("wt_hi", "wt_lo"))
        wg_hi, wg_lo = (st.sb(n, [128, KC, W2], F16) for n in ("wg_hi", "wg_lo"))
        th_hi, th_lo = (st.sb(n, [Z, GT], F16) for n in ("th_hi", "th_lo"))
        two = range(2)
        pg_hi, pg_lo = ([st.sb(f"{n}{p}", [L, W2], F16) for p in two] for n in ("pg_hi", "pg_lo"))
        m_hi, m_lo = ([st.sb(f"{n}{p}", [Z, D], F16) for p in two] for n in ("m_hi", "m_lo"))
        pth = st.ps("pth", [Z, 512])
        ppg, pm, po = ([st.ps(f"{n}{p}", [s, 512]) for p in two] for n, s in (("ppg", L), ("pm", Z), ("po", L)))
        th_ready, th_high, th_split = st.sem("th_ready"), st.sem("th_high"), st.sem("th_split")
        g_ready, g_high, g_split, m_ready, m_high, m_split, o_ready, o_free = (
            [st.sem(f"{n}{p}") for p in two] for n in (
                "g_ready", "g_high", "g_split", "m_ready", "m_high", "m_split", "o_ready", "o_free"))
        flat = lambda t: t[:].rearrange("p a n -> p (a n)")
        w_sync, w_act, w_dve, (w_ready, w_n) = split_weights(st, core, [
            ("wt", d["w_theta"], flat(wt_hi), flat(wt_lo)), ("wg", d["w_phi_g"], flat(wg_hi), flat(wg_lo)),
        ])
        with nc.Block() as block:
            @block.sync
            def _(sp):
                w_sync(sp)

            @block.tensor
            def _(pe):
                pe.wait_ge(w_ready, w_n)
                with pe.Fori(0, NG) as q:
                    cols = bass.ds(q * GT, GT)
                    pe.wait_ge(th_split, q)
                    for k in range(KC):
                        last = mm3(pe, pth[:, 0:GT], wt_hi[:, k, :], wt_lo[:, k, :], core.xt_hi[:, k, cols],
                                   core.xt_lo[:, k, cols], k == 0, k == KC - 1)
                    last.then_inc(th_ready, 1)

                    def project(j):
                        p = j % 2
                        tok = bass.ds(q * GT + j * L, L)
                        pe.wait_ge(g_split[p], q * 2 + j // 2)
                        for k in range(KC):
                            last = mm3(pe, ppg[p][:, 0:W2], core.xt_hi[:, k, tok], core.xt_lo[:, k, tok],
                                       wg_hi[:, k, :], wg_lo[:, k, :], k == 0, k == KC - 1)
                        last.then_inc(g_ready[p], 1)

                    def collect(j):
                        p, before = j % 2, q * 2 + j // 2
                        pe.wait_ge(g_split[p], before + 1)
                        pe.wait_ge(m_split[p], before)
                        mm3(pe, pm[p][:, 0:D], pg_hi[p][:, 0:Z], pg_lo[p][:, 0:Z], pg_hi[p][:, Z:W2],
                            pg_lo[p][:, Z:W2], True, True).then_inc(m_ready[p], 1)

                    def spread(j):
                        p, before = j % 2, q * 2 + j // 2
                        pe.wait_ge(th_split, q + 1)
                        pe.wait_ge(m_split[p], before + 1)
                        pe.wait_ge(o_free[p], before)
                        tok = slice(j * L, (j + 1) * L)
                        mm3(pe, po[p][:, 0:D], th_hi[:, tok], th_lo[:, tok], m_hi[p][:], m_lo[p][:], True,
                            True).then_inc(o_ready[p], 1)

                    project(0)
                    for j in range(GB):
                        if j + 1 < GB:
                            project(j + 1)
                        collect(j)
                        if j:
                            spread(j - 1)
                    spread(GB - 1)

            @block.scalar
            def _(act):
                w_act(act)
                with act.Fori(0, NG) as q:
                    act.wait_ge(th_ready, q + 1)
                    for p in two:
                        act.wait_ge(o_ready[p], q * 2)
                    act.activation(th_hi[:], pth[:, 0:GT], ACT.Copy, scale=1.0 / WS).then_inc(th_high, 1)
                    for j in range(GB):
                        p, before = j % 2, q * 2 + j // 2
                        act.wait_ge(g_ready[p], before + 1)
                        act.wait_ge(m_ready[p], before)
                        act.activation(pg_hi[p][:], ppg[p][:, 0:W2], ACT.Copy, scale=1.0 / WS).then_inc(g_high[p], 1)
                        act.wait_ge(m_ready[p], before + 1)
                        act.wait_ge(o_ready[p], before)
                        act.activation(m_hi[p][:], pm[p][:, 0:D], ACT.Copy, scale=1.0 / 16).then_inc(m_high[p], 1)

            @block.vector
            def _(dve):
                w_dve(dve)

                def add(q, j):
                    p = j % 2
                    dve.wait_ge(o_ready[p], q * 2 + (j // 2 + 1))
                    b = bass.ds(q * GB + j, 1)
                    dve.tensor_tensor(core.h[:, b, :], po[p][:, 0:D].unsqueeze(1), core.h[:, b, :],
                                      ALU.add).then_inc(o_free[p], 1)

                with dve.Fori(0, NG) as q:
                    dve.wait_ge(th_high, q + 1)
                    dve.scalar_tensor_tensor(th_lo[:], pth[:, 0:GT], 1.0 / WS, th_hi[:], ALU.mult,
                                             ALU.subtract).then_inc(th_split, 1)
                    for j in range(GB):
                        p, before = j % 2, q * 2 + j // 2
                        dve.wait_ge(g_high[p], before + 1)
                        dve.scalar_tensor_tensor(pg_lo[p][:], ppg[p][:, 0:W2], 1.0 / WS, pg_hi[p][:], ALU.mult,
                                                 ALU.subtract).then_inc(g_split[p], 1)
                        dve.wait_ge(m_high[p], before + 1)
                        dve.scalar_tensor_tensor(m_lo[p][:], pm[p][:, 0:D], 1.0 / 16, m_hi[p][:], ALU.mult,
                                                 ALU.subtract).then_inc(m_split[p], 1)
                        if j:
                            add(q, j - 1)
                    add(q, GB - 1)


MAGIC = 12582912.0


def stage_bit_glu(nc, core, d):
    FC, HF = 8, 1024
    with Stage(nc, "glu") as outer:
        wg, wu = outer.sb("wg", [128, KC, HF], F16), outer.sb("wu", [128, KC, HF], F16)
        wd = outer.sb("wd", [128, FC, D], F16)
        scales = outer.sb("scales", [128, 3])
        xq = outer.sb("xq", [128, KC, T], F16)
        deq = outer.sb("deq", [L, NB, 2])
        flat = lambda t: t[:].rearrange("p a n -> p (a n)")
        stage_ternary(nc, core, "glut", [(d["w_gate"], flat(wg), scales[:, 0:1]), (d["w_up"], flat(wu), scales[:, 1:2]),
                                         (d["w_dn"], flat(wd), scales[:, 2:3])],
                      lambda dve, out, tot, inv: dve.tensor_scalar(out, tot, inv, 1e-5, ALU.mult, ALU.max))
        with Stage(nc, "gluq") as st:
            two = range(2)
            amax, sc = st.sb("amax", [L, NB]), st.sb("sc", [L, NB])
            xn = st.sb("xn", [L, NB, D])
            xi = st.sb("xi", [L, NB, D], F16)
            pt = [[st.ps(f"pt{u}{c}", [128, 512], F16) for c in range(KC)] for u in two]
            normed, chain_sem, rounded, t_ready = (st.sem(n) for n in ("normed", "chain", "rounded", "t_ready"))
            copied = [st.sem(f"copied{u}") for u in two]
            with nc.Block() as block:
                @block.vector
                def _(dve):
                    with dve.Fori(0, NB) as i:
                        b = bass.ds(i, 1)
                        dve.tensor_scalar(xn[:, b, :], core.h[:, b, :], core.mean[:, b], core.rstd[:, b],
                                          ALU.subtract, ALU.mult).then_inc(normed, 1)
                    dve.wait_ge(normed, NB)
                    ch = Chain(dve, chain_sem)
                    ch.step(dve.tensor_reduce(out=amax[:], in_=xn[:], op=ALU.max, axis=AX.X,
                                              apply_absolute_value=True))
                    ch.step(dve.tensor_scalar(amax[:], amax[:], 1e-5, None, ALU.max))
                    ch.step(dve.reciprocal(sc[:], amax[:]))
                    ch.step(dve.tensor_scalar(sc[:], sc[:], 127.0, None, ALU.mult))
                    ch.step(dve.tensor_scalar(amax[:], amax[:], 1.0 / 127.0, None, ALU.mult))
                    for n in range(2):
                        ch.step(dve.tensor_scalar(deq[:, :, n], amax[:], scales[0:L, n:n + 1], None, ALU.mult))
                    with dve.Fori(0, NB) as i:
                        b = bass.ds(i, 1)
                        dve.tensor_scalar(xn[:, b, :], xn[:, b, :], sc[:, b], MAGIC, ALU.mult,
                                          ALU.add).then_inc(normed, 1)
                    with dve.Fori(0, NB) as i:
                        b = bass.ds(i, 1)
                        dve.wait_ge(normed, i + (NB + 1))
                        dve.tensor_scalar(xi[:, b, :], xn[:, b, :], MAGIC, 127.0, ALU.subtract,
                                          ALU.min).then_inc(rounded, 1)

                @block.tensor
                def _(pe):
                    for q in range(NG):
                        u = q % 2
                        pe.wait_ge(copied[u], q // 2 * KC)
                        pe.wait_ge(rounded, q * GB + GB)
                        for c in range(KC):
                            for j in range(GB):
                                last = pe.transpose(pt[u][c][:, j * 128:j * 128 + L],
                                                    xi[:, q * GB + j, c * 128:(c + 1) * 128], core.ident16[0:L, 0:L])
                            last.then_inc(t_ready, 1)

                @block.scalar
                def _(act):
                    for q in range(NG):
                        for c in range(KC):
                            act.wait_ge(t_ready, q * KC + c + 1)
                            act.activation(xq[:, c, q * GT:(q + 1) * GT].rearrange("p (j t) -> p j t", t=L),
                                           pt[q % 2][c][:].rearrange("p (j t) -> p j t", t=128)[:, :, 0:L],
                                           ACT.Copy).then_inc(copied[q % 2], 1)
        with Stage(nc, "glum") as st:
            two = range(2)
            s = [st.sb(f"s{p}", [L, 512]) for p in two]
            gu = [st.sb(f"gu{p}", [L, HF]) for p in two]
            qi = [st.sb(f"qi{p}", [L, HF], F16) for p in two]
            qt = [st.sb(f"qt{p}", [128, FC, 128], F16) for p in two]
            amax, sc, dq, dg = ([st.sb(f"{n}{p}", [L, 1]) for p in two] for n in ("amax", "sc", "dq", "dg"))
            dg_done = st.sem("dg_done")
            pg, pu = ([st.ps(f"{n}{p}", [L, 512]) for p in two] for n in ("pg", "pu"))
            pt = [st.ps(f"pt{p}", [128, FC, 128], F16) for p in two]
            po = [st.ps(f"po{p}", [L, D]) for p in two]
            g_ready, silu_done, gu_done = st.sem("g_ready"), st.sem("silu_done"), st.sem("gu_done")
            maxed, chain_sem, quant = st.sem("maxed"), st.sem("chain"), st.sem("quant")
            t_ready, copied, o_ready, o_free = ([st.sem(f"{n}{p}") for p in two] for n in (
                "t_ready", "copied", "o_ready", "o_free"))
            with nc.Block() as block:
                @block.tensor
                def _(pe):
                    def turn(p, uses, tile):
                        pe.wait_ge(quant, tile + 1)
                        pe.wait_ge(copied[p], uses)
                        for f in range(FC):
                            last = pe.transpose(pt[p][:, f, 0:L], qi[p][:, f * 128:(f + 1) * 128],
                                                core.ident16[0:L, 0:L])
                        last.then_inc(t_ready[p], 1)

                    def down(p, uses):
                        pe.wait_ge(copied[p], uses + 1)
                        pe.wait_ge(o_free[p], uses)
                        for f in range(FC):
                            last = pe.matmul(po[p][:], qt[p][:, f, 0:L], wd[:, f, :], start=f == 0, stop=f == FC - 1)
                        last.then_inc(o_ready[p], 1)

                    def halves(tile):
                        for s in range(2):
                            pe.wait_ge(gu_done, tile * 2 - 2 + s + 1)
                            multiply(tile, s)

                    def multiply(tile, s):
                        tok = bass.ds(tile * L, L)
                        for out, w in ((pg[s], wg), (pu[s], wu)):
                            for k in range(KC):
                                last = pe.matmul(out[:], xq[:, k, tok], w[:, k, s * 512:(s + 1) * 512],
                                                 start=k == 0, stop=k == KC - 1)
                        last.then_inc(g_ready, 1)

                    for s in range(2):
                        multiply(0, s)
                    with pe.Fori(0, NB // 2 - 1) as i:
                        for u in range(2):
                            halves(i * 2 + (u + 1))
                            turn(u, i, i * 2 + u)
                            down(u, i)
                    halves(NB - 1)
                    for u in range(2):
                        turn(u, NB // 2 - 1, NB - 2 + u)
                        down(u, NB // 2 - 1)

                @block.scalar
                def _(act):
                    def step(j, p, before):
                        b = bass.ds(j, 1)
                        act.activation(dg[p][:].unsqueeze(1), deq[:, b, 0:1], ACT.Copy).then_inc(dg_done, 1)
                        act.wait_ge(dg_done, j + 1)
                        for s_ in range(2):
                            act.wait_ge(g_ready, j * 2 + (s_ + 1))
                            act.wait_ge(gu_done, j * 2)
                            act.activation(s[s_][:], pg[s_][:], ACT.Silu, scale=dg[p][:]).then_inc(silu_done, 1)
                        act.wait_ge(t_ready[p], before + 1)
                        act.wait_ge(o_ready[p], before)
                        act.activation(qt[p][:, :, 0:L], pt[p][:, :, 0:L], ACT.Copy).then_inc(copied[p], 1)
                    ring(act, NB, step)

                @block.vector
                def _(dve):
                    def step(j, p, before):
                        b = bass.ds(j, 1)
                        for s_ in range(2):
                            dve.wait_ge(silu_done, j * 2 + (s_ + 1))
                            dve.scalar_tensor_tensor(gu[p][:, s_ * 512:(s_ + 1) * 512], pu[s_][:],
                                                     deq[:, b, 1:2].rearrange("p a n -> p (a n)"), s[s_][:],
                                                     ALU.mult, ALU.mult).then_inc(gu_done, 1)
                        dve.wait_ge(gu_done, j * 2 + 2)
                        ch = Chain(dve, chain_sem, j * 5)
                        ch.step(dve.tensor_reduce(out=amax[p][:], in_=gu[p][:], op=ALU.max, axis=AX.X,
                                                  apply_absolute_value=True))
                        ch.step(dve.tensor_scalar(amax[p][:], amax[p][:], 1e-5, None, ALU.max))
                        dve.tensor_scalar(dq[p][:], amax[p][:], scales[0:L, 2:3], 1.0 / 127.0, ALU.mult, ALU.mult)
                        ch.step(dve.reciprocal(sc[p][:], amax[p][:]))
                        ch.step(dve.tensor_scalar(sc[p][:], sc[p][:], 127.0, None, ALU.mult))
                        ch.step(dve.tensor_scalar(gu[p][:], gu[p][:], sc[p][:], MAGIC, ALU.mult, ALU.add))
                        dve.wait_ge(t_ready[p], before)
                        dve.tensor_scalar(qi[p][:], gu[p][:], MAGIC, 127.0, ALU.subtract, ALU.min).then_inc(quant, 1)
                        dve.wait_ge(o_ready[p], before + 1)
                        dve.scalar_tensor_tensor(core.h[:, b, :], po[p][:].unsqueeze(1), dq[p][:], core.h[:, b, :],
                                                 ALU.mult, ALU.add).then_inc(o_free[p], 1)
                    ring(dve, NB, step)


def stage_attention(nc, core, d):
    H, HD = 16, 16
    HG = 4
    MS = 64.0
    with Stage(nc, "mha") as st:
        wl_hi, wl_lo = (st.sb(n, [128, H // HG, 128], F16) for n in ("wl_hi", "wl_lo"))
        wv_hi, wv_lo, wo_hi, wo_lo = (st.sb(n, [128, KC, D], F16) for n in ("wv_hi", "wv_lo", "wo_hi", "wo_lo"))
        bv_hi, bv_lo, bo_hi, bo_lo = (st.sb(n, [1, D], F16) for n in ("bv_hi", "bv_lo", "bo_hi", "bo_lo"))
        two = range(2)
        row, low_row = st.sb("row", [128, 1], I32), st.sb("low_row", [128, 1])
        to_q, to_same, to_cross = (st.sb(n, [128, 1]) for n in ("to_q", "to_same", "to_cross"))
        to_qm = st.sb("to_qm", [128, 1])
        spread = st.sb("spread", [128, H, L], F16)
        q, same, cross = ([st.sb(f"{n}{p}", [128, HG, L], F16) for p in two] for n in ("q", "same", "cross"))
        v = [st.sb(f"v{p}", [L, H, HD + 1]) for p in two]
        peak = [st.sb(f"peak{p}", [L, H]) for p in two]
        peaks8, qm = st.sb("peaks8", [L, 8, H]), st.sb("qm", [128, L], F16)
        am = [st.sb(f"am{p}", [128, L], F16) for p in two]
        prob = [st.sb(f"prob{r}", [L, HG, L]) for r in two]
        rec = st.sb("rec", [L, H])
        o = st.sb("o", [L, H, HD])
        ot_hi, ot_lo = (st.sb(n, [128, KC, L], F16) for n in ("ot_hi", "ot_lo"))
        pu = st.ps("pu", [128, 512])
        pvo = st.ps("pvo", [L, 2, D])
        s1, s2 = ([st.ps(f"{n}{r}", [L, 512]) for r in two] for n in ("s1", "s2"))
        pacc, pt = st.ps("pacc", [L, 512]), st.ps("pt", [128, 512])
        (made, masks, ones_set, u_ready, q_ready, ac_ready, v_ready, v_out, s1_ready, maxed, peaks_ready, mt_ready,
         qm_ready, am_ready, s2_ready, exped, pv_done, rec_ready, o_made, ot_ready, oh_ready, ol_ready, out_ready,
         h_added) = (st.sem(n) for n in (
             "made", "masks", "ones_set", "u_ready", "q_ready", "ac_ready", "v_ready", "v_out", "s1_ready", "maxed",
             "peaks_ready", "mt_ready", "qm_ready", "am_ready", "s2_ready", "exped", "pv_done", "rec_ready", "o_made",
             "ot_ready", "oh_ready", "ol_ready", "out_ready", "h_added"))
        flat = lambda t: t[:].rearrange("p a n -> p (a n)")
        w_sync, w_act, w_dve, (w_ready, w_n) = split_weights(st, core, [
            ("wl", d["w_l"], flat(wl_hi), flat(wl_lo)), ("wv", d["w_v"], flat(wv_hi), flat(wv_lo)),
            ("bv", d["b_v"], bv_hi[:], bv_lo[:]), ("wo", d["w_o"], flat(wo_hi), flat(wo_lo)),
            ("bo", d["b_o"], bo_hi[:], bo_lo[:]),
        ])
        heads = lambda t: t[:, 0:HG * L].rearrange("p (h t) -> p h t", t=L)

        def need(eng, sem, value):
            if not isinstance(value, int) or value > 0:
                eng.wait_ge(sem, value)

        def turns(eng, prologue, turn):
            prologue()
            turn(0, 0, True, True, True, False)
            with eng.Fori(0, (NB - 4) // 2) as i:
                for u in range(2):
                    turn(i * 2 + (1 + u), (1 + u) % 2, True, True, True, True)
            for j in range(NB - 3, NB + 1):
                turn(j, j % 2, j < NB, j + 1 < NB, j + 2 < NB, True)

        with nc.Block() as block:
            @block.sync
            def _(sp):
                w_sync(sp)

            @block.gpsimd
            def _(pool):
                ch = Chain(pool, made)
                ch.step(pool.iota(row[:], pattern=[[0, 1]], base=0, channel_multiplier=1))
                ch.step(pool.memset(spread[:], 0.0))
                for half in range(8):
                    ch.step(pool.affine_select(out=spread[:], in_=spread[:], compare_op=ALU.not_equal, fill=MS,
                                               base=-16 * half, pattern=[[-1, H], [0, L]], channel_multiplier=1))
                for p in two:
                    pool.memset(v[p][:, :, HD:HD + 1], 1.0).then_inc(ones_set, 1)

            @block.tensor
            def _(pe):
                def project_u(j):
                    need(pe, ac_ready, j)
                    cols = bass.ds(j * L, L)
                    for c in range(H // HG):
                        last = mm3(pe, pu[:, c * L:(c + 1) * L], wl_hi[:, c, :], wl_lo[:, c, :],
                                   core.xt_hi[:, c // 2, cols], core.xt_lo[:, c // 2, cols], True, True)
                    last.then_inc(u_ready, 1)

                def project_v(j):
                    need(pe, v_out, j)
                    need(pe, h_added, j - 2)
                    cols = bass.ds(j * L, L)
                    for k in range(KC):
                        mm3(pe, pvo[:, 0, :], core.xt_hi[:, k, cols], core.xt_lo[:, k, cols], wv_hi[:, k, :],
                            wv_lo[:, k, :], k == 0, False)
                    pe.matmul(pvo[:, 0, :], core.ones16[0:1, 0:L], bv_hi[:], start=False, stop=False)
                    pe.matmul(pvo[:, 0, :], core.ones16[0:1, 0:L], bv_lo[:], start=False,
                              stop=True).then_inc(v_ready, 1)

                def first_pass(j, p, g):
                    need(pe, ac_ready, j + 1)
                    need(pe, maxed, j * 4 + (g - 1))
                    rows = slice(32 * g, 32 * g + 32)
                    for c in range(HG):
                        out = s1[g % 2][:, c * L:(c + 1) * L]
                        pe.matmul(out, same[p][rows, c, :], same[p][rows, c, :], start=True, stop=False)
                        last = pe.matmul(out, same[p][rows, c, :], cross[p][rows, c, :], start=False, stop=True)
                    last.then_inc(s1_ready, 1)

                def turn_peaks(j):
                    need(pe, peaks_ready, j + 1)
                    need(pe, am_ready, j)
                    need(pe, ol_ready, j - 1)
                    pe.transpose(pt[:, 256:256 + L], peaks8[:].rearrange("p a h -> p (a h)"),
                                 core.ident[0:L, 0:L]).then_inc(mt_ready, 1)

                def second_pass(j, p, g):
                    need(pe, am_ready, j + 1)
                    need(pe, exped, j * 4 + (g - 1))
                    rows = slice(32 * g, 32 * g + 32)
                    for c in range(HG):
                        out = s2[g % 2][:, c * L:(c + 1) * L]
                        pe.matmul(out, same[p][rows, c, :], same[p][rows, c, :], start=True, stop=False)
                        pe.matmul(out, same[p][rows, c, :], cross[p][rows, c, :], start=False, stop=False)
                        last = pe.matmul(out, spread[rows, c * HG + g, :], am[p][rows, :], start=False, stop=True)
                    last.then_inc(s2_ready, 1)

                def weigh_v(j, p, g):
                    need(pe, exped, j * 4 + (g + 1))
                    if g == 0:
                        need(pe, v_out, j + 1)
                        need(pe, o_made, j)
                    for c in range(HG):
                        h = c * HG + g
                        last = pe.matmul(pacc[:, h * (HD + 1):(h + 1) * (HD + 1)], prob[g % 2][:, c, :],
                                         v[p][:, h, :], start=True, stop=True)
                    last.then_inc(pv_done, 1)

                def turn_o(j):
                    need(pe, o_made, j + 1)
                    need(pe, ol_ready, j)
                    for c in range(KC):
                        last = pe.transpose(pt[:, c * L:(c + 1) * L],
                                            o[:].rearrange("p h e -> p (h e)")[:, c * 128:(c + 1) * 128],
                                            core.ident[0:L, 0:L])
                    last.then_inc(ot_ready, 1)

                def project_out(j):
                    need(pe, ol_ready, j + 1)
                    need(pe, h_added, j)
                    need(pe, v_out, min(j + 3, NB) if isinstance(j, int) else j + 3)
                    for k in range(KC):
                        mm3(pe, pvo[:, 1, :], ot_hi[:, k, :], ot_lo[:, k, :], wo_hi[:, k, :], wo_lo[:, k, :],
                            k == 0, False)
                    pe.matmul(pvo[:, 1, :], core.ones16[0:1, 0:L], bo_hi[:], start=False, stop=False)
                    pe.matmul(pvo[:, 1, :], core.ones16[0:1, 0:L], bo_lo[:], start=False,
                              stop=True).then_inc(out_ready, 1)

                def prologue():
                    pe.wait_ge(w_ready, w_n)
                    pe.wait_ge(made, 10)
                    pe.wait_ge(ones_set, 2)
                    for j in range(2):
                        project_u(j)
                        project_v(j)
                    for g in range(4):
                        first_pass(0, 0, g)
                    turn_peaks(0)

                def turn(j, p, now, ahead1, ahead2, behind):
                    for g in range(4):
                        if now:
                            second_pass(j, p, g)
                        if behind and g == 1:
                            turn_o(j - 1)
                        if now and g:
                            weigh_v(j, p, g - 1)
                        if behind and g == 2:
                            project_out(j - 1)
                        if ahead1:
                            first_pass(j + 1, 1 - p, g)
                    if ahead2:
                        project_u(j + 2)
                        project_v(j + 2)
                    if now:
                        weigh_v(j, p, 3)
                    if ahead1:
                        turn_peaks(j + 1)

                turns(pe, prologue, turn)

            @block.scalar
            def _(act):
                def take_q(j, p):
                    act.wait_ge(u_ready, j + 1)
                    need(act, ac_ready, j - 1)
                    act.activation(q[p][:], heads(pu), ACT.Identity, scale=to_q[:]).then_inc(q_ready, 1)

                def take_v(j, p):
                    act.wait_ge(v_ready, j + 1)
                    need(act, pv_done, j * 4 - 4)
                    act.activation(v[p][:, :, 0:HD], pvo[:, 0, :].rearrange("p (h e) -> p h e", e=HD), ACT.Copy,
                                   scale=1.0 / WS).then_inc(v_out, 1)

                def take_qm(j):
                    act.wait_ge(mt_ready, j + 1)
                    need(act, am_ready, j)
                    act.activation(qm[:], pt[:, 256:256 + L], ACT.Identity, scale=to_qm[:]).then_inc(qm_ready, 1)

                def exponential(j, g):
                    act.wait_ge(s2_ready, j * 4 + (g + 1))
                    need(act, pv_done, j * 4 + (g - 1))
                    act.activation(prob[g % 2][:], heads(s2[g % 2]), ACT.Exp, scale=0.25).then_inc(exped, 1)

                def take_o(j):
                    act.wait_ge(ot_ready, j + 1)
                    need(act, out_ready, j)
                    act.activation(ot_hi[:], pt[:, 0:KC * L].rearrange("p (c t) -> p c t", t=L),
                                   ACT.Copy).then_inc(oh_ready, 1)

                def prologue():
                    w_act(act)
                    act.wait_ge(ones_set, 2)
                    act.wait_ge(masks, 8)
                    for j in range(2):
                        take_q(j, j)
                        take_v(j, j)
                    take_qm(0)

                def turn(j, p, now, ahead1, ahead2, behind):
                    for g in range(4):
                        if now:
                            exponential(j, g)
                        if behind and g == 1:
                            take_o(j - 1)
                    if ahead2:
                        take_q(j + 2, p)
                        take_v(j + 2, p)
                    if ahead1:
                        take_qm(j + 1)

                turns(act, prologue, turn)

            @block.vector
            def _(dve):
                def split_u(j, p):
                    dve.wait_ge(q_ready, j + 1)
                    need(dve, s2_ready, j * 4 - 4)
                    dve.scalar_tensor_tensor(same[p][:], heads(pu), to_same[:], q[p][:], ALU.mult, ALU.subtract)
                    dve.scalar_tensor_tensor(cross[p][:], heads(pu), to_cross[:], q[p][:], ALU.mult,
                                             ALU.add).then_inc(ac_ready, 1)

                def maxima(j, p, g):
                    dve.wait_ge(s1_ready, j * 4 + (g + 1))
                    if g == 0:
                        need(dve, peaks_ready, j - 1)
                    dve.tensor_reduce(out=peak[p][:].rearrange("p (c g) -> p g c", g=HG)[:, g, :], in_=heads(s1[g % 2]), op=ALU.max,
                                      axis=AX.X).then_inc(maxed, 1)

                def repeat_peaks(j, p):
                    dve.wait_ge(maxed, j * 4 + 4)
                    need(dve, mt_ready, j)
                    dve.tensor_scalar(peaks8[:], peak[p][:].unsqueeze(1).to_broadcast([L, 8, H]), -1.0 / MS, None,
                                      ALU.mult).then_inc(peaks_ready, 1)

                def split_peaks(j, p):
                    dve.wait_ge(qm_ready, j + 1)
                    need(dve, s2_ready, j * 4 - 4)
                    dve.scalar_tensor_tensor(am[p][:], pt[:, 256:256 + L], low_row[:], qm[:], ALU.mult,
                                             ALU.subtract).then_inc(am_ready, 1)

                def normalize(j):
                    dve.wait_ge(pv_done, j * 4 + 4)
                    need(dve, o_made, j)
                    acc = pacc[:, 0:H * (HD + 1)].rearrange("p (h e) -> p h e", e=HD + 1)
                    dve.reciprocal(rec[:], acc[:, :, HD]).then_inc(rec_ready, 1)
                    dve.wait_ge(rec_ready, j + 1)
                    need(dve, ot_ready, j)
                    dve.tensor_tensor(o[:], acc[:, :, 0:HD], rec[:].unsqueeze(2).to_broadcast([L, H, HD]),
                                      ALU.mult).then_inc(o_made, 1)

                def split_o(j):
                    dve.wait_ge(oh_ready, j + 1)
                    need(dve, out_ready, j)
                    dve.tensor_tensor(ot_lo[:], pt[:, 0:KC * L].rearrange("p (c t) -> p c t", t=L), ot_hi[:],
                                      ALU.subtract).then_inc(ol_ready, 1)

                def add(j):
                    dve.wait_ge(out_ready, j + 1)
                    b = bass.ds(j, 1)
                    dve.scalar_tensor_tensor(core.h[:, b, :], pvo[:, 1, :].unsqueeze(1), 1.0 / WS, core.h[:, b, :],
                                             ALU.mult, ALU.add).then_inc(h_added, 1)

                def prologue():
                    w_dve(dve)
                    dve.wait_ge(made, 1)
                    ch = Chain(dve, masks)
                    ch.step(dve.tensor_scalar(row[:], row[:], 16, None, ALU.bitwise_and))
                    ch.step(dve.tensor_scalar(row[:], row[:], 4, None, ALU.logical_shift_right))
                    ch.step(dve.tensor_copy(low_row[:], row[:]))
                    ch.step(dve.tensor_scalar(to_same[:], low_row[:], 1.0 / WS, None, ALU.mult))
                    ch.step(dve.tensor_scalar(to_cross[:], low_row[:], -1.0 / WS, 1.0 / WS, ALU.mult, ALU.add))
                    ch.step(dve.tensor_scalar(to_q[:], low_row[:], 2.0 / WS, -1.0 / WS, ALU.mult, ALU.add))
                    ch.step(dve.tensor_scalar(to_qm[:], low_row[:], 2.0, -1.0, ALU.mult, ALU.add))
                    dve.sem_inc(masks, 1)
                    for j in range(2):
                        split_u(j, j)
                    for g in range(4):
                        maxima(0, 0, g)
                    repeat_peaks(0, 0)
                    split_peaks(0, 0)

                def turn(j, p, now, ahead1, ahead2, behind):
                    if behind:
                        normalize(j - 1)
                    for g in range(4):
                        if ahead1:
                            maxima(j + 1, 1 - p, g)
                        if behind and g == 1:
                            split_o(j - 1)
                        if behind and g == 2:
                            add(j - 1)
                    if ahead1:
                        repeat_peaks(j + 1, 1 - p)
                    if ahead2:
                        split_u(j + 2, p)
                    if ahead1:
                        split_peaks(j + 1, 1 - p)

                turns(dve, prologue, turn)


def program(nc, d, out):
    Stage.available, Stage.resting = list(nc.free_semaphores), []
    with ExitStack() as ctx:
        core = Core()

        def sb(name, shape, dt=F32):
            return ctx.enter_context(nc.sbuf_tensor(name, shape, dt))

        core.h = sb("h", [L, NB, D])
        core.xt_hi, core.xt_lo = sb("xt_hi", [128, KC, T], F16), sb("xt_lo", [128, KC, T], F16)
        core.ident, core.ident16 = sb("ident", [128, 128]), sb("ident16", [128, 128], F16)
        core.ones16, core.eps = sb("ones16", [128, 128], F16), sb("eps", [128, 1])
        core.ones = sb("ones", [128, 128])
        core.mean, core.rstd = sb("mean", [L, NB]), sb("rstd", [L, NB])
        core.gate = nc.alloc_semaphore("gate", Stage.available.pop(0))
        stage_constants(nc, core)
        stage_tokens(nc, core, d)
        with ExitStack() as mid:
            ssm = Core()
            msb = lambda n, s, dt=F32: mid.enter_context(nc.sbuf_tensor(f"ssm_{n}", s, dt))
            ssm.dt_hi, ssm.dt_lo, ssm.dx_hi, ssm.dx_lo = (msb(n, [128, KC, T], F16)
                                                          for n in ("dt_hi", "dt_lo", "dx_hi", "dx_lo"))
            ssm.bt, ssm.ct, ssm.a = msb("bt", [128, T]), msb("ct", [128, T]), msb("a", [128, 32])
            with ExitStack() as mid2:
                ssm.xn = mid2.enter_context(nc.sbuf_tensor("ssm_xn", [128, KC, T], F32))
                with ExitStack() as mid3:
                    core.xn = mid3.enter_context(nc.sbuf_tensor("xn", [L, NB, D], F32))
                    gam, bet = (mid3.enter_context(nc.sbuf_tensor(n, [128, KC], F32)) for n in ("gam", "bet"))
                    stage_load(nc, "gb", [(gam[:], d["gamma"]), (bet[:], d["beta"])])
                    stage_norm_stats(nc, core, "st0", core.h)
                    stage_norm_twice(nc, core, d["d_param"])
                    stage_features(nc, core, "f0", core.xn, affine=(gam, bet), full=ssm.xn)
                stage_ssm_inputs(nc, core, d, ssm)
            stage_ssm_scan(nc, core, ssm)
        for m, tag, shared in ((Moe("m0", 15, 3, 4, 2, True, True, True), "ffn0", True),
                               (None, "gru", 0), (None, "bg", 0), (None, "la", 0), (None, "glu", 0), (None, "mha", 0),
                               (Moe("m3", 8, 1, 8, 8, False, False, False), "ffn3", False)):
            if m is None:
                stage_norm_stats(nc, core, tag + "s", core.h)
                if tag == "glu":
                    stage_bit_glu(nc, core, d)
                else:
                    stage_features(nc, core, tag + "f", core.h)
                    {"gru": stage_gru, "bg": stage_bit_gelu, "la": stage_linear_attention,
                     "mha": stage_attention}[tag](nc, core, d)
            else:
                with ExitStack() as mid:
                    msb = lambda n, s, dt=F16: mid.enter_context(nc.sbuf_tensor(f"{m.name}_{n}", s, dt))
                    m.w1_hi, m.w1_lo = (msb(n, [128, m.E, KC, m.NF * 128]) for n in ("w1_hi", "w1_lo"))
                    m.w2_hi, m.w2_lo = (msb(n, [128, m.E, m.FH, D]) for n in ("w2_hi", "w2_lo"))
                    m.b1 = msb("b1", [128, m.E, m.NF], F32)
                    m.weight, m.slot = msb("weight", [L, NB, m.K], F32), msb("slot", [L, NB, m.K], U32)
                    m.ids, m.expert = msb("ids", [128, m.blocks], U32), msb("expert", [1, m.blocks], I32)
                    m.rows = nc.dram_tensor(f"{m.name}_rows", [T, 2 * D], F16, kind="Internal").ap()
                    m.out = nc.dram_tensor(f"{m.name}_out", [m.blocks * 128, D], F32, kind="Internal").ap()
                    stage_moe_weights(nc, core, m, d)
                    stage_norm_stats(nc, core, m.name + "s", core.h)
                    stage_features(nc, core, m.name + "f", core.h, rows=m.rows)
                    stage_route(nc, core, m, d)
                    if shared:
                        stage_shared(nc, core, d)
                    stage_experts(nc, core, m)
                    stage_combine(nc, core, m)
        with Stage(nc, "out") as st:
            s = st.sem("stored")
            with nc.Block() as block:
                @block.sync
                def _(sp):
                    sp.dma_start(out.rearrange("b t d -> t b d"), core.h[:]).then_inc(s, 16)
                    sp.wait_ge(s, 16)


def stage_load(nc, name, pairs):
    with Stage(nc, name) as st:
        s = st.sem("landed")
        with nc.Block() as block:
            @block.sync
            def _(sp):
                for dst, src in pairs:
                    sp.dma_start(dst, src).then_inc(s, 16)
                sp.wait_ge(s, 16 * len(pairs))


def kmajor(w):
    K, N = w.shape
    return w.reshape(K // 128, 128, N).transpose(1, 0, 2).reshape(128, -1)


def columns(v):
    return v.reshape(-1, 128).T


def head_factors(params):
    H, HD = 16, 16
    rows, cols = np.tril_indices(HD)
    tril = np.zeros((H, HD, HD), params.dtype)
    tril[:, rows, cols] = params
    out = np.zeros((128, 4, 128), params.dtype)
    for h in range(H):
        c, j = divmod(h, 4)
        k = h * HD % 128
        for half in range(2):
            out[k:k + HD, c, 32 * j + 16 * half:32 * j + 16 * half + HD] = tril[h]
    return out.reshape(128, -1)


def layout(i):
    i = {k: np.asarray(v) for k, v in i.items()}
    P = 16
    x = i["x"]
    B, C, H, W = x.shape
    pt = x.reshape(B, C, H // P, P, W // P, P).transpose(0, 2, 4, 1, 3, 5).reshape(B * 36, C * P * P)
    out = {
        "patches": kmajor(pt.T), "txt": i["txt"].transpose(1, 0, 2),
        "w1": kmajor(i["L0_tok_W1"]), "b1": columns(i["L0_tok_b1"]), "w2": kmajor(i["L0_tok_W2"]),
        "b2": i["L0_tok_b2"][None, :],
        "w_dt": kmajor(i["L0_attn_W_dt"].T), "b_dt": columns(i["L0_attn_b_dt"]),
        "w_bc": np.stack([kmajor(np.tile(i[f"L0_attn_W_{s}"], (8, 1)).T) for s in "BC"], 1).reshape(128, -1),
        "a_log": i["L0_attn_A_log"].reshape(32, 8, 16).transpose(1, 2, 0).reshape(128, 32),
        "gamma": columns(i["L0_attn_gamma"]), "beta": columns(i["L0_attn_beta"]),
        "d_param": i["L0_attn_D_param"],
        "m0w": np.concatenate([np.stack([kmajor(w.T) for w in i["L0_ffn_fc1_w"]], 1),
                               np.stack([kmajor(w.T) for w in i["L0_ffn_fc2_w"]], 1)], 2),
        "m0mult": i["L0_ffn_geglu_mult"].reshape(15, 2, 128).transpose(2, 0, 1).reshape(128, -1),
        "m0b1": i["L0_ffn_fc1_b"].reshape(15, 4, 128).transpose(2, 0, 1),
        "m0router": kmajor(i["L0_ffn_gate_w"].T), "m0b2": i["L0_ffn_fc2_b"],
        "m3w": np.stack([kmajor(w) for e in range(8) for w in (i["L3_ffn_w1"][e], i["L3_ffn_w2"][e])], 1),
        "m3b1": i["L3_ffn_b1"].reshape(8, 8, 128).transpose(2, 0, 1),
        "m3router": kmajor(i["L3_ffn_w_router"]), "m3b2": i["L3_ffn_b2"],
    }
    out |= {
        "s1": kmajor(i["L0_ffn_s_fc1_w"].T), "s_b1": columns(i["L0_ffn_s_fc1_b"]),
        "s_mult": columns(i["L0_ffn_s_geglu_mult"]), "s2": kmajor(i["L0_ffn_s_fc2_w"].T),
        "s_b2": i["L0_ffn_s_fc2_b"][None, :],
        "w_f": kmajor(i["L1_attn_W_f"].T), "b_f": columns(i["L1_attn_b_f"]), "w_down": kmajor(i["L1_attn_W_down"].T),
        "w_fc": kmajor(i["L1_ffn_W_fc"].T), "w_proj": kmajor(i["L1_ffn_W_proj"].T),
        "ln_w": columns(i["L1_ffn_ln_w"]), "ln_b": columns(i["L1_ffn_ln_b"]),
        "w_theta": kmajor(i["L2_attn_W_theta"].T),
        "w_phi_g": kmajor(np.concatenate([i["L2_attn_W_phi"], i["L2_attn_W_g"]], 0).T),
        "w_gate": kmajor(i["L2_ffn_w_gate"].T), "w_up": kmajor(i["L2_ffn_w_up"].T),
        "w_dn": kmajor(i["L2_ffn_w_down"].T),
        "w_l": head_factors(i["L3_attn_params"]), "w_v": kmajor(i["L3_attn_Wv"].T), "b_v": i["L3_attn_bv"][None, :],
        "w_o": kmajor(i["L3_attn_Wo"].T), "b_o": i["L3_attn_bo"][None, :],
    }
    return {k: np.ascontiguousarray(v) for k, v in out.items()}


def kernel(**inputs):
    import numpy as np
    import concourse.bacc as bacc
    from concourse import mybir
    from concourse.bass_utils import run_bass_kernel_spmd

    nc = bacc.Bacc("TRN2", target_bir_lowering=False, num_devices=1)
    arrays = layout(inputs)
    aps = {name: nc.dram_tensor(name, a.shape, mybir.dt.from_np(a.dtype), kind="ExternalInput").ap()
           for name, a in arrays.items()}
    out = nc.dram_tensor("out", (NB, L, D), mybir.dt.float32, kind="ExternalOutput").ap()
    program(nc, aps, out)
    return run_bass_kernel_spmd(nc, [arrays], core_ids=[0]).results[0]["out"]
```

```python
import numpy as np
import concourse.bass as bass
from concourse import mybir
from contextlib import ExitStack

F32 = mybir.dt.float32
F16 = mybir.dt.float16
I32 = mybir.dt.int32
U32 = mybir.dt.uint32
ALU = mybir.AluOpType
ACT = mybir.ActivationFunctionType
AX = mybir.AxisListType

NB = 16
L = 113
LP = 36
D = 256
KC = D // 128
GB = 4
NG = NB // GB
GT = GB * L
T = NB * L
WS = 64.0
EPS = 1e-5


def wait_alone(eng, core, sem, value):
    if not isinstance(value, int):
        value = eng.to_reg(value)
    eng.wait_ge(core.gate, 1)
    eng.wait_ge(sem, value)


class Chain:

    def __init__(self, eng, sem, base=0):
        self.eng, self.sem, self.base, self.n = eng, sem, base, 0

    def step(self, ins):
        ins.then_inc(self.sem, 1)
        self.n += 1
        self.eng.wait_ge(self.sem, self.base + self.n)


class Stage:

    available, resting = [], []

    def __init__(self, nc, name):
        self.nc, self.name, self.ctx, self.sems = nc, name, ExitStack(), []

    def __enter__(self):
        return self

    def sb(self, name, shape, dt=F32):
        return self.ctx.enter_context(self.nc.sbuf_tensor(f"{self.name}_{name}", shape, dt))

    def ps(self, name, shape, dt=F32):
        return self.ctx.enter_context(self.nc.psum_tensor(f"{self.name}_{name}", shape, dt))

    def sem(self, name):
        number = Stage.available.pop(0)
        self.sems.append(self.nc.alloc_semaphore(f"{self.name}_{name}", number))
        return self.sems[-1]

    def __exit__(self, *exc):
        self.ctx.close()
        if exc[0] is None and self.sems:
            numbers = [s.num for s in self.sems]
            self.nc.clear_and_free_semaphores(self.sems)
            Stage.available += Stage.resting
            Stage.resting = numbers
        return False


class Core:
    pass


def split_weights(st, core, loads, again=()):
    bufs, sems = [], []
    names, again = [load[0] for load in loads], dict(again)
    for name, dram, hi, lo in loads:
        bufs.append(bufs[names.index(again[name])] if name in again else st.sb(f"{name}_f32", list(dram.shape)))
        sems.append(st.sem(f"{name}_landed"))
    hi_done = st.sem("weights_hi")
    ready = st.sem("weights_split")

    def on_sync(sp):
        for (name, dram, hi, lo), buf, landed in zip(loads, bufs, sems):
            if name in again:
                sp.wait_ge(ready, names.index(again[name]) + 1)
            sp.dma_start(buf[:], dram).then_inc(landed, 16)

    def on_scalar(act):
        for (name, dram, hi, lo), buf, landed in zip(loads, bufs, sems):
            act.wait_ge(landed, 16)
            act.activation(hi, buf[:], ACT.Copy, scale=WS).then_inc(hi_done, 1)

    def on_vector(dve):
        for n, ((name, dram, hi, lo), buf) in enumerate(zip(loads, bufs)):
            dve.wait_ge(hi_done, n + 1)
            dve.scalar_tensor_tensor(lo, buf[:], WS, hi, ALU.mult, ALU.subtract).then_inc(ready, 1)

    return on_sync, on_scalar, on_vector, (ready, len(loads))


def mm3(pe, out, w_hi, w_lo, x_hi, x_lo, start, stop):
    pe.matmul(out, w_hi, x_hi, start=start, stop=False)
    pe.matmul(out, w_hi, x_lo, start=False, stop=False)
    return pe.matmul(out, w_lo, x_hi, start=False, stop=stop)


def stage_constants(nc, core):
    with Stage(nc, "const") as st:
        zeroed, made, cast = st.sem("zeroed"), st.sem("made"), st.sem("cast")
        with nc.Block() as block:
            @block.gpsimd
            def _(pool):
                pool.memset(core.ident[:, :], 0.0).then_inc(zeroed, 1)
                pool.wait_ge(zeroed, 1)
                pool.affine_select(out=core.ident[:, :], in_=core.ident[:, :], compare_op=ALU.not_equal, fill=1.0,
                                   base=0, pattern=[[-1, 128]], channel_multiplier=1).then_inc(made, 1)
                pool.memset(core.eps[:, :], EPS)
                pool.memset(core.ones16[:, :], 1.0)
                pool.memset(core.ones[:, :], 1.0)
                pool.wait_ge(made, 1)
                pool.tensor_copy(core.ident16[:, :], core.ident[:, :]).then_inc(cast, 1)
                pool.sem_inc(core.gate, 1)
                pool.wait_ge(cast, 1)


def stage_tokens(nc, core, d):
    PC = 6
    NP = NB * LP
    HP = NP // 2
    with Stage(nc, "tok") as st:
        pt_hi, pt_lo = st.sb("pt_hi", [128, PC, NP], F16), st.sb("pt_lo", [128, PC, NP], F16)
        w1_hi, w1_lo = st.sb("w1_hi", [128, PC, D], F16), st.sb("w1_lo", [128, PC, D], F16)
        w2_hi, w2_lo = st.sb("w2_hi", [128, KC, D], F16), st.sb("w2_lo", [128, KC, D], F16)
        b2_hi, b2_lo = st.sb("b2_hi", [1, D], F16), st.sb("b2_lo", [1, D], F16)
        b1 = st.sb("b1", [128, KC])
        g = st.sb("g", [128, KC, NP])
        g_hi, g_lo = st.sb("g_hi", [128, KC, NP], F16), st.sb("g_lo", [128, KC, NP], F16)
        hid = [st.ps(f"hid{j}", [128, 512]) for j in range(2)]
        emb = [st.ps(f"emb{j}", [128, D]) for j in range(2)]
        consts = st.sem("consts_landed")
        hid_ready, hid_free = st.sem("hid_ready"), st.sem("hid_free")
        g_high, g_split = st.sem("g_high"), st.sem("g_split")
        emb_ready = [st.sem(f"emb_ready{j}") for j in range(2)]
        emb_free = [st.sem(f"emb_free{j}") for j in range(2)]
        text = st.sem("text_landed")
        w_sync, w_act, w_dve, (w_ready, w_n) = split_weights(st, core, [
            ("w1", d["w1"], w1_hi[:].rearrange("p c n -> p (c n)"), w1_lo[:].rearrange("p c n -> p (c n)")),
            ("pt", d["patches"], pt_hi[:].rearrange("p c n -> p (c n)"), pt_lo[:].rearrange("p c n -> p (c n)")),
            ("w2", d["w2"], w2_hi[:].rearrange("p c n -> p (c n)"), w2_lo[:].rearrange("p c n -> p (c n)")),
            ("b2", d["b2"], b2_hi[:], b2_lo[:]),
        ])
        units = [(c, s) for c in range(KC) for s in range(2)]
        with nc.Block() as block:
            @block.sync
            def _(sp):
                w_sync(sp)
                sp.dma_start(b1[:], d["b1"]).then_inc(consts, 16)
                sp.dma_start(core.h[LP:L, :, :], d["txt"]).then_inc(text, 16)
                sp.wait_ge(text, 16)

            @block.scalar
            def _(act):
                w_act(act)
                act.wait_ge(consts, 16)
                for n, (c, s) in enumerate(units):
                    act.wait_ge(hid_ready, n + 1)
                    act.activation(g[:, c, s * HP:(s + 1) * HP], hid[n % 2][:, 0:HP], ACT.Silu, bias=b1[:, c:c + 1],
                                   scale=1.0 / (WS * WS)).then_inc(hid_free, 1)
                    act.wait_ge(hid_free, n + 1)
                    act.activation(g_hi[:, c, s * HP:(s + 1) * HP], g[:, c, s * HP:(s + 1) * HP],
                                   ACT.Copy).then_inc(g_high, 1)

            @block.vector
            def _(dve):
                w_dve(dve)
                for n, (c, s) in enumerate(units):
                    dve.wait_ge(g_high, n + 1)
                    dve.tensor_tensor(g_lo[:, c, s * HP:(s + 1) * HP], g[:, c, s * HP:(s + 1) * HP],
                                      g_hi[:, c, s * HP:(s + 1) * HP], ALU.subtract).then_inc(g_split, 1)
                with dve.Fori(0, NB // 2) as i:
                    for j in range(2):
                        dve.wait_ge(emb_ready[j], i + 1)
                        dve.tensor_scalar(core.h[0:LP, bass.ds(2 * i + j, 1), :],
                                          emb[j][0:LP, :].rearrange("p (a n) -> p a n", a=1),
                                          1.0 / WS, None, ALU.mult).then_inc(emb_free[j], 1)

            @block.tensor
            def _(pe):
                pe.wait_ge(w_ready, w_n)
                for n, (c, s) in enumerate(units):
                    if n >= 2:
                        pe.wait_ge(hid_free, n - 1)
                    for k in range(PC):
                        last = mm3(pe, hid[n % 2][:, 0:HP], w1_hi[:, k, c * 128:(c + 1) * 128],
                                   w1_lo[:, k, c * 128:(c + 1) * 128], pt_hi[:, k, s * HP:(s + 1) * HP],
                                   pt_lo[:, k, s * HP:(s + 1) * HP], k == 0, k == PC - 1)
                    last.then_inc(hid_ready, 1)
                pe.wait_ge(g_split, len(units))
                with pe.Fori(0, NB // 2) as i:
                    for j in range(2):
                        pe.wait_ge(emb_free[j], i)
                        tok = bass.ds(i * (2 * LP) + j * LP, LP)
                        for k in range(KC):
                            mm3(pe, emb[j][0:LP, :], g_hi[:, k, tok], g_lo[:, k, tok],
                                w2_hi[:, k, :], w2_lo[:, k, :], k == 0, False)
                        pe.matmul(emb[j][0:LP, :], core.ones16[0:1, 0:LP], b2_hi[:], start=False, stop=False)
                        pe.matmul(emb[j][0:LP, :], core.ones16[0:1, 0:LP], b2_lo[:], start=False,
                                  stop=True).then_inc(emb_ready[j], 1)


def stage_norm_stats(nc, core, name, src, second=None):
    with Stage(nc, name) as st:
        six = st.sb("six", [L, NB, 6])
        s, dd, sd = st.sb("s", [L, NB]), st.sb("dd", [L, NB]), st.sb("sd", [L, NB])
        var = st.sb("var", [L, NB])
        counted, chain_sem = st.sem("counted"), st.sem("chain")
        var_ready, sd_ready = st.sem("var_ready"), st.sem("sd_ready")
        with nc.Block() as block:
            @block.scalar
            def _(act):
                act.preload_act_table(ACT.Sqrt)
                act.wait_ge(var_ready, 1)
                act.activation(sd[:], var[:], ACT.Sqrt, bias=core.eps[0:L, :], scale=1.0 / D).then_inc(sd_ready, 1)

            @block.vector
            def _(dve):
                for b in range(NB):
                    ins = dve.bn_stats(six[:, b, :], src[:, b, :])
                ins.then_inc(counted, 1)
                dve.wait_ge(counted, 1)
                norm_moments(dve, Chain(dve, chain_sem), six, s, dd, var, core.mean, var_ready)
                dve.wait_ge(sd_ready, 1)
                dve.reciprocal(core.rstd[:], sd[:]).then_inc(counted, 1)
                dve.wait_ge(counted, 2)


def norm_moments(dve, chain, six, s, dd, var, mean, var_ready):
    me, m2e, mo, m2o = six[:, :, 1], six[:, :, 2], six[:, :, 4], six[:, :, 5]
    dve.tensor_tensor(s[:], me, mo, ALU.add)
    chain.step(dve.tensor_tensor(dd[:], me, mo, ALU.subtract))
    dve.tensor_scalar(mean[:], s[:], 0.5, None, ALU.mult)
    chain.step(dve.tensor_tensor(dd[:], dd[:], dd[:], ALU.mult))
    chain.step(dve.scalar_tensor_tensor(var[:], dd[:], D / 4.0, m2e, ALU.mult, ALU.add))
    dve.tensor_tensor(var[:], var[:], m2o, ALU.add).then_inc(var_ready, 1)


def stage_features(nc, core, name, src, affine=None, full=None, rows=None):
    with Stage(nc, name) as st:
        xr = [st.sb(f"xr{u}", [L, GB, D]) for u in range(2)]
        tp = [[st.ps(f"tp{u}{c}", [128, 512]) for c in range(KC)] for u in range(2)]
        normed, tp_ready, hi_done = st.sem("normed"), st.sem("tp_ready"), st.sem("hi_done")
        tp_free = [st.sem(f"tp_free{u}") for u in range(2)]
        if affine is not None:
            full_done = st.sem("full_done")
        if rows is not None:
            parts = [st.sb(f"parts{u}", [L, GB, 2, D], F16) for u in range(2)]
            row_hi, row_lo = st.sem("row_hi"), st.sem("row_lo")
            stored = [st.sem(f"stored{u}") for u in range(2)]
        with nc.Block() as block:
            @block.vector
            def _(dve):
                for i in range(NG // 2):
                    for u in range(2):
                        if rows is not None:
                            dve.wait_ge(row_lo, i * 2)
                        for j in range(GB):
                            b = bass.ds(i * (2 * GB) + (u * GB + j), 1)
                            dve.tensor_scalar(xr[u][:, j, :].rearrange("p (a n) -> p a n", a=1), src[:, b, :],
                                              core.mean[:, b], core.rstd[:, b],
                                              ALU.subtract, ALU.mult).then_inc(normed, 1)
                    for u in range(2):
                        for c in range(KC):
                            done = i * 4 + (u * KC + c + 1)
                            cols = bass.ds(i * (2 * GT) + u * GT, GT)
                            source = tp[u][c][:, 0:GT]
                            dve.wait_ge(hi_done, done)
                            if affine is not None:
                                source = full[:, c, cols]
                                dve.tensor_scalar(source, tp[u][c][:, 0:GT], affine[0][:, c:c + 1],
                                                  affine[1][:, c:c + 1], ALU.mult, ALU.add).then_inc(full_done, 1)
                                dve.wait_ge(full_done, done)
                            dve.tensor_tensor(core.xt_lo[:, c, cols], source, core.xt_hi[:, c, cols],
                                              ALU.subtract).then_inc(tp_free[u], 1)

            @block.tensor
            def _(pe):
                for i in range(NG // 2):
                    for u in range(2):
                        pe.wait_ge(tp_free[u], i * KC)
                        for j in range(GB):
                            pe.wait_ge(normed, i * 8 + (u * 4 + j + 1))
                            for c in range(KC):
                                last = pe.transpose(tp[u][c][:, j * L:(j + 1) * L], xr[u][:, j, c * 128:(c + 1) * 128],
                                                    core.ident[0:L, 0:L])
                                if j == GB - 1:
                                    last.then_inc(tp_ready, 1)

            @block.scalar
            def _(act):
                for i in range(NG // 2):
                    for u in range(2):
                        for c in range(KC):
                            cols = bass.ds(i * (2 * GT) + u * GT, GT)
                            act.wait_ge(tp_ready, i * 4 + (u * KC + c + 1))
                            if affine is not None:
                                act.activation(core.xt_hi[:, c, cols], tp[u][c][:, 0:GT], ACT.Identity,
                                               bias=affine[1][:, c:c + 1],
                                               scale=affine[0][:, c:c + 1]).then_inc(hi_done, 1)
                            else:
                                act.activation(core.xt_hi[:, c, cols], tp[u][c][:, 0:GT], ACT.Copy).then_inc(hi_done, 1)
                        if rows is not None:
                            act.wait_ge(stored[u], i * 16)
                            act.activation(parts[u][:, :, 0, :], xr[u][:], ACT.Copy).then_inc(row_hi, 1)

            if rows is not None:
                @block.gpsimd
                def _(pool):
                    for i in range(NG // 2):
                        for u in range(2):
                            pool.wait_ge(row_hi, i * 2 + (u + 1))
                            pool.tensor_tensor(parts[u][:, :, 1, :], xr[u][:], parts[u][:, :, 0, :],
                                               ALU.subtract).then_inc(row_lo, 1)

                @block.sync
                def _(sp):
                    table = rows.rearrange("(g b t) n -> g t b n", b=GB, t=L)
                    with sp.Fori(0, NG // 2) as i:
                        for u in range(2):
                            sp.wait_ge(row_lo, i * 2 + (u + 1))
                            sp.dma_start(table[bass.ds(i * 2 + u, 1)].rearrange("a t b n -> (a t) b n"),
                                         parts[u][:].rearrange("p b a n -> p b (a n)").bitcast(F32)).then_inc(stored[u], 16)
                    for u in range(2):
                        sp.wait_ge(stored[u], 16 * (NG // 2))


def stage_norm_twice(nc, core, d_row):
    with Stage(nc, "twice") as st:
        skip = st.sb("skip", [L, D])
        six = st.sb("six", [L, NB, 6])
        s, dd, sd, var = (st.sb(n, [L, NB]) for n in ("s", "dd", "sd", "var"))
        prod = [st.sb(f"prod{j}", [L, GB // 2, D]) for j in range(2)]
        landed, normed, counted = st.sem("skip_landed"), st.sem("normed"), st.sem("counted")
        chain_sem, pool_mul, pool_add = st.sem("chain"), st.sem("pool_mul"), st.sem("pool_add")
        var_ready, sd_ready = st.sem("var_ready"), st.sem("sd_ready")
        with nc.Block() as block:
            @block.sync
            def _(sp):
                sp.dma_start(skip[:], d_row.partition_broadcast(L)).then_inc(landed, 16)

            @block.vector
            def _(dve):
                for b in range(NB):
                    dve.tensor_scalar(core.xn[:, b, :], core.h[:, b, :], core.mean[:, b:b + 1], core.rstd[:, b:b + 1],
                                      ALU.subtract, ALU.mult).then_inc(normed, 1)
                for b in range(NB):
                    dve.wait_ge(normed, b + 1)
                    dve.bn_stats(six[:, b, :], core.xn[:, b, :]).then_inc(counted, 1)
                dve.wait_ge(counted, NB)
                norm_moments(dve, Chain(dve, chain_sem), six, s, dd, var, core.mean, var_ready)
                dve.wait_ge(sd_ready, 1)
                dve.reciprocal(core.rstd[:], sd[:]).then_inc(counted, 1)
                dve.wait_ge(counted, NB + 1)

            @block.scalar
            def _(act):
                act.wait_ge(var_ready, 1)
                act.activation(sd[:], var[:], ACT.Sqrt, bias=core.eps[0:L, :], scale=1.0 / D).then_inc(sd_ready, 1)

            @block.gpsimd
            def _(pool):
                pool.wait_ge(landed, 16)
                row = skip[:].unsqueeze(1).to_broadcast([L, GB // 2, D])
                for n in range(2 * NG):
                    b = slice(n * (GB // 2), (n + 1) * (GB // 2))
                    pool.wait_ge(normed, b.stop)
                    if n >= 2:
                        pool.wait_ge(pool_add, n - 1)
                    pool.tensor_tensor(prod[n % 2][:], core.xn[:, b, :], row, ALU.mult).then_inc(pool_mul, 1)
                    pool.wait_ge(pool_mul, n + 1)
                    pool.tensor_tensor(core.h[:, b, :], core.h[:, b, :], prod[n % 2][:], ALU.add).then_inc(pool_add, 1)


def stage_ssm_inputs(nc, core, d, ssm):
    with Stage(nc, "ssmin") as st:
        wd_hi, wd_lo = st.sb("wd_hi", [128, KC, D], F16), st.sb("wd_lo", [128, KC, D], F16)
        wb_hi, wb_lo = st.sb("wb_hi", [128, 2, KC, 128], F16), st.sb("wb_lo", [128, 2, KC, 128], F16)
        b_dt = st.sb("b_dt", [128, KC])
        alog = st.sb("alog", [128, 32])
        az, ez, lz, rz, dt, dx = ([st.sb(f"{n}{j}", [128, GT]) for j in range(2)]
                                  for n in ("az", "ez", "lz", "rz", "dt", "dx"))
        pd = [st.ps(f"pd{j}", [128, 512]) for j in range(2)]
        pb = [st.ps(f"pb{j}", [128, 512]) for j in range(2)]
        landed = st.sem("landed")
        pd_ready, pd_abs, pd_lin, ln_done = st.sem("pd_ready"), st.sem("pd_abs"), st.sem("pd_lin"), st.sem("ln_done")
        pb_ready, pb_free = st.sem("pb_ready"), st.sem("pb_free")
        act_chain, neg = st.sem("act_chain"), st.sem("neg")
        dt_done, dt_hi, dx_done, dx_hi, split = (st.sem(n) for n in ("dt_done", "dt_hi", "dx_done", "dx_hi", "split"))
        flat = lambda t: t[:].rearrange("p a n -> p (a n)")
        w_sync, w_act, w_dve, (w_ready, w_n) = split_weights(st, core, [
            ("wd", d["w_dt"], flat(wd_hi), flat(wd_lo)),
            ("wb", d["w_bc"], wb_hi[:].rearrange("p s c n -> p (s c n)"), wb_lo[:].rearrange("p s c n -> p (s c n)")),
        ])
        with nc.Block() as block:
            @block.sync
            def _(sp):
                w_sync(sp)
                sp.dma_start(b_dt[:], d["b_dt"]).then_inc(landed, 16)
                sp.dma_start(alog[:], d["a_log"]).then_inc(landed, 16)

            @block.tensor
            def _(pe):
                pe.wait_ge(w_ready, w_n)
                with pe.Fori(0, NG) as i:
                    cols = bass.ds(i * GT, GT)
                    for c in range(KC):
                        pe.wait_ge(pd_lin, i * 2)
                        pe.wait_ge(pd_abs, i * 2)
                        for k in range(KC):
                            last = mm3(pe, pd[c][:, 0:GT], wd_hi[:, k, c * 128:(c + 1) * 128],
                                       wd_lo[:, k, c * 128:(c + 1) * 128], core.xt_hi[:, k, cols],
                                       core.xt_lo[:, k, cols], k == 0, k == KC - 1)
                        last.then_inc(pd_ready, 1)
                    for s in range(2):
                        pe.wait_ge(pb_free, i * 2)
                        for k in range(KC):
                            last = mm3(pe, pb[s][:, 0:GT], wb_hi[:, s, k, :], wb_lo[:, s, k, :],
                                       core.xt_hi[:, k, cols], core.xt_lo[:, k, cols], k == 0, k == KC - 1)
                        last.then_inc(pb_ready, 1)

            @block.scalar
            def _(act):
                act.preload_act_table_set("natural_log_exp_and_others")
                w_act(act)
                act.wait_ge(landed, 32)
                act.activation(ssm.a[:], alog[:], ACT.Exp).then_inc(neg, 1)
                act.wait_ge(neg, 1)
                act.activation(ssm.a[:], ssm.a[:], ACT.Copy, scale=-1.0).then_inc(neg, 1)
                with act.Fori(0, NG) as i:
                    cols = bass.ds(i * GT, GT)
                    for c in range(KC):
                        act.wait_ge(pd_ready, i * 2 + (c + 1))
                        act.activation(az[c][:], pd[c][:, 0:GT], ACT.Abs, bias=b_dt[:, c:c + 1],
                                       scale=1.0 / WS).then_inc(pd_abs, 1)
                    for c in range(KC):
                        act.wait_ge(pd_abs, i * 2 + (c + 1))
                        act.activation(ez[c][:], az[c][:], ACT.Exp, scale=-1.0).then_inc(act_chain, 1)
                    for c in range(KC):
                        act.wait_ge(act_chain, i * 2 + (c + 1))
                        act.wait_ge(dt_done, i * 2)
                        act.activation(lz[c][:], ez[c][:], ACT.Ln, bias=1.0).then_inc(ln_done, 1)
                    for s, dst in enumerate((ssm.bt, ssm.ct)):
                        act.wait_ge(pb_ready, i * 2 + (s + 1))
                        act.activation(dst[:, cols], pb[s][:, 0:GT], ACT.Copy, scale=1.0 / WS).then_inc(pb_free, 1)
                    for c in range(KC):
                        act.wait_ge(dt_done, i * 2 + (c + 1))
                        act.activation(ssm.dt_hi[:, c, cols], dt[c][:], ACT.Copy).then_inc(dt_hi, 1)
                    for c in range(KC):
                        act.wait_ge(dx_done, i * 2 + (c + 1))
                        act.activation(ssm.dx_hi[:, c, cols], dx[c][:], ACT.Copy).then_inc(dx_hi, 1)
                act.wait_ge(neg, 2)

            @block.vector
            def _(dve):
                w_dve(dve)
                dve.wait_ge(landed, 32)
                with dve.Fori(0, NG) as i:
                    cols = bass.ds(i * GT, GT)
                    for c in range(KC):
                        dve.wait_ge(pd_abs, i * 2 + (c + 1))
                        dve.tensor_scalar(rz[c][:], pd[c][:, 0:GT], 1.0 / WS, b_dt[:, c:c + 1],
                                          ALU.mult, ALU.add).then_inc(pd_lin, 1)
                    for c in range(KC):
                        dve.wait_ge(ln_done, i * 2 + (c + 1))
                        dve.wait_ge(pd_lin, i * 2 + (c + 1))
                        dve.wait_ge(split, i * 4)
                        dve.scalar_tensor_tensor(dt[c][:], rz[c][:], 0.0, lz[c][:],
                                                 ALU.max, ALU.add).then_inc(dt_done, 1)
                    for c in range(KC):
                        dve.wait_ge(dt_done, i * 2 + (c + 1))
                        dve.tensor_tensor(dx[c][:], dt[c][:], ssm.xn[:, c, cols], ALU.mult).then_inc(dx_done, 1)
                    for c in range(KC):
                        dve.wait_ge(dt_hi, i * 2 + (c + 1))
                        dve.tensor_tensor(ssm.dt_lo[:, c, cols], dt[c][:], ssm.dt_hi[:, c, cols],
                                          ALU.subtract).then_inc(split, 1)
                    for c in range(KC):
                        dve.wait_ge(dx_hi, i * 2 + (c + 1))
                        dve.tensor_tensor(ssm.dx_lo[:, c, cols], dx[c][:], ssm.dx_hi[:, c, cols],
                                          ALU.subtract).then_inc(split, 1)


def stage_ssm_scan(nc, core, ssm):
    NS, DS = 16, 8
    UN = 128 // DS
    R = 4
    with Stage(nc, "scan") as st:
        sel = st.sb("sel", [128, UN, 128], F16)
        ssum = st.sb("ssum", [128, UN, 128])
        abar = [st.sb(f"abar{r}", [128, GB, L]) for r in range(R)]
        bx = [st.sb(f"bx{r}", [128, GT]) for r in range(R)]
        hs = [st.sb(f"hs{r}", [128, GT]) for r in range(R)]
        ch = [st.sb(f"ch{r}", [128, GT]) for r in range(R)]
        yt = [st.sb(f"yt{r}", [128, GT]) for r in range(2)]
        pdt = [st.ps(f"pdt{j}", [128, 512]) for j in range(2)]
        pdx = [st.ps(f"pdx{j}", [128, 512]) for j in range(2)]
        py = [st.ps(f"py{j}", [128, 512]) for j in range(2)]
        pt = [st.ps(f"pt{j}", [128, GB, 128]) for j in range(2)]
        sel_made, ssum_made, zeroed = st.sem("sel_made"), st.sem("ssum_made"), st.sem("zeroed")
        dt_ready, dx_ready = st.sem("dt_ready"), st.sem("dx_ready")
        decay, drive, scanned, weighed = st.sem("decay"), st.sem("drive"), st.sem("scanned"), st.sem("weighed")
        summed = st.sem("summed")
        y_ready, y_out, turned, added = st.sem("y_ready"), st.sem("y_out"), st.sem("turned"), st.sem("added")
        per_q = KC * UN
        with nc.Block() as block:
            @block.gpsimd
            def _(pool):
                made = Chain(pool, sel_made)
                made.step(pool.memset(sel[:], 0.0))
                made.step(pool.affine_select(out=sel[:].rearrange("p g (s n) -> p g s n", n=NS),
                                             in_=sel[:].rearrange("p g (s n) -> p g s n", n=NS),
                                             compare_op=ALU.not_equal, fill=1.0, base=0,
                                             pattern=[[-DS, UN], [-1, DS], [0, NS]], channel_multiplier=1))
                made.step(pool.memset(ssum[:], 1.0))
                made.step(pool.affine_select(out=ssum[:], in_=ssum[:], compare_op=ALU.is_ge, fill=0.0, base=0,
                                             pattern=[[128, UN], [-NS, 128]], channel_multiplier=1))
                made.step(pool.affine_select(out=ssum[:], in_=ssum[:], compare_op=ALU.is_ge, fill=0.0, base=NS - 1,
                                             pattern=[[-128, UN], [NS, 128]], channel_multiplier=-1))
                with pool.Fori(0, NG) as q:
                    for n in range(per_q):
                        r = n % R
                        wait_alone(pool, core, summed, q * per_q + max(n + 1 - R, 0))
                        wait_alone(pool, core, scanned, q * per_q + (n + 1))
                        pool.tensor_tensor(ch[r][:], hs[r][:], ssm.ct[:, bass.ds(q * GT, GT)],
                                           ALU.mult).then_inc(weighed, 1)

            @block.tensor
            def _(pe):
                pe.wait_ge(sel_made, 5)
                LAG = 3

                def sum_states(q, n):
                    c, g = divmod(n, UN)
                    pe.wait_ge(weighed, q * per_q + (n + 1))
                    if g == 0:
                        pe.wait_ge(y_out, q * KC)
                    ins = pe.matmul(py[c][:, 0:GT], ssum[:, g, :], ch[n % R][:], start=g == 0, stop=g == UN - 1)
                    ins.then_inc(summed, 1)

                def turn(q, c):
                    pe.wait_ge(y_out, q * KC + (c + 1))
                    pe.wait_ge(added, q * KC)
                    for j in range(GB):
                        last = pe.transpose(pt[c][0:L, j, :], yt[c][:, j * L:(j + 1) * L], core.ident[:])
                    last.then_inc(turned, 1)

                with pe.Fori(0, NG) as q:
                    cols = bass.ds(q * GT, GT)
                    for n in range(per_q):
                        c, g = divmod(n, UN)
                        if n >= 2:
                            pe.wait_ge(decay, q * per_q + (n - 1))
                            pe.wait_ge(drive, q * per_q + (n - 1))
                        else:
                            pe.wait_ge(decay, q * per_q)
                            pe.wait_ge(drive, q * per_q)
                        pe.matmul(pdt[n % 2][:, 0:GT], sel[:, g, :], ssm.dt_hi[:, c, cols], start=True, stop=False)
                        pe.matmul(pdt[n % 2][:, 0:GT], sel[:, g, :], ssm.dt_lo[:, c, cols], start=False,
                                  stop=True).then_inc(dt_ready, 1)
                        pe.matmul(pdx[n % 2][:, 0:GT], sel[:, g, :], ssm.dx_hi[:, c, cols], start=True, stop=False)
                        pe.matmul(pdx[n % 2][:, 0:GT], sel[:, g, :], ssm.dx_lo[:, c, cols], start=False,
                                  stop=True).then_inc(dx_ready, 1)
                        if n >= LAG:
                            sum_states(q, n - LAG)
                        if n == UN + LAG + 3:
                            turn(q, 0)
                    for n in range(per_q - LAG, per_q):
                        sum_states(q, n)
                    turn(q, 1)

            @block.scalar
            def _(act):
                act.wait_ge(zeroed, R)

                def copy_out(q, c):
                    act.wait_ge(summed, q * per_q + UN * (c + 1))
                    act.wait_ge(turned, q * KC)
                    act.activation(yt[c][:], py[c][:, 0:GT], ACT.Copy).then_inc(y_out, 1)

                with act.Fori(0, NG) as q:
                    for n in range(per_q):
                        c, g = divmod(n, UN)
                        act.wait_ge(dt_ready, q * per_q + (n + 1))
                        if n >= R:
                            act.wait_ge(scanned, q * per_q + (n + 1 - R))
                        else:
                            act.wait_ge(scanned, q * per_q)
                        act.activation(abar[n % R][:, :, 1:L],
                                       pdt[n % 2][:, 0:GT].rearrange("p (b t) -> p b t", t=L)[:, :, 1:L],
                                       ACT.Exp, scale=ssm.a[:, n:n + 1]).then_inc(decay, 1)
                        if n == UN + 4:
                            copy_out(q, 0)
                    copy_out(q, 1)

            @block.vector
            def _(dve):
                for r in range(R):
                    dve.memset(abar[r][:, :, 0:1], 0.0).then_inc(zeroed, 1)

                def add_y(q, c):
                    dve.wait_ge(turned, q * KC + (c + 1))
                    b = bass.ds(q * GB, GB)
                    half = slice(c * 128, (c + 1) * 128)
                    dve.tensor_tensor(core.h[:, b, half], core.h[:, b, half], pt[c][0:L, :, :],
                                      ALU.add).then_inc(added, 1)

                with dve.Fori(0, NG) as q:
                    for n in range(per_q):
                        r = n % R
                        dve.wait_ge(dx_ready, q * per_q + (n + 1))
                        if n >= R:
                            dve.wait_ge(scanned, q * per_q + (n + 1 - R))
                        else:
                            dve.wait_ge(scanned, q * per_q)
                        dve.tensor_tensor(bx[r][:], pdx[n % 2][:, 0:GT], ssm.bt[:, bass.ds(q * GT, GT)],
                                          ALU.mult).then_inc(drive, 1)
                        dve.wait_ge(drive, q * per_q + (n + 1))
                        dve.wait_ge(decay, q * per_q + (n + 1))
                        if n >= R:
                            dve.wait_ge(weighed, q * per_q + (n + 1 - R))
                        else:
                            dve.wait_ge(weighed, q * per_q)
                        dve.tensor_tensor_scan(hs[r][:], abar[r][:].rearrange("p b t -> p (b t)"), bx[r][:], 0.0,
                                               ALU.mult, ALU.add).then_inc(scanned, 1)
                        if n == UN + 8:
                            add_y(q, 0)
                    add_y(q, 1)


def ring(eng, n, body):
    off = n % 2
    if off:
        body(0, 0, 0)
    with eng.Fori(0, n // 2) as i:
        for u in range(2):
            body(i * 2 + (off + u), (off + u) % 2, i + (off + u) // 2)


class At:

    def __init__(self, i, c):
        self.i, self.c, self.j = i, c, i * 4 + c

    def of(self, depth):
        return self.c % depth, self.i * (4 // depth) + self.c // depth

    def __add__(self, k):
        return At(self.i, self.c + k)


def steps(eng, n, body):
    for c in range(n % 4):
        body(At(0, c))
    with eng.Fori(0, n // 4) as i:
        for c in range(4):
            body(At(i, n % 4 + c))


class Moe:

    def __init__(self, name, experts, picks, in_chunks, hid_chunks, gelu, mult, norm):
        self.name, self.E, self.K, self.NF, self.FH = name, experts, picks, in_chunks, hid_chunks
        self.gelu, self.mult, self.norm = gelu, mult, norm
        self.blocks = (picks * T + 127 * experts) // 128
        self.blocks += 1 - self.blocks % 2
        self.halves = 2 if KC * in_chunks * 128 > 1024 else 1
        self.steps = experts * self.halves

    def buffers(self, nc, ctx):
        def sb(name, shape, dt):
            return ctx.enter_context(nc.sbuf_tensor(f"{self.name}_{name}", shape, dt))

        self.w1_hi, self.w1_lo = (sb(n, [128, self.E, KC, self.NF * 128], F16) for n in ("w1_hi", "w1_lo"))
        self.w2_hi, self.w2_lo = (sb(n, [128, self.E, self.FH, D], F16) for n in ("w2_hi", "w2_lo"))
        self.b1 = sb("b1", [128, self.E, self.NF], F32)
        self.weight, self.slot = sb("weight", [L, NB, self.K], F32), sb("slot", [L, NB, self.K], U32)
        self.ids, self.expert = sb("ids", [128, self.blocks], U32), sb("expert", [1, self.blocks], I32)
        self.rows = nc.dram_tensor(f"{self.name}_rows", [T, D], F32, kind="Internal").ap()
        self.out = nc.dram_tensor(f"{self.name}_out", [self.blocks * 128, D], F32, kind="Internal").ap()


class MoeWeights:

    def __init__(self, st, m, d, depth):
        self.m, self.d, self.depth = m, d, depth
        self.n1 = KC * m.NF * 128
        self.buf = [st.sb(f"wbuf{p}", [128, (self.n1 + m.FH * D) // m.halves]) for p in range(depth)]
        self.landed, self.hi_done, self.lo_done = ([st.sem(f"w_{n}{p}") for p in range(depth)]
                                                   for n in ("landed", "hi", "lo"))
        self.small, self.ready = st.sem("small_landed"), st.sem("mult_ready")
        self.w1h, self.w1l, self.w2h, self.w2l = (w[:].rearrange("p e k n -> p e (k n)")
                                                  for w in (m.w1_hi, m.w1_lo, m.w2_hi, m.w2_lo))
        if m.mult:
            self.gain = st.sb("gain", [128, m.E, m.FH])

    def parts(self, j, p, before, w1, w2):
        m, n1, buf = self.m, self.n1, self.buf[p % self.depth]
        if m.halves == 2:
            return [((w1 if p == 0 else w2)[:, bass.ds(before, 1), :], buf[:], None)]
        e = bass.ds(j, 1)
        return [(w1[:, e, :], buf[:, 0:n1], None)] + [
            (w2[:, e, f * D:(f + 1) * D], buf[:, n1 + f * D:n1 + (f + 1) * D],
             self.gain[:, e, f:f + 1].rearrange("p a b -> p (a b)")) for f in range(m.FH)]

    def uses(self, j, p, before):
        return (p, before) if self.depth == 2 else (0, j)

    def load_small(self, sp):
        m, d = self.m, self.d
        if m.mult:
            sp.dma_start(self.gain[:].rearrange("p e f -> p (e f)"), d[m.name + "mult"]).then_inc(self.small, 16)
        sp.dma_start(m.b1[:], d[m.name + "b1"]).then_inc(self.small, 16)

    def load(self, sp, j, p, before):
        b, uses = self.uses(j, p, before)
        sp.wait_ge(self.lo_done[b], uses)
        sp.dma_start(self.buf[b][:].rearrange("p (a n) -> p a n", a=1),
                     self.d[self.m.name + "w"][:, bass.ds(j, 1), :]).then_inc(self.landed[b], 16)

    def high(self, act, j, p, before):
        b, uses = self.uses(j, p, before)
        act.wait_ge(self.landed[b], uses * 16 + 16)
        for dst, src, g in self.parts(j, p, before, self.w1h, self.w2h):
            ins = act.activation(dst, src.rearrange("p (a n) -> p a n", a=1), ACT.Copy if g is None
                                 else ACT.Identity, scale=WS if g is None else g)
        ins.then_inc(self.hi_done[b], 1)

    def scale_small(self, dve):
        m = self.m
        dve.wait_ge(self.small, 32 if m.mult else 16)
        if m.mult:
            dve.tensor_scalar(self.gain[:], self.gain[:], WS, None, ALU.mult).then_inc(self.ready, 1)
            dve.tensor_scalar(m.b1[:, :, 0:m.NF // 2], m.b1[:, :, 0:m.NF // 2], WS, None,
                              ALU.mult).then_inc(self.ready, 1)
        else:
            dve.tensor_scalar(m.b1[:], m.b1[:], WS, None, ALU.mult).then_inc(self.ready, 2)
        dve.wait_ge(self.ready, 2)

    def low(self, dve, j, p, before):
        b, uses = self.uses(j, p, before)
        dve.wait_ge(self.hi_done[b], uses + 1)
        for (dst, src, g), (hi, _, _) in zip(self.parts(j, p, before, self.w1l, self.w2l),
                                             self.parts(j, p, before, self.w1h, self.w2h)):
            ins = dve.scalar_tensor_tensor(dst, src.rearrange("p (a n) -> p a n", a=1),
                                           WS if g is None else g, hi, ALU.mult, ALU.subtract)
        ins.then_inc(self.lo_done[b], 1)


def stage_moe_weights(nc, core, m, d):
    with Stage(nc, m.name + "w") as st:
        mw = MoeWeights(st, m, d, 2)
        with nc.Block() as block:
            @block.sync
            def _(sp):
                mw.load_small(sp)
                ring(sp, m.steps, lambda j, p, before: mw.load(sp, j, p, before))

            @block.scalar
            def _(act):
                act.wait_ge(mw.ready, 1)
                ring(act, m.steps, lambda j, p, before: mw.high(act, j, p, before))

            @block.vector
            def _(dve):
                mw.scale_small(dve)
                ring(dve, m.steps, lambda j, p, before: mw.low(dve, j, p, before))


def stage_route(nc, core, m, d):
    E, K, N = m.E, m.K, m.blocks
    with Stage(nc, m.name + "r") as st:
        wr_hi, wr_lo = st.sb("wr_hi", [128, KC * E], F16), st.sb("wr_lo", [128, KC * E], F16)
        b2_hi, b2_lo = st.sb("b2_hi", [E, D], F16), st.sb("b2_lo", [E, D], F16)
        logit, prob = st.sb("logit", [L, NB, E]), st.sb("prob", [L, NB, E])
        top, rsum = st.sb("top", [L, NB]), st.sb("rsum", [L, NB])
        vals, idx, idxf = st.sb("vals", [L, NB, 8]), st.sb("idx", [L, NB, 8], U32), st.sb("idxf", [L, NB, 8])
        iota_e = st.sb("iota_e", [L, E])
        iota_n, iota_p, token = st.sb("iota_n", [L, N]), st.sb("iota_p", [L, 128]), st.sb("token", [L, NB])
        below = st.sb("below", [L, L], F16)
        hot = [st.sb(f"hot{k}", [L, NB, E]) for k in range(K)]
        comb, comb_hi, comb_lo = st.sb("comb", [L, NB, E]), st.sb("ch", [E, T], F16), st.sb("cl", [E, T], F16)
        part = st.sb("part", [L, NB, E])
        many = st.sb("many", [L, NB, E], F16)
        tot, run, keep = st.sb("tot", [L, E, NB]), st.sb("run", [L, E, NB]), st.sb("keep", [L, E, NB])
        cnt, cnt_i, nblk = st.sb("cnt", [L, E]), st.sb("cnt_i", [L, E], I32), st.sb("nblk", [L, E])
        bend, base, one_e = st.sb("bend", [L, E]), st.sb("base", [L, E]), st.sb("one_e", [L, E])
        rank = st.sb("rank", [L, NB, E])
        slotf = st.sb("slotf", [L, NB, K])
        lane_i, block_i = st.sb("lane_i", [L, NB, K], I32), st.sb("block_i", [L, NB, K], I32)
        lane, blockf = st.sb("lane", [L, NB, K]), st.sb("blockf", [L, NB, K])
        past = st.sb("past", [1, N, E])
        owner = st.sb("owner", [1, N])
        R = 4
        lane_hot = [st.sb(f"lane_hot{r}", [L, 128], F16) for r in range(R)]
        block_hot = [st.sb(f"block_hot{r}", [L, N], F16) for r in range(R)]
        plog, ppos, ptot = (st.ps(n, [L, NB, E]) for n in ("plog", "ppos", "ptot"))
        pids = st.ps("pids", [128, N])
        pcomb = st.ps("pcomb", [E, 512])
        pbias = [st.ps(f"pbias{u}", [L, D]) for u in range(2)]
        (log_ready, log_out, shifted, exped, masks, hot_ready, counts, hots, used, ids_ready, comb_done, turned,
         comb_high, comb_split, consts) = (st.sem(n) for n in (
             "log_ready", "log_out", "shifted", "exped", "masks", "hot_ready", "counts", "hots", "used", "ids_ready",
             "comb_done", "turned", "comb_high", "comb_split", "consts"))
        bias_ready, bias_free = ([st.sem(f"{n}{u}") for u in range(2)] for n in ("bias_ready", "bias_free"))
        chain_sem = st.sem("chain")
        w_sync, w_act, w_dve, (w_ready, w_n) = split_weights(st, core, [
            ("wr", d[m.name + "router"], wr_hi[:], wr_lo[:]),
            ("b2", d[m.name + "b2"], b2_hi[:], b2_lo[:]),
        ])
        with nc.Block() as block:
            @block.sync
            def _(sp):
                w_sync(sp)

            @block.gpsimd
            def _(pool):
                made = Chain(pool, masks)
                made.step(pool.memset(below[:], 1.0))
                made.step(pool.affine_select(out=below[:], in_=below[:], compare_op=ALU.is_ge, fill=0.0, base=-1,
                                             pattern=[[1, L]], channel_multiplier=-1))
                imprecise = dict(allow_small_or_imprecise_dtypes=True)
                made.step(pool.iota(iota_e[:], pattern=[[1, E]], base=0, channel_multiplier=0, **imprecise))
                made.step(pool.iota(iota_n[:], pattern=[[1, N]], base=0, channel_multiplier=0, **imprecise))
                made.step(pool.iota(iota_p[:], pattern=[[1, 128]], base=0, channel_multiplier=0, **imprecise))
                made.step(pool.iota(token[:], pattern=[[L, NB]], base=0, channel_multiplier=1, **imprecise))
                made.step(pool.memset(keep[:], 1.0))
                made.step(pool.memset(keep[:, :, 0:1], 0.0))
                made.step(pool.memset(one_e[:], 1.0))

            @block.tensor
            def _(pe):
                pe.wait_ge(w_ready, w_n)
                with pe.Fori(0, NB) as b:
                    cols = bass.ds(b * L, L)
                    for k in range(KC):
                        last = mm3(pe, plog[:, bass.ds(b, 1), :], core.xt_hi[:, k, cols], core.xt_lo[:, k, cols],
                                   wr_hi[:, k * E:(k + 1) * E].rearrange("p (a n) -> p a n", a=1),
                                   wr_lo[:, k * E:(k + 1) * E].rearrange("p (a n) -> p a n", a=1), k == 0,
                                   k == KC - 1)
                    last.then_inc(log_ready, 1)
                pe.wait_ge(hot_ready, 1)
                flat = many[:].rearrange("p b e -> p (b e)")
                pe.matmul(ppos[:].rearrange("p b e -> p (b e)"), below[:], flat, start=True, stop=True)
                pe.matmul(ptot[:].rearrange("p b e -> p (b e)"), core.ones16[0:L, 0:L], flat, start=True,
                          stop=True).then_inc(counts, 1)
                for n in range(NB * K):
                    pe.wait_ge(hots, n + 1)
                    pe.matmul(pids[:], lane_hot[n % R][:], block_hot[n % R][:], start=n == 0,
                              stop=n == NB * K - 1).then_inc(used, 1)
                pe.wait_ge(comb_done, 1)
                for q in range(NG):
                    if q:
                        pe.wait_ge(comb_split, q)
                    for j in range(GB):
                        last = pe.transpose(pcomb[:, j * L:(j + 1) * L], comb[:, q * GB + j, :],
                                            core.ident[0:L, 0:L])
                    last.then_inc(turned, 1)
                pe.wait_ge(comb_split, NG)

                def bias(j, p, before):
                    pe.wait_ge(bias_free[p], before)
                    cols = bass.ds(j * L, L)
                    mm3(pe, pbias[p][:], comb_hi[:, cols], comb_lo[:, cols], b2_hi[:], b2_lo[:], True,
                        True).then_inc(bias_ready[p], 1)
                ring(pe, NB, bias)

            @block.scalar
            def _(act):
                w_act(act)
                act.wait_ge(log_ready, NB)
                act.activation(logit[:], plog[:], ACT.Copy, scale=1.0 / WS).then_inc(log_out, 1)
                act.wait_ge(shifted, 1)
                act.activation(prob[:], part[:], ACT.Exp).then_inc(exped, 1)
                for q in range(NG):
                    act.wait_ge(turned, q + 1)
                    act.activation(comb_hi[:, q * GT:(q + 1) * GT], pcomb[:, 0:GT], ACT.Copy).then_inc(comb_high, 1)

            @block.vector
            def _(dve):
                w_dve(dve)
                dve.wait_ge(masks, 9)
                ch = Chain(dve, chain_sem)
                over_e = lambda a: a.unsqueeze(2).to_broadcast([L, NB, E])
                dve.wait_ge(log_out, 1)
                ch.step(dve.tensor_reduce(out=top[:], in_=logit[:], op=ALU.max, axis=AX.X))
                dve.tensor_tensor(part[:], logit[:], over_e(top[:]), ALU.subtract).then_inc(shifted, 1)
                dve.wait_ge(exped, 1)
                ch.step(dve.tensor_reduce(out=rsum[:], in_=prob[:], op=ALU.add, axis=AX.X))
                ch.step(dve.reciprocal(rsum[:], rsum[:]))
                ch.step(dve.tensor_tensor(prob[:], prob[:], over_e(rsum[:]), ALU.mult))
                for b in range(NB):
                    ins = dve.max(vals[:, b, :], prob[:, b, :])
                ch.step(ins)
                for b in range(NB):
                    ins = dve.max_index(idx[:, b, :], vals[:, b, :], prob[:, b, :])
                ch.step(ins)
                ch.step(dve.tensor_copy(idxf[:], idx[:]))
                for k in range(K):
                    ins = dve.tensor_tensor(hot[k][:], iota_e[:].unsqueeze(1).to_broadcast([L, NB, E]),
                                            over_e(idxf[:, :, k]), ALU.is_equal)
                ch.step(ins)
                if K == 1:
                    dve.tensor_copy(many[:], hot[0][:]).then_inc(hot_ready, 1)
                else:
                    ch.step(dve.tensor_tensor(part[:], hot[0][:], hot[1][:], ALU.add))
                    dve.tensor_tensor(many[:], part[:], hot[2][:], ALU.add).then_inc(hot_ready, 1)
                if m.norm:
                    ch.step(dve.tensor_tensor(rsum[:], vals[:, :, 0], vals[:, :, 1], ALU.add))
                    ch.step(dve.tensor_tensor(rsum[:], rsum[:], vals[:, :, 2], ALU.add))
                    ch.step(dve.tensor_scalar(rsum[:], rsum[:], 1e-20, None, ALU.add))
                    ch.step(dve.reciprocal(rsum[:], rsum[:]))
                    ch.step(dve.tensor_tensor(m.weight[:], vals[:, :, 0:K],
                                              rsum[:].unsqueeze(2).to_broadcast([L, NB, K]), ALU.mult))
                else:
                    ch.step(dve.tensor_copy(m.weight[:], vals[:, :, 0:K]))
                ch.step(dve.tensor_tensor(comb[:], hot[0][:], over_e(m.weight[:, :, 0]), ALU.mult))
                for k in range(1, K):
                    ch.step(dve.tensor_tensor(rank[:], hot[k][:], over_e(m.weight[:, :, k]), ALU.mult))
                    ch.step(dve.tensor_tensor(comb[:], comb[:], rank[:], ALU.add))
                dve.sem_inc(comb_done, 1)
                dve.wait_ge(counts, 1)
                ch.step(dve.tensor_copy(tot[:], ptot[:].rearrange("p b e -> p e b")))
                ch.step(dve.tensor_tensor_scan(run[:].rearrange("p e b -> p (e b)"),
                                               keep[:].rearrange("p e b -> p (e b)"),
                                               tot[:].rearrange("p e b -> p (e b)"), 0.0, ALU.mult, ALU.add))
                ch.step(dve.tensor_scalar(cnt_i[:], run[:, :, NB - 1], 127.0, None, ALU.add))
                ch.step(dve.tensor_scalar(cnt_i[:], cnt_i[:], 7, None, ALU.logical_shift_right))
                ch.step(dve.tensor_copy(nblk[:], cnt_i[:]))
                ch.step(dve.tensor_tensor_scan(bend[:], one_e[:], nblk[:], 0.0, ALU.mult, ALU.add))
                ch.step(dve.tensor_tensor(base[:], bend[:], nblk[:], ALU.subtract))
                ch.step(dve.tensor_tensor(run[:], run[:], tot[:], ALU.subtract))
                ch.step(dve.scalar_tensor_tensor(run[:], base[:].unsqueeze(2).to_broadcast([L, E, NB]), 128.0, run[:],
                                                 ALU.mult, ALU.add))
                ch.step(dve.tensor_tensor(rank[:], ppos[:], run[:].rearrange("p e b -> p b e"), ALU.add))
                for k in range(K):
                    ch.step(dve.tensor_tensor(part[:], hot[k][:], rank[:], ALU.mult))
                    ch.step(dve.tensor_reduce(out=slotf[:, :, k], in_=part[:], op=ALU.add, axis=AX.X))
                dve.tensor_copy(m.slot[:], slotf[:])
                ch.step(dve.tensor_copy(block_i[:], slotf[:]))
                dve.tensor_scalar(lane_i[:], block_i[:], 127, None, ALU.bitwise_and)
                ch.step(dve.tensor_scalar(block_i[:], block_i[:], 7, None, ALU.logical_shift_right))
                dve.tensor_copy(lane[:], lane_i[:])
                ch.step(dve.tensor_copy(blockf[:], block_i[:]))
                for b in range(NB):
                    for k in range(K):
                        n = b * K + k
                        if n >= R:
                            dve.wait_ge(used, n - R + 1)
                        dve.tensor_scalar(lane_hot[n % R][:], iota_p[:], lane[:, b, k:k + 1], None, ALU.is_equal)
                        dve.tensor_scalar(block_hot[n % R][:], iota_n[:], blockf[:, b, k:k + 1], token[:, b:b + 1],
                                          ALU.is_equal, ALU.mult).then_inc(hots, 1)
                ch.step(dve.tensor_tensor(past[:], bend[0:1, :].unsqueeze(1).to_broadcast([1, N, E]),
                                          iota_n[0:1, :].unsqueeze(2).to_broadcast([1, N, E]), ALU.is_le))
                ch.step(dve.tensor_reduce(out=owner[:], in_=past[:], op=ALU.add, axis=AX.X))
                ch.step(dve.tensor_scalar(m.expert[:], owner[:], E - 1.0, None, ALU.min))
                dve.wait_ge(used, NB * K)
                ch.step(dve.tensor_copy(m.ids[:], pids[:]))
                for q in range(NG):
                    dve.wait_ge(comb_high, q + 1)
                    dve.tensor_tensor(comb_lo[:, q * GT:(q + 1) * GT], pcomb[:, 0:GT],
                                      comb_hi[:, q * GT:(q + 1) * GT], ALU.subtract).then_inc(comb_split, 1)

                def add(j, p, before):
                    dve.wait_ge(bias_ready[p], before + 1)
                    b = bass.ds(j, 1)
                    dve.scalar_tensor_tensor(core.h[:, b, :], pbias[p][:].unsqueeze(1), 1.0 / WS, core.h[:, b, :],
                                             ALU.mult, ALU.add).then_inc(bias_free[p], 1)
                ring(dve, NB, add)


def stage_experts(nc, core, m):
    N, NF, FH = m.blocks, m.NF, m.FH
    with Stage(nc, m.name + "x") as st:
        two, four = range(2), range(4)
        idx = [st.sb(f"idx{p}", [128, 1], U32) for p in four]
        xg = [st.sb(f"xg{p}", [128, D]) for p in four]
        xb = [st.sb(f"xb{p}", [128, 2 * KC, 128], F16) for p in two]
        b1 = [st.sb(f"b1{p}", [128, 1, NF]) for p in two]
        gate = [st.sb(f"gate{p}", [128, FH, 128]) for p in two] if m.gelu else None
        act32 = [st.sb(f"a{p}", [128, FH, 128]) for p in two]
        a_hi, a_lo = ([st.sb(f"{n}{p}", [128, FH, 128], F16) for p in two] for n in ("ah", "al"))
        yo = [st.sb(f"yo{p}", [128, D]) for p in two]
        pt = [st.ps(f"pt{p}", [128, 1024], F16) for p in two]
        ph = [st.ps(f"ph{p}", [128, NF, 128]) for p in two]
        py = [st.ps(f"py{p}", [128, 512]) for p in two]
        idx_ready, gathered, turned = ([st.sem(f"{n}{p}") for p in four] for n in ("idx_ready", "gathered", "turned"))
        xb_ready, h_ready, b1_ready, gate_ready, a_ready, hi_ready, lo_ready, y_ready, y_out, stored = (
            [st.sem(f"{n}{p}") for p in two] for n in (
                "xb_ready", "h_ready", "b1_ready", "gate_ready", "a_ready", "hi_ready", "lo_ready", "y_ready",
                "y_out", "stored"))
        with nc.Block() as block:
            @block.gpsimd
            def _(pool):
                def gather(at):
                    p, before = at.of(4)
                    wait_alone(pool, core, turned[p], before)
                    pool.tensor_copy(idx[p][:], m.ids[:, bass.ds(at.j, 1)]).then_inc(idx_ready[p], 1)
                    wait_alone(pool, core, idx_ready[p], before + 1)
                    pool.indirect_dma_start(xg[p][:], None, m.rows[:, :],
                                            bass.IndirectOffsetOnAxis(ap=idx[p][:, 0:1], axis=0)
                                            ).then_inc(gathered[p], 16)

                def bias(at):
                    p, before = at.of(2)
                    e = pool.value_load(m.expert[0:1, bass.ds(at.j, 1)], min_val=0, max_val=m.E - 1)
                    wait_alone(pool, core, lo_ready[p], before)
                    pool.tensor_copy(b1[p][:], m.b1[:, bass.ds(e, 1), :]).then_inc(b1_ready[p], 1)

                def step(at):
                    gather(at + 2)
                    bias(at)

                gather(At(0, 0))
                gather(At(0, 1))
                steps(pool, N - 2, step)
                bias(At(0, N - 2))
                bias(At(0, N - 1))

            @block.tensor
            def _(pe):
                def expert(at):
                    return pe.value_load(m.expert[0:1, bass.ds(at.j, 1)], min_val=0, max_val=m.E - 1)

                def turn(at):
                    (p, before), (q, uses) = at.of(2), at.of(4)
                    pe.wait_ge(gathered[q], uses * 16 + 16)
                    pe.wait_ge(xb_ready[p], before)
                    for c in range(2 * KC):
                        last = pe.transpose(pt[p][:, c * 128:(c + 1) * 128],
                                            xg[q][:].bitcast(F16)[:, c * 128:(c + 1) * 128], core.ident16[:])
                    last.then_inc(turned[q], 1)

                def first(at):
                    p, before = at.of(2)
                    e = expert(at)
                    pe.wait_ge(xb_ready[p], before + 1)
                    pe.wait_ge(lo_ready[p], before)
                    for f in range(NF):
                        for k in range(KC):
                            w = [w[:, bass.ds(e, 1), k, f * 128:(f + 1) * 128].rearrange("p a n -> p (a n)")
                                 for w in (m.w1_hi, m.w1_lo)]
                            last = mm3(pe, ph[p][:, f, :], w[0], w[1], xb[p][:, k, :], xb[p][:, KC + k, :],
                                       k == 0, k == KC - 1)
                    last.then_inc(h_ready[p], 1)
                    return e

                def second(at, e):
                    p, before = at.of(2)
                    pe.wait_ge(y_out[p], before)
                    pe.wait_ge(hi_ready[p], before + 1)
                    pe.wait_ge(lo_ready[p], before + 1)
                    for f in range(FH):
                        w = [w[:, bass.ds(e, 1), f, :].rearrange("p a n -> p (a n)") for w in (m.w2_hi, m.w2_lo)]
                        last = mm3(pe, py[p][:, 0:D], a_hi[p][:, f, :], a_lo[p][:, f, :], w[0], w[1],
                                   f == 0, f == FH - 1)
                    last.then_inc(y_ready[p], 1)

                def step(at, e):
                    turn(at + 2)
                    ahead = first(at + 1)
                    second(at, e)
                    return ahead

                turn(At(0, 0))
                turn(At(0, 1))
                e = first(At(0, 0))
                for c in range((N - 2) % 4):
                    e = step(At(0, c), e)
                with pe.Fori(0, (N - 2) // 4) as i:
                    e = expert(At(i, (N - 2) % 4))
                    for c in range(4):
                        e = step(At(i, (N - 2) % 4 + c), e)
                e = expert(At(0, N - 2))
                ahead = first(At(0, N - 1))
                second(At(0, N - 2), e)
                second(At(0, N - 1), ahead)

            @block.scalar
            def _(act):
                def take_tokens(at):
                    (p, before), (q, uses) = at.of(2), at.of(4)
                    act.wait_ge(turned[q], uses + 1)
                    act.wait_ge(h_ready[p], before)
                    act.activation(xb[p][:].rearrange("p c n -> p (c n)"), pt[p][:, 0:2 * KC * 128],
                                   ACT.Copy).then_inc(xb_ready[p], 1)

                def hidden(at):
                    p, before = at.of(2)
                    act.wait_ge(h_ready[p], before + 1)
                    act.wait_ge(b1_ready[p], before + 1)
                    if m.gelu:
                        act.wait_ge(a_ready[p], before)
                        for f in range(FH):
                            ins = act.activation(gate[p][:, f, :], ph[p][:, FH + f, :], ACT.Gelu,
                                                 bias=b1[p][:, 0, FH + f:FH + f + 1], scale=1.0 / WS)
                        ins.then_inc(gate_ready[p], 1)
                        act.wait_ge(a_ready[p], before + 1)
                        act.wait_ge(y_ready[p], before)
                        act.activation(a_hi[p][:], act32[p][:], ACT.Copy).then_inc(hi_ready[p], 1)
                    else:
                        act.wait_ge(y_ready[p], before)
                        for f in range(FH):
                            ins = act.activation(a_hi[p][:, f, :], ph[p][:, f, :], ACT.Relu,
                                                 bias=b1[p][:, 0, f:f + 1])
                        ins.then_inc(hi_ready[p], 1)

                def step(at):
                    take_tokens(at + 2)
                    hidden(at + 1)

                take_tokens(At(0, 0))
                take_tokens(At(0, 1))
                hidden(At(0, 0))
                steps(act, N - 2, step)
                hidden(At(0, N - 1))

            @block.vector
            def _(dve):
                def hidden(at):
                    p, before = at.of(2)
                    if m.gelu:
                        dve.wait_ge(gate_ready[p], before + 1)
                        dve.wait_ge(hi_ready[p], before)
                        for f in range(FH):
                            ins = dve.scalar_tensor_tensor(act32[p][:, f, :], ph[p][:, f, :], b1[p][:, 0, f:f + 1],
                                                           gate[p][:, f, :], ALU.add, ALU.mult)
                        ins.then_inc(a_ready[p], 1)
                    else:
                        dve.wait_ge(hi_ready[p], before + 1)
                        for f in range(FH):
                            ins = dve.tensor_scalar(act32[p][:, f, :], ph[p][:, f, :], b1[p][:, 0, f:f + 1], 0.0,
                                                    ALU.add, ALU.max)
                        ins.then_inc(a_ready[p], 1)
                        dve.wait_ge(a_ready[p], before + 1)
                    dve.wait_ge(hi_ready[p], before + 1)
                    dve.wait_ge(y_ready[p], before)
                    dve.tensor_tensor(a_lo[p][:], act32[p][:], a_hi[p][:], ALU.subtract).then_inc(lo_ready[p], 1)

                def output(at):
                    p, before = at.of(2)
                    dve.wait_ge(y_ready[p], before + 1)
                    dve.wait_ge(stored[p], before * 16)
                    dve.tensor_scalar(yo[p][:], py[p][:, 0:D], 1.0 / (WS * WS), None,
                                      ALU.mult).then_inc(y_out[p], 1)

                def step(at):
                    hidden(at + 1)
                    output(at)

                hidden(At(0, 0))
                steps(dve, N - 1, step)
                output(At(0, N - 1))

            @block.sync
            def _(sp):
                def store(at):
                    p, before = at.of(2)
                    sp.wait_ge(y_out[p], before + 1)
                    sp.dma_start(m.out[bass.ds(at.j * 128, 128), :], yo[p][:]).then_inc(stored[p], 16)
                steps(sp, N, store)
                sp.wait_ge(stored[0], 16 * ((N + 1) // 2))
                sp.wait_ge(stored[1], 16 * (N // 2))


def stage_combine(nc, core, m):
    K = m.K
    with Stage(nc, m.name + "c") as st:
        two = range(2)
        idx = [st.sb(f"idx{p}", [L, K], U32) for p in two]
        got = [[st.sb(f"got{p}{k}", [L, 1, D]) for k in range(K)] for p in two]
        gathered = [st.sem(f"gathered{p}") for p in two]
        added = [st.sem(f"added{p}") for p in two]
        idx_ready = [st.sem(f"idx_ready{p}") for p in two]
        chain_sem = st.sem("chain")
        with nc.Block() as block:
            @block.gpsimd
            def _(pool):
                def step(j, p, before):
                    wait_alone(pool, core, added[p], before)
                    pool.tensor_copy(idx[p][:].unsqueeze(1), m.slot[:, bass.ds(j, 1), :]).then_inc(idx_ready[p], 1)
                    wait_alone(pool, core, idx_ready[p], before + 1)
                    for k in range(K):
                        pool.indirect_dma_start(got[p][k][:].rearrange("p a n -> p (a n)"), None, m.out[:, :],
                                                bass.IndirectOffsetOnAxis(ap=idx[p][:, k:k + 1], axis=0)
                                                ).then_inc(gathered[p], 16)
                ring(pool, NB, step)

            @block.vector
            def _(dve):
                def step(j, p, before):
                    dve.wait_ge(gathered[p], before * (16 * K) + 16 * K)
                    b = bass.ds(j, 1)
                    for k in range(K):
                        ins = dve.scalar_tensor_tensor(core.h[:, b, :], got[p][k][:], m.weight[:, b, k:k + 1]
                                                       .rearrange("p a b -> p (a b)"), core.h[:, b, :],
                                                       ALU.mult, ALU.add)
                        if k < K - 1:
                            ins.then_inc(chain_sem, 1)
                            dve.wait_ge(chain_sem, j * (K - 1) + (k + 1))
                    ins.then_inc(added[p], 1)
                ring(dve, NB, step)



def stage_shared(nc, core, d):
    FC = 4
    with Stage(nc, "shared") as st:
        s1_hi, s1_lo = (st.sb(n, [128, KC, 2 * FC * 128], F16) for n in ("s1_hi", "s1_lo"))
        s2_hi, s2_lo = (st.sb(n, [128, FC, D], F16) for n in ("s2_hi", "s2_lo"))
        s2_f, gain, b1 = st.sb("s2_f", [128, FC, D]), st.sb("gain", [128, FC]), st.sb("b1", [128, 2 * FC])
        b2_hi, b2_lo = st.sb("b2_hi", [1, D], F16), st.sb("b2_lo", [1, D], F16)
        b2_scaled = st.sb("b2_scaled", [1, D])
        two = range(2)
        gate, a32 = ([st.sb(f"{n}{p}", [128, GT]) for p in two] for n in ("gate", "a32"))
        a_hi, a_lo = (st.sb(n, [128, FC, GT], F16) for n in ("a_hi", "a_lo"))
        px, pg = ([st.ps(f"{n}{p}", [128, 512]) for p in two] for n in ("px", "pg"))
        po = [st.ps(f"po{p}", [L, D]) for p in two]
        small, scaled, gained = st.sem("small"), st.sem("scaled"), st.sem("gained")
        x_ready, g_ready, gated, a_ready, hi_ready, lo_ready = (st.sem(n) for n in (
            "x_ready", "g_ready", "gated", "a_ready", "hi_ready", "lo_ready"))
        o_ready, o_free = ([st.sem(f"{n}{p}") for p in two] for n in ("o_ready", "o_free"))
        flat = lambda t: t[:].rearrange("p a n -> p (a n)")
        w_sync, w_act, w_dve, (w_ready, w_n) = split_weights(st, core, [
            ("s1", d["s1"], flat(s1_hi), flat(s1_lo)),
        ])
        with nc.Block() as block:
            @block.sync
            def _(sp):
                w_sync(sp)
                for dst, src in ((flat(s2_f), d["s2"]), (gain[:], d["s_mult"]), (b1[:], d["s_b1"]),
                                 (b2_scaled[:], d["s_b2"])):
                    sp.dma_start(dst, src).then_inc(small, 16)

            @block.tensor
            def _(pe):
                pe.wait_ge(w_ready, w_n)
                pe.wait_ge(gained, 2)
                with pe.Fori(0, NG) as q:
                    cols = bass.ds(q * GT, GT)
                    for f in range(FC):
                        p = f % 2
                        pe.wait_ge(a_ready, q * FC + max(f - 1, 0))
                        for out, ff, sem in ((pg[p], FC + f, g_ready), (px[p], f, x_ready)):
                            for k in range(KC):
                                last = mm3(pe, out[:, 0:GT], s1_hi[:, k, ff * 128:(ff + 1) * 128],
                                           s1_lo[:, k, ff * 128:(ff + 1) * 128], core.xt_hi[:, k, cols],
                                           core.xt_lo[:, k, cols], k == 0, k == KC - 1)
                            last.then_inc(sem, 1)
                    for j in range(GB):
                        p = j % 2
                        pe.wait_ge(lo_ready, q * FC + FC)
                        pe.wait_ge(o_free[p], q * 2 + j // 2)
                        tok = slice(j * L, (j + 1) * L)
                        for f in range(FC):
                            mm3(pe, po[p][:], a_hi[:, f, tok], a_lo[:, f, tok], s2_hi[:, f, :], s2_lo[:, f, :],
                                f == 0, False)
                        pe.matmul(po[p][:], core.ones16[0:1, 0:L], b2_hi[:], start=False, stop=False)
                        pe.matmul(po[p][:], core.ones16[0:1, 0:L], b2_lo[:], start=False,
                                  stop=True).then_inc(o_ready[p], 1)

            @block.scalar
            def _(act):
                w_act(act)
                act.wait_ge(scaled, 3)
                for f in range(FC):
                    act.activation(s2_hi[:, f, :], s2_f[:, f, :], ACT.Identity, scale=gain[:, f:f + 1])
                act.activation(b2_hi[:], b2_scaled[:], ACT.Copy).then_inc(gained, 1)
                with act.Fori(0, NG) as q:
                    for f in range(FC):
                        p = f % 2
                        act.wait_ge(g_ready, q * FC + (f + 1))
                        act.wait_ge(a_ready, q * FC + max(f - 1, 0))
                        act.activation(gate[p][:], pg[p][:, 0:GT], ACT.Gelu, bias=b1[:, FC + f:FC + f + 1],
                                       scale=1.0 / WS).then_inc(gated, 1)
                        act.wait_ge(a_ready, q * FC + (f + 1))
                        if f == 0:
                            act.wait_ge(o_ready[0], q * 2)
                            act.wait_ge(o_ready[1], q * 2)
                        act.activation(a_hi[:, f, :], a32[p][:], ACT.Copy).then_inc(hi_ready, 1)

            @block.vector
            def _(dve):
                w_dve(dve)
                dve.wait_ge(small, 64)
                dve.tensor_scalar(gain[:], gain[:], WS, None, ALU.mult).then_inc(scaled, 1)
                dve.tensor_scalar(b2_scaled[:], b2_scaled[:], WS * WS, None, ALU.mult).then_inc(scaled, 1)
                dve.tensor_scalar(b1[:, 0:FC], b1[:, 0:FC], WS, None, ALU.mult).then_inc(scaled, 1)
                dve.wait_ge(gained, 1)
                for f in range(FC):
                    dve.scalar_tensor_tensor(s2_lo[:, f, :], s2_f[:, f, :], gain[:, f:f + 1], s2_hi[:, f, :],
                                             ALU.mult, ALU.subtract)
                dve.tensor_tensor(b2_lo[:], b2_scaled[:], b2_hi[:], ALU.subtract).then_inc(gained, 1)
                with dve.Fori(0, NG) as q:
                    for f in range(FC):
                        p = f % 2
                        dve.wait_ge(x_ready, q * FC + (f + 1))
                        dve.wait_ge(gated, q * FC + (f + 1))
                        dve.wait_ge(lo_ready, q * FC + max(f - 1, 0))
                        dve.scalar_tensor_tensor(a32[p][:], px[p][:, 0:GT], b1[:, f:f + 1], gate[p][:],
                                                 ALU.add, ALU.mult).then_inc(a_ready, 1)
                        dve.wait_ge(hi_ready, q * FC + (f + 1))
                        dve.tensor_tensor(a_lo[:, f, :], a32[p][:], a_hi[:, f, :], ALU.subtract).then_inc(lo_ready, 1)
                    for j in range(GB):
                        p = j % 2
                        dve.wait_ge(o_ready[p], q * 2 + (j // 2 + 1))
                        b = bass.ds(q * GB + j, 1)
                        dve.scalar_tensor_tensor(core.h[:, b, :], po[p][:].unsqueeze(1), 1.0 / (WS * WS),
                                                 core.h[:, b, :], ALU.mult, ALU.add).then_inc(o_free[p], 1)


def stage_gru(nc, core, d):
    EC = 3
    LS = L + 1
    with Stage(nc, "gru") as st:
        wf_hi, wf_lo = (st.sb(n, [128, KC, 2 * EC * 128], F16) for n in ("wf_hi", "wf_lo"))
        wd_hi, wd_lo = (st.sb(n, [128, EC, D], F16) for n in ("wd_hi", "wd_lo"))
        bf, nbf = st.sb("bf", [128, 2 * EC]), st.sb("nbf", [128, 2 * EC])
        two = range(2)
        keep, drive, hs = ([st.sb(f"{n}{p}", [128, GB, LS]) for p in two] for n in ("keep", "drive", "hs"))
        zg, sx, rx = ([st.sb(f"{n}{p}", [128, GT]) for p in two] for n in ("zg", "sx", "rx"))
        h_hi, h_lo = (st.sb(n, [128, EC, GB, LS], F16) for n in ("h_hi", "h_lo"))
        pk, px = ([st.ps(f"{n}{p}", [128, 512]) for p in two] for n in ("pk", "px"))
        po = [st.ps(f"po{p}", [L, D]) for p in two]
        small, negated, edges = st.sem("small"), st.sem("negated"), st.sem("edges")
        k_ready, x_ready, sig_ready, rx_ready, sum_ready, drive_ready, scanned, hi_ready, lo_ready = (
            st.sem(n) for n in ("k_ready", "x_ready", "sig_ready", "rx_ready", "sum_ready", "drive_ready", "scanned",
                                "hi_ready", "lo_ready"))
        o_ready, o_free = ([st.sem(f"{n}{p}") for p in two] for n in ("o_ready", "o_free"))
        flat = lambda t: t[:].rearrange("p a n -> p (a n)")
        w_sync, w_act, w_dve, (w_ready, w_n) = split_weights(st, core, [
            ("wf", d["w_f"], flat(wf_hi), flat(wf_lo)), ("wd", d["w_down"], flat(wd_hi), flat(wd_lo)),
        ])
        N = NG * EC
        unit = lambda n: divmod(n, EC)
        groups = lambda t: t.rearrange("p (b t) -> p b t", t=L)
        with nc.Block() as block:
            @block.sync
            def _(sp):
                w_sync(sp)
                sp.dma_start(bf[:], d["b_f"]).then_inc(small, 16)

            @block.gpsimd
            def _(pool):
                for p in two:
                    pool.memset(keep[p][:, :, 0:1], 0.0).then_inc(edges, 1)
                    pool.memset(drive[p][:, :, 0:1], 0.5).then_inc(edges, 1)

            @block.tensor
            def _(pe):
                pe.wait_ge(w_ready, w_n)
                for n in range(N):
                    q, e = unit(n)
                    p = n % 2
                    cols = slice(q * GT, (q + 1) * GT)
                    if n >= 2:
                        pe.wait_ge(sig_ready, n - 1)
                        pe.wait_ge(rx_ready, n - 1)
                    for out, ee, sem in ((pk[p], e, k_ready), (px[p], EC + e, x_ready)):
                        for k in range(KC):
                            last = mm3(pe, out[:, 0:GT], wf_hi[:, k, ee * 128:(ee + 1) * 128],
                                       wf_lo[:, k, ee * 128:(ee + 1) * 128], core.xt_hi[:, k, cols],
                                       core.xt_lo[:, k, cols], k == 0, k == KC - 1)
                        last.then_inc(sem, 1)
                    if e == EC - 1:
                        pe.wait_ge(lo_ready, n + 1)
                        for j in range(GB):
                            p2 = j % 2
                            pe.wait_ge(o_free[p2], q * 2 + j // 2)
                            for k in range(EC):
                                last = mm3(pe, po[p2][:], h_hi[:, k, j, 1:LS], h_lo[:, k, j, 1:LS], wd_hi[:, k, :],
                                           wd_lo[:, k, :], k == 0, k == EC - 1)
                            last.then_inc(o_ready[p2], 1)

            @block.scalar
            def _(act):
                w_act(act)
                act.wait_ge(small, 16)
                act.activation(nbf[:], bf[:], ACT.Copy, scale=-1.0).then_inc(negated, 1)
                act.wait_ge(negated, 1)
                act.wait_ge(edges, 4)
                for n in range(N):
                    q, e = unit(n)
                    p = n % 2
                    act.wait_ge(k_ready, n + 1)
                    if n >= 2:
                        act.wait_ge(scanned, n - 1)
                    act.activation(keep[p][:, :, 1:LS], groups(pk[p][:, 0:GT]), ACT.Sigmoid, bias=nbf[:, e:e + 1],
                                   scale=-1.0 / WS)
                    act.activation(zg[p][:], pk[p][:, 0:GT], ACT.Sigmoid, bias=bf[:, e:e + 1], scale=1.0 / WS)
                    act.wait_ge(x_ready, n + 1)
                    act.activation(sx[p][:], px[p][:, 0:GT], ACT.Sigmoid, bias=bf[:, EC + e:EC + e + 1],
                                   scale=1.0 / WS).then_inc(sig_ready, 1)
                    act.wait_ge(scanned, n + 1)
                    if e == 0 and q:
                        act.wait_ge(o_ready[0], q * 2)
                        act.wait_ge(o_ready[1], q * 2)
                    act.activation(h_hi[:, e, :, :], hs[p][:], ACT.Copy).then_inc(hi_ready, 1)

            @block.vector
            def _(dve):
                w_dve(dve)
                dve.wait_ge(edges, 4)
                dve.wait_ge(small, 16)
                for n in range(N):
                    q, e = unit(n)
                    p = n % 2
                    dve.wait_ge(sig_ready, n + 1)
                    dve.tensor_scalar(rx[p][:], px[p][:, 0:GT], 1.0 / WS, bf[:, EC + e:EC + e + 1],
                                      ALU.mult, ALU.add).then_inc(rx_ready, 1)
                    dve.wait_ge(rx_ready, n + 1)
                    dve.tensor_scalar(rx[p][:], rx[p][:], 0.0, None, ALU.max).then_inc(sum_ready, 1)
                    dve.wait_ge(sum_ready, 2 * n + 1)
                    dve.scalar_tensor_tensor(rx[p][:], sx[p][:], 0.5, rx[p][:], ALU.min, ALU.add).then_inc(sum_ready, 1)
                    dve.wait_ge(sum_ready, 2 * n + 2)
                    dve.tensor_tensor(drive[p][:, :, 1:LS], groups(rx[p][:]), groups(zg[p][:]),
                                      ALU.mult).then_inc(drive_ready, 1)
                    dve.wait_ge(drive_ready, n + 1)
                    if n >= 2:
                        dve.wait_ge(hi_ready, n - 1)
                    dve.tensor_tensor_scan(hs[p][:].rearrange("p b t -> p (b t)"),
                                           keep[p][:].rearrange("p b t -> p (b t)"),
                                           drive[p][:].rearrange("p b t -> p (b t)"), 0.0,
                                           ALU.mult, ALU.add).then_inc(scanned, 1)
                    dve.wait_ge(hi_ready, n + 1)
                    dve.tensor_tensor(h_lo[:, e, :, :], hs[p][:], h_hi[:, e, :, :], ALU.subtract).then_inc(lo_ready, 1)
                    if e == EC - 1:
                        for j in range(GB):
                            p2 = j % 2
                            dve.wait_ge(o_ready[p2], q * 2 + (j // 2 + 1))
                            dve.scalar_tensor_tensor(core.h[:, q * GB + j, :], po[p2][:], 1.0 / WS,
                                                     core.h[:, q * GB + j, :], ALU.mult, ALU.add).then_inc(o_free[p2], 1)


def stage_ternary(nc, core, name, mats, floor):
    M = len(mats)
    with Stage(nc, name) as st:
        buf = [st.sb(f"buf{i}", list(m[0].shape)) for i, m in enumerate(mats)]
        neg = [st.sb(f"neg{i}", list(m[0].shape), F16) for i, m in enumerate(mats)]
        asum, thr, nthr = st.sb("asum", [128, M]), st.sb("thr", [128, M]), st.sb("nthr", [128, M])
        tot = st.ps("tot", [128, M])
        landed = [st.sem(f"landed{i}") for i in range(M)]
        summed, totals, chain_sem = st.sem("summed"), st.sem("totals"), st.sem("chain")
        with nc.Block() as block:
            @block.sync
            def _(sp):
                for b, m, s in zip(buf, mats, landed):
                    sp.dma_start(b[:], m[0]).then_inc(s, 16)

            @block.tensor
            def _(pe):
                pe.wait_ge(summed, M)
                pe.matmul(tot[:], core.ones[:], asum[:], start=True, stop=True).then_inc(totals, 1)

            @block.vector
            def _(dve):
                for i, s in enumerate(landed):
                    dve.wait_ge(s, 16)
                    dve.tensor_reduce(out=asum[:, i:i + 1], in_=buf[i][:], op=ALU.add, axis=AX.X,
                                      apply_absolute_value=True).then_inc(summed, 1)
                dve.wait_ge(totals, 1)
                ch = Chain(dve, chain_sem)
                for i, (dram, out, scale) in enumerate(mats):
                    floor(dve, scale, tot[:, i:i + 1], 1.0 / (128 * dram.shape[1])).then_inc(summed, 1)
                dve.wait_ge(summed, 2 * M)
                for i, (dram, out, scale) in enumerate(mats):
                    dve.tensor_scalar(thr[:, i:i + 1], scale, 0.5, None, ALU.mult)
                    ch.step(dve.tensor_scalar(nthr[:, i:i + 1], scale, -0.5, None, ALU.mult))
                for i, (dram, out, scale) in enumerate(mats):
                    ch.step(dve.tensor_scalar(neg[i][:], buf[i][:], nthr[:, i:i + 1], None, ALU.is_lt))
                    ch.step(dve.scalar_tensor_tensor(out, buf[i][:], thr[:, i:i + 1], neg[i][:],
                                                     ALU.is_gt, ALU.subtract))


def stage_bit_gelu(nc, core, d):
    FC, HF = 8, 1024
    with Stage(nc, "bg") as outer:
        wq, wp = outer.sb("wq", [128, KC, HF], F16), outer.sb("wp", [128, FC, D], F16)
        scales = outer.sb("scales", [128, 2])
        lnw, lnb = outer.sb("lnw", [128, FC]), outer.sb("lnb", [128, FC])
        flat = lambda t: t[:].rearrange("p a n -> p (a n)")
        stage_ternary(nc, core, "bgt", [(d["w_fc"], flat(wq), scales[:, 0:1]), (d["w_proj"], flat(wp), scales[:, 1:2])],
                      lambda dve, out, tot, inv: dve.tensor_scalar(out, tot, inv, 1e-6, ALU.mult, ALU.add))
        with Stage(nc, "bgm") as st:
            two = range(2)
            g = [st.sb(f"g{p}", [L, HF]) for p in two]
            gn = st.sb("gn", [L, GB, HF])
            six, mv, rs = st.sb("six", [L, 2, 6]), st.sb("mv", [L, 2]), st.sb("rs", [L, 1])
            half = st.sb("half", [L, 1])
            full = [st.sb(f"full{p}", [128, GT]) for p in two]
            a_hi, a_lo = (st.sb(n, [128, FC, GT], F16) for n in ("a_hi", "a_lo"))
            ph = [st.ps(f"ph{p}", [L, HF]) for p in two]
            pt = [st.ps(f"pt{p}", [128, 512]) for p in two]
            po = [st.ps(f"po{p}", [L, D]) for p in two]
            small, pow_ready, half_made = st.sem("small"), st.sem("pow_ready"), st.sem("half_made")
            h_ready, gelu_done, stats, aggr, normed = (st.sem(n) for n in (
                "h_ready", "gelu_done", "stats", "aggr", "normed"))
            eps_added = st.sem("eps_added")
            t_ready, hi_ready, full_ready, lo_ready = (st.sem(n) for n in (
                "t_ready", "hi_ready", "full_ready", "lo_ready"))
            o_ready, o_free = ([st.sem(f"{n}{p}") for p in two] for n in ("o_ready", "o_free"))
            with nc.Block() as block:
                @block.sync
                def _(sp):
                    sp.dma_start(lnw[:], d["ln_w"]).then_inc(small, 16)
                    sp.dma_start(lnb[:], d["ln_b"]).then_inc(small, 16)

                @block.gpsimd
                def _(pool):
                    pool.memset(half[:], -0.5).then_inc(half_made, 1)
                    pool.wait_ge(half_made, 1)
                    with pool.Fori(0, NB) as b:
                        pool.wait_ge(eps_added, b + 1)
                        pool.tensor_tensor(rs[:], mv[:, 1:2], half[:], ALU.pow).then_inc(pow_ready, 1)

                @block.tensor
                def _(pe):
                    with pe.Fori(0, NG) as q:
                        for j in range(GB):
                            p = j % 2
                            if j >= 2:
                                pe.wait_ge(gelu_done, q * GB + (j - 1))
                            else:
                                pe.wait_ge(gelu_done, q * GB)
                            tok = bass.ds(q * GT + j * L, L)
                            for s in range(2):
                                n = 0
                                for k in range(KC):
                                    for x in (core.xt_hi, core.xt_lo):
                                        last = pe.matmul(ph[p][:, s * 512:(s + 1) * 512], x[:, k, tok],
                                                         wq[:, k, s * 512:(s + 1) * 512], start=n == 0, stop=n == 3)
                                        n += 1
                            last.then_inc(h_ready, 1)
                        pe.wait_ge(normed, q * GB + GB)
                        for f in range(FC):
                            pe.wait_ge(lo_ready, q * FC + max(f - 1, 0))
                            for j in range(GB):
                                last = pe.transpose(pt[f % 2][:, j * L:(j + 1) * L], gn[:, j, f * 128:(f + 1) * 128],
                                                    core.ident[0:L, 0:L])
                            last.then_inc(t_ready, 1)
                        pe.wait_ge(lo_ready, q * FC + FC)
                        for j in range(GB):
                            p = j % 2
                            pe.wait_ge(o_free[p], q * 2 + j // 2)
                            tok = slice(j * L, (j + 1) * L)
                            for f in range(FC):
                                pe.matmul(po[p][:], a_hi[:, f, tok], wp[:, f, :], start=f == 0, stop=False)
                                last = pe.matmul(po[p][:], a_lo[:, f, tok], wp[:, f, :], start=False,
                                                 stop=f == FC - 1)
                            last.then_inc(o_ready[p], 1)

                @block.scalar
                def _(act):
                    act.wait_ge(small, 32)
                    with act.Fori(0, NG) as q:
                        for j in range(GB):
                            p = j % 2
                            act.wait_ge(h_ready, q * GB + (j + 1))
                            act.wait_ge(normed, q * GB + max(j - 1, 0))
                            act.activation(g[p][:], ph[p][:], ACT.Gelu).then_inc(gelu_done, 1)
                        act.wait_ge(o_ready[0], q * 2)
                        act.wait_ge(o_ready[1], q * 2)
                        for f in range(FC):
                            act.wait_ge(t_ready, q * FC + (f + 1))
                            act.activation(a_hi[:, f, :], pt[f % 2][:, 0:GT], ACT.Identity, bias=lnb[:, f:f + 1],
                                           scale=lnw[:, f:f + 1]).then_inc(hi_ready, 1)

                @block.vector
                def _(dve):
                    dve.wait_ge(small, 32)
                    with dve.Fori(0, NG) as q:
                        for j in range(GB):
                            p, n = j % 2, q * GB + j
                            dve.wait_ge(gelu_done, n + 1)
                            dve.wait_ge(pow_ready, n)
                            dve.bn_stats(six[:, 0, :], g[p][:, 0:512])
                            dve.bn_stats(six[:, 1, :], g[p][:, 512:1024]).then_inc(stats, 1)
                            wait_alone(dve, core, stats, n + 1)
                            dve.bn_aggr(mv[:], six[:].rearrange("p a n -> p (a n)")).then_inc(aggr, 1)
                            dve.wait_ge(aggr, n + 1)
                            dve.tensor_scalar(mv[:, 1:2], mv[:, 1:2], EPS, None, ALU.add).then_inc(eps_added, 1)
                            dve.wait_ge(pow_ready, n + 1)
                            if j == 0:
                                dve.wait_ge(t_ready, q * FC)
                            dve.tensor_scalar(gn[:, j, :], g[p][:], mv[:, 0:1], rs[:],
                                              ALU.subtract, ALU.mult).then_inc(normed, 1)
                            dve.wait_ge(normed, n + 1)
                        for f in range(FC):
                            dve.wait_ge(hi_ready, q * FC + (f + 1))
                            dve.tensor_scalar(full[f % 2][:], pt[f % 2][:, 0:GT], lnw[:, f:f + 1], lnb[:, f:f + 1],
                                              ALU.mult, ALU.add).then_inc(full_ready, 1)
                            dve.wait_ge(full_ready, q * FC + (f + 1))
                            dve.tensor_tensor(a_lo[:, f, :], full[f % 2][:], a_hi[:, f, :],
                                              ALU.subtract).then_inc(lo_ready, 1)
                        for j in range(GB):
                            p = j % 2
                            dve.wait_ge(o_ready[p], q * 2 + (j // 2 + 1))
                            b = bass.ds(q * GB + j, 1)
                            dve.tensor_tensor(core.h[:, b, :], po[p][:].unsqueeze(1), core.h[:, b, :],
                                              ALU.add).then_inc(o_free[p], 1)


def stage_linear_attention(nc, core, d):
    Z = 64
    W2 = Z + D
    with Stage(nc, "la") as st:
        wt_hi, wt_lo = (st.sb(n, [128, KC, Z], F16) for n in ("wt_hi", "wt_lo"))
        wg_hi, wg_lo = (st.sb(n, [128, KC, W2], F16) for n in ("wg_hi", "wg_lo"))
        th_hi, th_lo = (st.sb(n, [Z, GT], F16) for n in ("th_hi", "th_lo"))
        two = range(2)
        pg_hi, pg_lo = ([st.sb(f"{n}{p}", [L, W2], F16) for p in two] for n in ("pg_hi", "pg_lo"))
        m_hi, m_lo = ([st.sb(f"{n}{p}", [Z, D], F16) for p in two] for n in ("m_hi", "m_lo"))
        pth = st.ps("pth", [Z, 512])
        ppg, pm, po = ([st.ps(f"{n}{p}", [s, 512]) for p in two] for n, s in (("ppg", L), ("pm", Z), ("po", L)))
        th_ready, th_high, th_split = st.sem("th_ready"), st.sem("th_high"), st.sem("th_split")
        g_ready, g_high, g_split, m_ready, m_high, m_split, o_ready, o_free = (
            [st.sem(f"{n}{p}") for p in two] for n in (
                "g_ready", "g_high", "g_split", "m_ready", "m_high", "m_split", "o_ready", "o_free"))
        flat = lambda t: t[:].rearrange("p a n -> p (a n)")
        w_sync, w_act, w_dve, (w_ready, w_n) = split_weights(st, core, [
            ("wt", d["w_theta"], flat(wt_hi), flat(wt_lo)), ("wg", d["w_phi_g"], flat(wg_hi), flat(wg_lo)),
        ])
        with nc.Block() as block:
            @block.sync
            def _(sp):
                w_sync(sp)

            @block.tensor
            def _(pe):
                pe.wait_ge(w_ready, w_n)
                with pe.Fori(0, NG) as q:
                    cols = bass.ds(q * GT, GT)
                    pe.wait_ge(th_split, q)
                    for k in range(KC):
                        last = mm3(pe, pth[:, 0:GT], wt_hi[:, k, :], wt_lo[:, k, :], core.xt_hi[:, k, cols],
                                   core.xt_lo[:, k, cols], k == 0, k == KC - 1)
                    last.then_inc(th_ready, 1)

                    def project(j):
                        p = j % 2
                        tok = bass.ds(q * GT + j * L, L)
                        pe.wait_ge(g_split[p], q * 2 + j // 2)
                        for k in range(KC):
                            last = mm3(pe, ppg[p][:, 0:W2], core.xt_hi[:, k, tok], core.xt_lo[:, k, tok],
                                       wg_hi[:, k, :], wg_lo[:, k, :], k == 0, k == KC - 1)
                        last.then_inc(g_ready[p], 1)

                    def collect(j):
                        p, before = j % 2, q * 2 + j // 2
                        pe.wait_ge(g_split[p], before + 1)
                        pe.wait_ge(m_split[p], before)
                        mm3(pe, pm[p][:, 0:D], pg_hi[p][:, 0:Z], pg_lo[p][:, 0:Z], pg_hi[p][:, Z:W2],
                            pg_lo[p][:, Z:W2], True, True).then_inc(m_ready[p], 1)

                    def spread(j):
                        p, before = j % 2, q * 2 + j // 2
                        pe.wait_ge(th_split, q + 1)
                        pe.wait_ge(m_split[p], before + 1)
                        pe.wait_ge(o_free[p], before)
                        tok = slice(j * L, (j + 1) * L)
                        mm3(pe, po[p][:, 0:D], th_hi[:, tok], th_lo[:, tok], m_hi[p][:], m_lo[p][:], True,
                            True).then_inc(o_ready[p], 1)

                    project(0)
                    for j in range(GB):
                        if j + 1 < GB:
                            project(j + 1)
                        collect(j)
                        if j:
                            spread(j - 1)
                    spread(GB - 1)

            @block.scalar
            def _(act):
                w_act(act)
                with act.Fori(0, NG) as q:
                    act.wait_ge(th_ready, q + 1)
                    for p in two:
                        act.wait_ge(o_ready[p], q * 2)
                    act.activation(th_hi[:], pth[:, 0:GT], ACT.Copy, scale=1.0 / WS).then_inc(th_high, 1)
                    for j in range(GB):
                        p, before = j % 2, q * 2 + j // 2
                        act.wait_ge(g_ready[p], before + 1)
                        act.wait_ge(m_ready[p], before)
                        act.activation(pg_hi[p][:], ppg[p][:, 0:W2], ACT.Copy, scale=1.0 / WS).then_inc(g_high[p], 1)
                        act.wait_ge(m_ready[p], before + 1)
                        act.wait_ge(o_ready[p], before)
                        act.activation(m_hi[p][:], pm[p][:, 0:D], ACT.Copy, scale=1.0 / 16).then_inc(m_high[p], 1)

            @block.vector
            def _(dve):
                w_dve(dve)

                def add(q, j):
                    p = j % 2
                    dve.wait_ge(o_ready[p], q * 2 + (j // 2 + 1))
                    b = bass.ds(q * GB + j, 1)
                    dve.tensor_tensor(core.h[:, b, :], po[p][:, 0:D].unsqueeze(1), core.h[:, b, :],
                                      ALU.add).then_inc(o_free[p], 1)

                with dve.Fori(0, NG) as q:
                    dve.wait_ge(th_high, q + 1)
                    dve.scalar_tensor_tensor(th_lo[:], pth[:, 0:GT], 1.0 / WS, th_hi[:], ALU.mult,
                                             ALU.subtract).then_inc(th_split, 1)
                    for j in range(GB):
                        p, before = j % 2, q * 2 + j // 2
                        dve.wait_ge(g_high[p], before + 1)
                        dve.scalar_tensor_tensor(pg_lo[p][:], ppg[p][:, 0:W2], 1.0 / WS, pg_hi[p][:], ALU.mult,
                                                 ALU.subtract).then_inc(g_split[p], 1)
                        dve.wait_ge(m_high[p], before + 1)
                        dve.scalar_tensor_tensor(m_lo[p][:], pm[p][:, 0:D], 1.0 / 16, m_hi[p][:], ALU.mult,
                                                 ALU.subtract).then_inc(m_split[p], 1)
                        if j:
                            add(q, j - 1)
                    add(q, GB - 1)


MAGIC = 12582912.0


def stage_bit_glu(nc, core, d):
    FC, HF = 8, 1024
    with Stage(nc, "glu") as outer:
        wg, wu = outer.sb("wg", [128, KC, HF], F16), outer.sb("wu", [128, KC, HF], F16)
        wd = outer.sb("wd", [128, FC, D], F16)
        scales = outer.sb("scales", [128, 3])
        xq = outer.sb("xq", [128, KC, T], F16)
        deq = outer.sb("deq", [L, NB, 2])
        flat = lambda t: t[:].rearrange("p a n -> p (a n)")
        stage_ternary(nc, core, "glut", [(d["w_gate"], flat(wg), scales[:, 0:1]), (d["w_up"], flat(wu), scales[:, 1:2]),
                                         (d["w_dn"], flat(wd), scales[:, 2:3])],
                      lambda dve, out, tot, inv: dve.tensor_scalar(out, tot, inv, 1e-5, ALU.mult, ALU.max))
        with Stage(nc, "gluq") as st:
            two = range(2)
            amax, sc = st.sb("amax", [L, NB]), st.sb("sc", [L, NB])
            xn = st.sb("xn", [L, NB, D])
            xi = st.sb("xi", [L, NB, D], F16)
            pt = [[st.ps(f"pt{u}{c}", [128, 512], F16) for c in range(KC)] for u in two]
            normed, chain_sem, rounded, t_ready = (st.sem(n) for n in ("normed", "chain", "rounded", "t_ready"))
            copied = [st.sem(f"copied{u}") for u in two]
            with nc.Block() as block:
                @block.vector
                def _(dve):
                    for b in range(NB):
                        dve.tensor_scalar(xn[:, b, :], core.h[:, b, :], core.mean[:, b:b + 1], core.rstd[:, b:b + 1],
                                          ALU.subtract, ALU.mult).then_inc(normed, 1)
                    dve.wait_ge(normed, NB)
                    ch = Chain(dve, chain_sem)
                    ch.step(dve.tensor_reduce(out=amax[:], in_=xn[:], op=ALU.max, axis=AX.X,
                                              apply_absolute_value=True))
                    ch.step(dve.tensor_scalar(amax[:], amax[:], 1e-5, None, ALU.max))
                    ch.step(dve.reciprocal(sc[:], amax[:]))
                    ch.step(dve.tensor_scalar(sc[:], sc[:], 127.0, None, ALU.mult))
                    ch.step(dve.tensor_scalar(amax[:], amax[:], 1.0 / 127.0, None, ALU.mult))
                    for n in range(2):
                        ch.step(dve.tensor_scalar(deq[:, :, n], amax[:], scales[0:L, n:n + 1], None, ALU.mult))
                    for b in range(NB):
                        dve.tensor_scalar(xn[:, b, :], xn[:, b, :], sc[:, b:b + 1], MAGIC, ALU.mult,
                                          ALU.add).then_inc(normed, 1)
                    for b in range(NB):
                        dve.wait_ge(normed, b + (NB + 1))
                        dve.tensor_scalar(xi[:, b, :], xn[:, b, :], MAGIC, 127.0, ALU.subtract,
                                          ALU.min).then_inc(rounded, 1)

                @block.tensor
                def _(pe):
                    for q in range(NG):
                        u = q % 2
                        pe.wait_ge(copied[u], q // 2 * KC)
                        pe.wait_ge(rounded, q * GB + GB)
                        for c in range(KC):
                            for j in range(GB):
                                last = pe.transpose(pt[u][c][:, j * 128:j * 128 + L],
                                                    xi[:, q * GB + j, c * 128:(c + 1) * 128], core.ident16[0:L, 0:L])
                            last.then_inc(t_ready, 1)

                @block.scalar
                def _(act):
                    for q in range(NG):
                        for c in range(KC):
                            act.wait_ge(t_ready, q * KC + c + 1)
                            act.activation(xq[:, c, q * GT:(q + 1) * GT].rearrange("p (j t) -> p j t", t=L),
                                           pt[q % 2][c][:].rearrange("p (j t) -> p j t", t=128)[:, :, 0:L],
                                           ACT.Copy).then_inc(copied[q % 2], 1)
        with Stage(nc, "glum") as st:
            two = range(2)
            s = [st.sb(f"s{p}", [L, 512]) for p in two]
            gu = [st.sb(f"gu{p}", [L, HF]) for p in two]
            qi = [st.sb(f"qi{p}", [L, HF], F16) for p in two]
            qt = [st.sb(f"qt{p}", [128, FC, 128], F16) for p in two]
            amax, sc, dq, dg = ([st.sb(f"{n}{p}", [L, 1]) for p in two] for n in ("amax", "sc", "dq", "dg"))
            dg_done = st.sem("dg_done")
            pg, pu = ([st.ps(f"{n}{p}", [L, 512]) for p in two] for n in ("pg", "pu"))
            pt = [st.ps(f"pt{p}", [128, FC, 128], F16) for p in two]
            po = [st.ps(f"po{p}", [L, D]) for p in two]
            g_ready, silu_done, gu_done = st.sem("g_ready"), st.sem("silu_done"), st.sem("gu_done")
            maxed, chain_sem, quant = st.sem("maxed"), st.sem("chain"), st.sem("quant")
            t_ready, copied, o_ready, o_free = ([st.sem(f"{n}{p}") for p in two] for n in (
                "t_ready", "copied", "o_ready", "o_free"))
            with nc.Block() as block:
                @block.tensor
                def _(pe):
                    def turn(p, uses, tile):
                        pe.wait_ge(quant, tile + 1)
                        pe.wait_ge(copied[p], uses)
                        for f in range(FC):
                            last = pe.transpose(pt[p][:, f, 0:L], qi[p][:, f * 128:(f + 1) * 128],
                                                core.ident16[0:L, 0:L])
                        last.then_inc(t_ready[p], 1)

                    def down(p, uses):
                        pe.wait_ge(copied[p], uses + 1)
                        pe.wait_ge(o_free[p], uses)
                        for f in range(FC):
                            last = pe.matmul(po[p][:], qt[p][:, f, 0:L], wd[:, f, :], start=f == 0, stop=f == FC - 1)
                        last.then_inc(o_ready[p], 1)

                    def halves(tile):
                        for s in range(2):
                            pe.wait_ge(gu_done, tile * 2 - 2 + s + 1)
                            multiply(tile, s)

                    def multiply(tile, s):
                        tok = bass.ds(tile * L, L)
                        for out, w in ((pg[s], wg), (pu[s], wu)):
                            for k in range(KC):
                                last = pe.matmul(out[:], xq[:, k, tok], w[:, k, s * 512:(s + 1) * 512],
                                                 start=k == 0, stop=k == KC - 1)
                        last.then_inc(g_ready, 1)

                    for s in range(2):
                        multiply(0, s)
                    with pe.Fori(0, NB // 2 - 1) as i:
                        for u in range(2):
                            halves(i * 2 + (u + 1))
                            turn(u, i, i * 2 + u)
                            down(u, i)
                    halves(NB - 1)
                    for u in range(2):
                        turn(u, NB // 2 - 1, NB - 2 + u)
                        down(u, NB // 2 - 1)

                @block.scalar
                def _(act):
                    def step(j, p, before):
                        b = bass.ds(j, 1)
                        act.activation(dg[p][:].unsqueeze(1), deq[:, b, 0:1], ACT.Copy).then_inc(dg_done, 1)
                        act.wait_ge(dg_done, j + 1)
                        for s_ in range(2):
                            act.wait_ge(g_ready, j * 2 + (s_ + 1))
                            act.wait_ge(gu_done, j * 2)
                            act.activation(s[s_][:], pg[s_][:], ACT.Silu, scale=dg[p][:]).then_inc(silu_done, 1)
                        act.wait_ge(t_ready[p], before + 1)
                        act.wait_ge(o_ready[p], before)
                        act.activation(qt[p][:, :, 0:L], pt[p][:, :, 0:L], ACT.Copy).then_inc(copied[p], 1)
                    ring(act, NB, step)

                @block.vector
                def _(dve):
                    def step(j, p, before):
                        b = bass.ds(j, 1)
                        for s_ in range(2):
                            dve.wait_ge(silu_done, j * 2 + (s_ + 1))
                            dve.scalar_tensor_tensor(gu[p][:, s_ * 512:(s_ + 1) * 512], pu[s_][:],
                                                     deq[:, b, 1:2].rearrange("p a n -> p (a n)"), s[s_][:],
                                                     ALU.mult, ALU.mult).then_inc(gu_done, 1)
                        dve.wait_ge(gu_done, j * 2 + 2)
                        ch = Chain(dve, chain_sem, j * 5)
                        ch.step(dve.tensor_reduce(out=amax[p][:], in_=gu[p][:], op=ALU.max, axis=AX.X,
                                                  apply_absolute_value=True))
                        ch.step(dve.tensor_scalar(amax[p][:], amax[p][:], 1e-5, None, ALU.max))
                        dve.tensor_scalar(dq[p][:], amax[p][:], scales[0:L, 2:3], 1.0 / 127.0, ALU.mult, ALU.mult)
                        ch.step(dve.reciprocal(sc[p][:], amax[p][:]))
                        ch.step(dve.tensor_scalar(sc[p][:], sc[p][:], 127.0, None, ALU.mult))
                        ch.step(dve.tensor_scalar(gu[p][:], gu[p][:], sc[p][:], MAGIC, ALU.mult, ALU.add))
                        dve.wait_ge(t_ready[p], before)
                        dve.tensor_scalar(qi[p][:], gu[p][:], MAGIC, 127.0, ALU.subtract, ALU.min).then_inc(quant, 1)
                        dve.wait_ge(o_ready[p], before + 1)
                        dve.scalar_tensor_tensor(core.h[:, b, :], po[p][:].unsqueeze(1), dq[p][:], core.h[:, b, :],
                                                 ALU.mult, ALU.add).then_inc(o_free[p], 1)
                    ring(dve, NB, step)


def stage_attention(nc, core, d, m):
    H, HD = 16, 16
    HG = 4
    MS = 64.0
    with Stage(nc, "mha") as st:
        wl_hi, wl_lo = (st.sb(n, [128, H // HG, 128], F16) for n in ("wl_hi", "wl_lo"))
        wv_hi, wv_lo, wo_hi, wo_lo = (st.sb(n, [128, KC, D], F16) for n in ("wv_hi", "wv_lo", "wo_hi", "wo_lo"))
        bv_hi, bv_lo, bo_hi, bo_lo = (st.sb(n, [1, D], F16) for n in ("bv_hi", "bv_lo", "bo_hi", "bo_lo"))
        two = range(2)
        row, low_row = st.sb("row", [128, 1], I32), st.sb("low_row", [128, 1])
        to_q, to_same, to_cross = (st.sb(n, [128, 1]) for n in ("to_q", "to_same", "to_cross"))
        to_qm = st.sb("to_qm", [128, 1])
        spread = st.sb("spread", [128, H, L], F16)
        q, same, cross = ([st.sb(f"{n}{p}", [128, HG, L], F16) for p in two] for n in ("q", "same", "cross"))
        v_hi = [st.sb(f"v_hi{p}", [L, H, HD + 1], F16) for p in two]
        v_lo = [st.sb(f"v_lo{p}", [L, H, HD], F16) for p in two]
        peak = [st.sb(f"peak{p}", [L, H]) for p in two]
        peaks8, qm = st.sb("peaks8", [L, 8, H]), st.sb("qm", [128, L], F16)
        am = [st.sb(f"am{p}", [128, L], F16) for p in two]
        prob = [st.sb(f"prob{r}", [L, HG, L]) for r in two]
        prob_hi, prob_lo = ([st.sb(f"{n}{g}", [L, HG, L], F16) for g in range(4)] for n in ("prob_hi", "prob_lo"))
        rec = st.sb("rec", [L, H])
        o = st.sb("o", [L, H, HD])
        ot_hi, ot_lo = (st.sb(n, [128, KC, L], F16) for n in ("ot_hi", "ot_lo"))
        pu = st.ps("pu", [128, 512])
        pvo = st.ps("pvo", [L, 2, D])
        s1, s2 = ([st.ps(f"{n}{r}", [L, 512]) for r in two] for n in ("s1", "s2"))
        pacc, pt = st.ps("pacc", [L, 512]), st.ps("pt", [128, 512])
        v_high, p_high, p_low = st.sem("v_high"), st.sem("p_high"), st.sem("p_low")
        mw = MoeWeights(st, m, d, 1)
        assert m.steps == NB
        (made, masks, ones_set, u_ready, q_ready, ac_ready, v_ready, v_out, s1_ready, maxed, peaks_ready, mt_ready,
         qm_ready, am_ready, s2_ready, exped, pv_done, rec_ready, o_made, ot_ready, oh_ready, ol_ready, out_ready,
         h_added) = (st.sem(n) for n in (
             "made", "masks", "ones_set", "u_ready", "q_ready", "ac_ready", "v_ready", "v_out", "s1_ready", "maxed",
             "peaks_ready", "mt_ready", "qm_ready", "am_ready", "s2_ready", "exped", "pv_done", "rec_ready", "o_made",
             "ot_ready", "oh_ready", "ol_ready", "out_ready", "h_added"))
        flat = lambda t: t[:].rearrange("p a n -> p (a n)")
        w_sync, w_act, w_dve, (w_ready, w_n) = split_weights(st, core, [
            ("wl", d["w_l"], flat(wl_hi), flat(wl_lo)), ("wv", d["w_v"], flat(wv_hi), flat(wv_lo)),
            ("bv", d["b_v"], bv_hi[:], bv_lo[:]), ("wo", d["w_o"], flat(wo_hi), flat(wo_lo)),
            ("bo", d["b_o"], bo_hi[:], bo_lo[:]),
        ], [("wo", "wl"), ("bo", "bv")])
        heads = lambda t: t[:, 0:HG * L].rearrange("p (h t) -> p h t", t=L)

        def need(eng, sem, value):
            if not isinstance(value, int) or value > 0:
                eng.wait_ge(sem, value)

        def turns(eng, prologue, turn):
            prologue()
            turn(0, 0, 0, True, True, True, False)
            with eng.Fori(0, (NB - 4) // 2) as i:
                for u in range(2):
                    turn(i * 2 + (1 + u), (1 + u) % 2, i + (1 + u) // 2, True, True, True, True)
            for j in range(NB - 3, NB + 1):
                turn(j, j % 2, j // 2, j < NB, j + 1 < NB, j + 2 < NB, True)

        with nc.Block() as block:
            @block.sync
            def _(sp):
                w_sync(sp)
                mw.load_small(sp)
                ring(sp, m.steps, lambda j, p, before: mw.load(sp, j, p, before))

            @block.gpsimd
            def _(pool):
                ch = Chain(pool, made)
                ch.step(pool.iota(row[:], pattern=[[0, 1]], base=0, channel_multiplier=1))
                ch.step(pool.memset(spread[:], 0.0))
                for half in range(8):
                    ch.step(pool.affine_select(out=spread[:], in_=spread[:], compare_op=ALU.not_equal, fill=MS,
                                               base=-16 * half, pattern=[[-1, H], [0, L]], channel_multiplier=1))
                for p in two:
                    pool.memset(v_hi[p][:, :, HD:HD + 1], 1.0).then_inc(ones_set, 1)
                with pool.Fori(0, NB) as j:
                    for g in range(4):
                        pool.wait_ge(p_high, j * 4 + (g + 1))
                        pool.tensor_tensor(prob_lo[g][:], prob[g % 2][:], prob_hi[g][:],
                                           ALU.subtract).then_inc(p_low, 1)

            @block.tensor
            def _(pe):
                def project_u(j):
                    need(pe, ac_ready, j)
                    cols = bass.ds(j * L, L)
                    for c in range(H // HG):
                        last = mm3(pe, pu[:, c * L:(c + 1) * L], wl_hi[:, c, :], wl_lo[:, c, :],
                                   core.xt_hi[:, c // 2, cols], core.xt_lo[:, c // 2, cols], True, True)
                    last.then_inc(u_ready, 1)

                def project_v(j):
                    need(pe, v_out, j)
                    need(pe, h_added, j - 2)
                    cols = bass.ds(j * L, L)
                    for k in range(KC):
                        mm3(pe, pvo[:, 0, :], core.xt_hi[:, k, cols], core.xt_lo[:, k, cols], wv_hi[:, k, :],
                            wv_lo[:, k, :], k == 0, False)
                    pe.matmul(pvo[:, 0, :], core.ones16[0:1, 0:L], bv_hi[:], start=False, stop=False)
                    pe.matmul(pvo[:, 0, :], core.ones16[0:1, 0:L], bv_lo[:], start=False,
                              stop=True).then_inc(v_ready, 1)

                def first_pass(j, p, g):
                    need(pe, ac_ready, j + 1)
                    need(pe, maxed, j * 4 + (g - 1))
                    rows = slice(32 * g, 32 * g + 32)
                    for c in range(HG):
                        out = s1[g % 2][:, c * L:(c + 1) * L]
                        pe.matmul(out, same[p][rows, c, :], same[p][rows, c, :], start=True, stop=False)
                        last = pe.matmul(out, same[p][rows, c, :], cross[p][rows, c, :], start=False, stop=True)
                    last.then_inc(s1_ready, 1)

                def turn_peaks(j):
                    need(pe, peaks_ready, j + 1)
                    need(pe, am_ready, j)
                    need(pe, ol_ready, j - 1)
                    pe.transpose(pt[:, 256:256 + L], peaks8[:].rearrange("p a h -> p (a h)"),
                                 core.ident[0:L, 0:L]).then_inc(mt_ready, 1)

                def second_pass(j, p, g):
                    need(pe, am_ready, j + 1)
                    need(pe, exped, j * 4 + (g - 1))
                    rows = slice(32 * g, 32 * g + 32)
                    for c in range(HG):
                        out = s2[g % 2][:, c * L:(c + 1) * L]
                        pe.matmul(out, same[p][rows, c, :], same[p][rows, c, :], start=True, stop=False)
                        pe.matmul(out, same[p][rows, c, :], cross[p][rows, c, :], start=False, stop=False)
                        last = pe.matmul(out, spread[rows, c * HG + g, :], am[p][rows, :], start=False, stop=True)
                    last.then_inc(s2_ready, 1)

                def weigh_v(j, p, g):
                    need(pe, p_low, j * 4 + (g + 1))
                    if g == 0:
                        need(pe, v_out, j + 1)
                        need(pe, o_made, j)
                    for c in range(HG):
                        h = c * HG + g
                        out = pacc[:, h * (HD + 1):(h + 1) * (HD + 1)]
                        pe.matmul(out, prob_hi[g][:, c, :], v_hi[p][:, h, :], start=True, stop=False)
                        pe.matmul(out[:, 0:HD], prob_hi[g][:, c, :], v_lo[p][:, h, :], start=False, stop=False)
                        last = pe.matmul(out, prob_lo[g][:, c, :], v_hi[p][:, h, :], start=False, stop=True)
                    last.then_inc(pv_done, 1)

                def turn_o(j):
                    need(pe, o_made, j + 1)
                    need(pe, ol_ready, j)
                    for c in range(KC):
                        last = pe.transpose(pt[:, c * L:(c + 1) * L],
                                            o[:].rearrange("p h e -> p (h e)")[:, c * 128:(c + 1) * 128],
                                            core.ident[0:L, 0:L])
                    last.then_inc(ot_ready, 1)

                def project_out(j):
                    need(pe, ol_ready, j + 1)
                    need(pe, h_added, j)
                    need(pe, v_out, min(j + 3, NB) if isinstance(j, int) else j + 3)
                    for k in range(KC):
                        mm3(pe, pvo[:, 1, :], ot_hi[:, k, :], ot_lo[:, k, :], wo_hi[:, k, :], wo_lo[:, k, :],
                            k == 0, False)
                    pe.matmul(pvo[:, 1, :], core.ones16[0:1, 0:L], bo_hi[:], start=False, stop=False)
                    pe.matmul(pvo[:, 1, :], core.ones16[0:1, 0:L], bo_lo[:], start=False,
                              stop=True).then_inc(out_ready, 1)

                def prologue():
                    pe.wait_ge(w_ready, w_n)
                    pe.wait_ge(made, 10)
                    pe.wait_ge(ones_set, 2)
                    for j in range(2):
                        project_u(j)
                        project_v(j)
                    for g in range(4):
                        first_pass(0, 0, g)
                    turn_peaks(0)

                def turn(j, p, before, now, ahead1, ahead2, behind):
                    for g in range(4):
                        if now:
                            second_pass(j, p, g)
                        if behind and g == 1:
                            turn_o(j - 1)
                        if now and g >= 2:
                            weigh_v(j, p, g - 2)
                        if behind and g == 2:
                            project_out(j - 1)
                        if ahead1:
                            first_pass(j + 1, 1 - p, g)
                    if ahead2:
                        project_u(j + 2)
                        project_v(j + 2)
                    if now:
                        weigh_v(j, p, 2)
                        weigh_v(j, p, 3)
                    if ahead1:
                        turn_peaks(j + 1)

                turns(pe, prologue, turn)

            @block.scalar
            def _(act):
                def take_q(j, p):
                    act.wait_ge(u_ready, j + 1)
                    need(act, ac_ready, j - 1)
                    act.activation(q[p][:], heads(pu), ACT.Identity, scale=to_q[:]).then_inc(q_ready, 1)

                def take_v(j, p):
                    act.wait_ge(v_ready, j + 1)
                    need(act, pv_done, j * 4 - 4)
                    act.activation(v_hi[p][:, :, 0:HD], pvo[:, 0, :].rearrange("p (h e) -> p h e", e=HD), ACT.Copy,
                                   scale=1.0 / WS).then_inc(v_high, 1)

                def take_qm(j):
                    act.wait_ge(mt_ready, j + 1)
                    need(act, am_ready, j)
                    act.activation(qm[:], pt[:, 256:256 + L], ACT.Identity, scale=to_qm[:]).then_inc(qm_ready, 1)

                def exponential(j, g):
                    act.wait_ge(s2_ready, j * 4 + (g + 1))
                    need(act, p_low, j * 4 + (g - 1))
                    act.activation(prob[g % 2][:], heads(s2[g % 2]), ACT.Exp, scale=0.25).then_inc(exped, 1)

                def round_prob(j, g):
                    act.wait_ge(exped, j * 4 + (g + 1))
                    need(act, pv_done, j * 4 + (g - 3))
                    act.activation(prob_hi[g][:], prob[g % 2][:], ACT.Copy).then_inc(p_high, 1)

                def take_o(j):
                    act.wait_ge(ot_ready, j + 1)
                    need(act, out_ready, j)
                    act.activation(ot_hi[:], pt[:, 0:KC * L].rearrange("p (c t) -> p c t", t=L),
                                   ACT.Copy).then_inc(oh_ready, 1)

                def prologue():
                    w_act(act)
                    act.wait_ge(mw.ready, 2)
                    act.wait_ge(ones_set, 2)
                    act.wait_ge(masks, 8)
                    for j in range(2):
                        take_q(j, j)
                        take_v(j, j)
                    take_qm(0)

                def turn(j, p, before, now, ahead1, ahead2, behind):
                    for g in range(4):
                        if now:
                            exponential(j, g)
                            round_prob(j, g)
                        if behind and g == 1:
                            take_o(j - 1)
                    if ahead2:
                        take_q(j + 2, p)
                        take_v(j + 2, p)
                    if ahead1:
                        take_qm(j + 1)
                    if now:
                        mw.high(act, j, p, before)

                turns(act, prologue, turn)

            @block.vector
            def _(dve):
                def split_u(j, p):
                    dve.wait_ge(q_ready, j + 1)
                    need(dve, s2_ready, j * 4 - 4)
                    dve.scalar_tensor_tensor(same[p][:], heads(pu), to_same[:], q[p][:], ALU.mult, ALU.subtract)
                    dve.scalar_tensor_tensor(cross[p][:], heads(pu), to_cross[:], q[p][:], ALU.mult,
                                             ALU.add).then_inc(ac_ready, 1)

                def split_v(j, p):
                    dve.wait_ge(v_high, j + 1)
                    need(dve, pv_done, j * 4 - 4)
                    dve.scalar_tensor_tensor(v_lo[p][:], pvo[:, 0, :].rearrange("p (h e) -> p h e", e=HD), 1.0 / WS,
                                             v_hi[p][:, :, 0:HD], ALU.mult, ALU.subtract).then_inc(v_out, 1)

                def maxima(j, p, g):
                    dve.wait_ge(s1_ready, j * 4 + (g + 1))
                    if g == 0:
                        need(dve, peaks_ready, j - 1)
                    dve.tensor_reduce(out=peak[p][:].rearrange("p (c g) -> p g c", g=HG)[:, g, :], in_=heads(s1[g % 2]), op=ALU.max,
                                      axis=AX.X).then_inc(maxed, 1)

                def repeat_peaks(j, p):
                    dve.wait_ge(maxed, j * 4 + 4)
                    need(dve, mt_ready, j)
                    dve.tensor_scalar(peaks8[:], peak[p][:].unsqueeze(1).to_broadcast([L, 8, H]), -1.0 / MS, None,
                                      ALU.mult).then_inc(peaks_ready, 1)

                def split_peaks(j, p):
                    dve.wait_ge(qm_ready, j + 1)
                    need(dve, s2_ready, j * 4 - 4)
                    dve.scalar_tensor_tensor(am[p][:], pt[:, 256:256 + L], low_row[:], qm[:], ALU.mult,
                                             ALU.subtract).then_inc(am_ready, 1)

                def normalize(j):
                    dve.wait_ge(pv_done, j * 4 + 4)
                    need(dve, o_made, j)
                    acc = pacc[:, 0:H * (HD + 1)].rearrange("p (h e) -> p h e", e=HD + 1)
                    dve.reciprocal(rec[:], acc[:, :, HD]).then_inc(rec_ready, 1)
                    dve.wait_ge(rec_ready, j + 1)
                    need(dve, ot_ready, j)
                    dve.tensor_tensor(o[:], acc[:, :, 0:HD], rec[:].unsqueeze(2).to_broadcast([L, H, HD]),
                                      ALU.mult).then_inc(o_made, 1)

                def split_o(j):
                    dve.wait_ge(oh_ready, j + 1)
                    need(dve, out_ready, j)
                    dve.tensor_tensor(ot_lo[:], pt[:, 0:KC * L].rearrange("p (c t) -> p c t", t=L), ot_hi[:],
                                      ALU.subtract).then_inc(ol_ready, 1)

                def add(j):
                    dve.wait_ge(out_ready, j + 1)
                    b = bass.ds(j, 1)
                    dve.scalar_tensor_tensor(core.h[:, b, :], pvo[:, 1, :].unsqueeze(1), 1.0 / WS, core.h[:, b, :],
                                             ALU.mult, ALU.add).then_inc(h_added, 1)

                def prologue():
                    w_dve(dve)
                    mw.scale_small(dve)
                    dve.wait_ge(made, 1)
                    ch = Chain(dve, masks)
                    ch.step(dve.tensor_scalar(row[:], row[:], 16, None, ALU.bitwise_and))
                    ch.step(dve.tensor_scalar(row[:], row[:], 4, None, ALU.logical_shift_right))
                    ch.step(dve.tensor_copy(low_row[:], row[:]))
                    ch.step(dve.tensor_scalar(to_same[:], low_row[:], 1.0 / WS, None, ALU.mult))
                    ch.step(dve.tensor_scalar(to_cross[:], low_row[:], -1.0 / WS, 1.0 / WS, ALU.mult, ALU.add))
                    ch.step(dve.tensor_scalar(to_q[:], low_row[:], 2.0 / WS, -1.0 / WS, ALU.mult, ALU.add))
                    ch.step(dve.tensor_scalar(to_qm[:], low_row[:], 2.0, -1.0, ALU.mult, ALU.add))
                    dve.sem_inc(masks, 1)
                    for j in range(2):
                        split_u(j, j)
                        split_v(j, j)
                    for g in range(4):
                        maxima(0, 0, g)
                    repeat_peaks(0, 0)
                    split_peaks(0, 0)

                def turn(j, p, before, now, ahead1, ahead2, behind):
                    if behind:
                        normalize(j - 1)
                    for g in range(4):
                        if ahead1:
                            maxima(j + 1, 1 - p, g)
                        if behind and g == 1:
                            split_o(j - 1)
                        if behind and g == 2:
                            add(j - 1)
                    if ahead1:
                        repeat_peaks(j + 1, 1 - p)
                    if ahead2:
                        split_u(j + 2, p)
                        split_v(j + 2, p)
                    if ahead1:
                        split_peaks(j + 1, 1 - p)
                    if now:
                        mw.low(dve, j, p, before)

                turns(dve, prologue, turn)


def program(nc, d, out):
    Stage.available, Stage.resting = list(nc.free_semaphores), []
    with ExitStack() as ctx:
        core = Core()

        def sb(name, shape, dt=F32):
            return ctx.enter_context(nc.sbuf_tensor(name, shape, dt))

        core.h = sb("h", [L, NB, D])
        core.xt_hi, core.xt_lo = sb("xt_hi", [128, KC, T], F16), sb("xt_lo", [128, KC, T], F16)
        core.ident, core.ident16 = sb("ident", [128, 128]), sb("ident16", [128, 128], F16)
        core.ones16, core.eps = sb("ones16", [128, 128], F16), sb("eps", [128, 1])
        core.ones = sb("ones", [128, 128])
        core.mean, core.rstd = sb("mean", [L, NB]), sb("rstd", [L, NB])
        core.gate = nc.alloc_semaphore("gate", Stage.available.pop(0))
        stage_constants(nc, core)
        stage_tokens(nc, core, d)
        with ExitStack() as mid:
            ssm = Core()
            msb = lambda n, s, dt=F32: mid.enter_context(nc.sbuf_tensor(f"ssm_{n}", s, dt))
            ssm.dt_hi, ssm.dt_lo, ssm.dx_hi, ssm.dx_lo = (msb(n, [128, KC, T], F16)
                                                          for n in ("dt_hi", "dt_lo", "dx_hi", "dx_lo"))
            ssm.bt, ssm.ct, ssm.a = msb("bt", [128, T]), msb("ct", [128, T]), msb("a", [128, 32])
            with ExitStack() as mid2:
                ssm.xn = mid2.enter_context(nc.sbuf_tensor("ssm_xn", [128, KC, T], F32))
                with ExitStack() as mid3:
                    core.xn = mid3.enter_context(nc.sbuf_tensor("xn", [L, NB, D], F32))
                    gam, bet = (mid3.enter_context(nc.sbuf_tensor(n, [128, KC], F32)) for n in ("gam", "bet"))
                    stage_load(nc, "gb", [(gam[:], d["gamma"]), (bet[:], d["beta"])])
                    stage_norm_stats(nc, core, "st0", core.h)
                    stage_norm_twice(nc, core, d["d_param"])
                    stage_features(nc, core, "f0", core.xn, affine=(gam, bet), full=ssm.xn)
                stage_ssm_inputs(nc, core, d, ssm)
            stage_ssm_scan(nc, core, ssm)
        for tag, stage in (("ffn0", None), ("gru", stage_gru), ("bg", stage_bit_gelu), ("la", stage_linear_attention)):
            if tag == "ffn0":
                with ExitStack() as mid:
                    m = Moe("m0", 15, 3, 4, 2, True, True, True)
                    m.buffers(nc, mid)
                    stage_moe_weights(nc, core, m, d)
                    stage_norm_stats(nc, core, "m0s", core.h)
                    stage_features(nc, core, "m0f", core.h, rows=m.rows)
                    stage_route(nc, core, m, d)
                    stage_shared(nc, core, d)
                    stage_experts(nc, core, m)
                    stage_combine(nc, core, m)
                continue
            stage_norm_stats(nc, core, tag + "s", core.h)
            stage_features(nc, core, tag + "f", core.h)
            stage(nc, core, d)
        stage_norm_stats(nc, core, "glus", core.h)
        stage_bit_glu(nc, core, d)
        m = Moe("m3", 8, 1, 8, 8, False, False, False)
        with ExitStack() as mid:
            m.buffers(nc, mid)
            stage_norm_stats(nc, core, "mhas", core.h)
            stage_features(nc, core, "mhaf", core.h)
            stage_attention(nc, core, d, m)
            stage_norm_stats(nc, core, "m3s", core.h)
            stage_features(nc, core, "m3f", core.h, rows=m.rows)
            stage_route(nc, core, m, d)
            stage_experts(nc, core, m)
            stage_combine(nc, core, m)
        with Stage(nc, "out") as st:
            s = st.sem("stored")
            with nc.Block() as block:
                @block.sync
                def _(sp):
                    sp.dma_start(out.rearrange("b t d -> t b d"), core.h[:]).then_inc(s, 16)
                    sp.wait_ge(s, 16)


def stage_load(nc, name, pairs):
    with Stage(nc, name) as st:
        s = st.sem("landed")
        with nc.Block() as block:
            @block.sync
            def _(sp):
                for dst, src in pairs:
                    sp.dma_start(dst, src).then_inc(s, 16)
                sp.wait_ge(s, 16 * len(pairs))


def kmajor(w):
    K, N = w.shape
    return w.reshape(K // 128, 128, N).transpose(1, 0, 2).reshape(128, -1)


def columns(v):
    return v.reshape(-1, 128).T


def head_factors(params):
    H, HD = 16, 16
    rows, cols = np.tril_indices(HD)
    tril = np.zeros((H, HD, HD), params.dtype)
    tril[:, rows, cols] = params
    out = np.zeros((128, 4, 128), params.dtype)
    for h in range(H):
        c, j = divmod(h, 4)
        k = h * HD % 128
        for half in range(2):
            out[k:k + HD, c, 32 * j + 16 * half:32 * j + 16 * half + HD] = tril[h]
    return out.reshape(128, -1)


def layout(i):
    i = {k: np.asarray(v) for k, v in i.items()}
    P = 16
    x = i["x"]
    B, C, H, W = x.shape
    pt = x.reshape(B, C, H // P, P, W // P, P).transpose(0, 2, 4, 1, 3, 5).reshape(B * 36, C * P * P)
    out = {
        "patches": kmajor(pt.T), "txt": i["txt"].transpose(1, 0, 2),
        "w1": kmajor(i["L0_tok_W1"]), "b1": columns(i["L0_tok_b1"]), "w2": kmajor(i["L0_tok_W2"]),
        "b2": i["L0_tok_b2"][None, :],
        "w_dt": kmajor(i["L0_attn_W_dt"].T), "b_dt": columns(i["L0_attn_b_dt"]),
        "w_bc": np.stack([kmajor(np.tile(i[f"L0_attn_W_{s}"], (8, 1)).T) for s in "BC"], 1).reshape(128, -1),
        "a_log": i["L0_attn_A_log"].reshape(32, 8, 16).transpose(1, 2, 0).reshape(128, 32),
        "gamma": columns(i["L0_attn_gamma"]), "beta": columns(i["L0_attn_beta"]),
        "d_param": i["L0_attn_D_param"],
        "m0w": np.concatenate([np.stack([kmajor(w.T) for w in i["L0_ffn_fc1_w"]], 1),
                               np.stack([kmajor(w.T) for w in i["L0_ffn_fc2_w"]], 1)], 2),
        "m0mult": i["L0_ffn_geglu_mult"].reshape(15, 2, 128).transpose(2, 0, 1).reshape(128, -1),
        "m0b1": i["L0_ffn_fc1_b"].reshape(15, 4, 128).transpose(2, 0, 1),
        "m0router": kmajor(i["L0_ffn_gate_w"].T), "m0b2": i["L0_ffn_fc2_b"],
        "m3w": np.stack([kmajor(w) for e in range(8) for w in (i["L3_ffn_w1"][e], i["L3_ffn_w2"][e])], 1),
        "m3b1": i["L3_ffn_b1"].reshape(8, 8, 128).transpose(2, 0, 1),
        "m3router": kmajor(i["L3_ffn_w_router"]), "m3b2": i["L3_ffn_b2"],
    }
    out |= {
        "s1": kmajor(i["L0_ffn_s_fc1_w"].T), "s_b1": columns(i["L0_ffn_s_fc1_b"]),
        "s_mult": columns(i["L0_ffn_s_geglu_mult"]), "s2": kmajor(i["L0_ffn_s_fc2_w"].T),
        "s_b2": i["L0_ffn_s_fc2_b"][None, :],
        "w_f": kmajor(i["L1_attn_W_f"].T), "b_f": columns(i["L1_attn_b_f"]), "w_down": kmajor(i["L1_attn_W_down"].T),
        "w_fc": kmajor(i["L1_ffn_W_fc"].T), "w_proj": kmajor(i["L1_ffn_W_proj"].T),
        "ln_w": columns(i["L1_ffn_ln_w"]), "ln_b": columns(i["L1_ffn_ln_b"]),
        "w_theta": kmajor(i["L2_attn_W_theta"].T),
        "w_phi_g": kmajor(np.concatenate([i["L2_attn_W_phi"], i["L2_attn_W_g"]], 0).T),
        "w_gate": kmajor(i["L2_ffn_w_gate"].T), "w_up": kmajor(i["L2_ffn_w_up"].T),
        "w_dn": kmajor(i["L2_ffn_w_down"].T),
        "w_l": head_factors(i["L3_attn_params"]), "w_v": kmajor(i["L3_attn_Wv"].T), "b_v": i["L3_attn_bv"][None, :],
        "w_o": kmajor(i["L3_attn_Wo"].T), "b_o": i["L3_attn_bo"][None, :],
    }
    return {k: np.ascontiguousarray(v) for k, v in out.items()}


def kernel(**inputs):
    import numpy as np
    import concourse.bacc as bacc
    from concourse import mybir
    from concourse.bass_utils import run_bass_kernel_spmd

    nc = bacc.Bacc("TRN2", target_bir_lowering=False, num_devices=1)
    arrays = layout(inputs)
    aps = {name: nc.dram_tensor(name, a.shape, mybir.dt.from_np(a.dtype), kind="ExternalInput").ap()
           for name, a in arrays.items()}
    out = nc.dram_tensor("out", (NB, L, D), mybir.dt.float32, kind="ExternalOutput").ap()
    program(nc, aps, out)
    return run_bass_kernel_spmd(nc, [arrays], core_ids=[0]).results[0]["out"]
```
